# Optimizing a Trainium2 kernel written in Bass

```python
import numpy as np
import jax
import jax.numpy as jnp

def _softmax(x, axis=-1):
    return jax.nn.softmax(x, axis=axis)

def _gelu(x):
    return jax.nn.gelu(x, approximate=True)

def _silu(x):
    return jax.nn.silu(x)

def _sigmoid(x):
    return jax.nn.sigmoid(x)

def _layernorm(x, axis=-1, eps=1e-05):
    m = jnp.mean(x, axis=axis, keepdims=True)
    v = jnp.var(x, axis=axis, keepdims=True)
    return (x - m) / jnp.sqrt(v + eps)

def _scatter_add(tgt, idx, src, axis=0):
    return tgt.at[idx].add(src)

def _segment_sum(src, seg, n):
    return jax.ops.segment_sum(src, seg, n)
kernel_name = 'mk_xattn_ffn_d1_seqx_r4_6c2756'

def setup_inputs(seed: int=0):
    np.random.seed(seed)
    _w = jnp.asarray

    def _rec_inputs():
        import jax
        import jax.numpy as jnp
        _rk = jax.random.key(seed)
        x = -0.0002928 + 1 * jax.random.normal(jax.random.fold_in(_rk, 1), (8, 256, 256), jnp.float32)
        _lenS = 256 - jax.random.randint(jax.random.fold_in(_rk, 7), (8,), 0, max(1, 256 // 4) + 1, jnp.int32)
        _lenS2 = 256 - jax.random.randint(jax.random.fold_in(_rk, 8), (8,), 0, max(1, 256 // 4) + 1, jnp.int32)
        _ctx_1024P = jax.random.normal(jax.random.fold_in(_rk, 11), (8, 16, 256), jnp.float32)
        _ctx_1024c = jax.random.dirichlet(jax.random.fold_in(_rk, 511), 0.3 * jnp.ones((16,), jnp.float32), (8, 256))
        _ctx_1024t = jnp.einsum('bsk,bkd->bsd', _ctx_1024c, _ctx_1024P)
        _ctx_1024t = _ctx_1024t * jax.lax.rsqrt(jnp.mean(jnp.square(_ctx_1024t)) + 1e-12) * 0.953939
        ctx_1024 = -1.39393e-06 + 0.999914 * (_ctx_1024t + 0.3 * jax.random.normal(jax.random.fold_in(_rk, 611), (8, 256, 256), jnp.float32))
        return (x, ctx_1024)
    x, ctx_1024 = _rec_inputs()

    def _L0_xattn_setup():
        import jax, jax.numpy as jnp
        import numpy as np
        EMBED = 256
        HEADS = 16
        HIDDEN = 256
        HEAD_DIM = EMBED // HEADS
        key = jax.random.key(seed)
        ks = jax.random.split(key, 9)
        s = 1.0 / np.sqrt(HIDDEN)
        return {'q': jax.random.normal(ks[0], (2, 512, HIDDEN), jnp.float32), 'k': jax.random.normal(ks[1], (2, 512, HIDDEN), jnp.float32), 'v': jax.random.normal(ks[2], (2, 512, HIDDEN), jnp.float32), 'wq': jax.random.normal(ks[3], (HIDDEN, EMBED), jnp.float32) * s, 'bq': jax.random.normal(ks[4], (EMBED,), jnp.float32) * s, 'wk': jax.random.normal(ks[5], (HIDDEN, EMBED), jnp.float32) * s, 'bk': jax.random.normal(ks[6], (EMBED,), jnp.float32) * s, 'wv': jax.random.normal(ks[7], (HIDDEN, EMBED), jnp.float32) * s, 'bv': jax.random.normal(ks[8], (EMBED,), jnp.float32) * s}
    _L0_xattn_all = _L0_xattn_setup()
    _L0_xattn_in = {k: v for k, v in _L0_xattn_all.items() if k in ('wq', 'bq', 'wk', 'bk', 'wv', 'bv')}
    del _L0_xattn_all

    def _L0_ffn_setup():
        import jax, jax.numpy as jnp
        import numpy as np
        DIM = 256
        DEPTH = 2
        HEADS = 8
        DIM_HEAD = 64
        WINDOW = 128
        INNER = HEADS * DIM_HEAD
        HID = int(DIM * 4 * 2 / 3)
        B, N = (2, 2048)
        QK_SCALE = 8.0

        def shift_token(t):
            t1, t2 = jnp.split(t, 2, axis=-1)
            t2 = jnp.pad(t2, ((0, 0), (1, 0), (0, 0)))[:, :-1]
            return jnp.concatenate([t1, t2], axis=-1)

        def l2norm(t):
            return t / jnp.clip(jnp.linalg.norm(t, axis=-1, keepdims=True), 1e-12)

        def rotate_half(x):
            x1, x2 = jnp.split(x, 2, axis=-1)
            return jnp.concatenate([-x2, x1], axis=-1)

        def rotary_xpos(q, k):
            n = q.shape[-2]
            half_idx = jnp.arange(0, DIM_HEAD, 2, dtype=jnp.float32)
            inv_freq = 1.0 / 10000.0 ** (half_idx / DIM_HEAD)
            t = jnp.arange(n, dtype=jnp.float32)
            freqs = t[:, None] * inv_freq[None, :]
            freqs = jnp.concatenate([freqs, freqs], axis=-1)
            base = (half_idx + 0.4 * DIM_HEAD) / (1.4 * DIM_HEAD)
            power = (t - n // 2) / float(WINDOW // 2)
            scale = base[None, :] ** power[:, None]
            scale = jnp.concatenate([scale, scale], axis=-1)
            cos, sin = (jnp.cos(freqs), jnp.sin(freqs))
            q = q * cos * scale + rotate_half(q) * sin * scale
            k = k * cos / scale + rotate_half(k) * sin / scale
            return (q, k)

        def local_attention(q, k, v):
            b, h, n, d = q.shape
            w = n // WINDOW
            bq = q.reshape(b, h, w, WINDOW, d) * QK_SCALE
            bk = k.reshape(b, h, w, WINDOW, d)
            bv = v.reshape(b, h, w, WINDOW, d)

            def look_around(t):
                p = jnp.pad(t, ((0, 0), (0, 0), (1, 0), (0, 0), (0, 0)))
                return jnp.concatenate([p[:, :, :w], p[:, :, 1:]], axis=3)
            bk, bv = (look_around(bk), look_around(bv))
            bt = jnp.arange(n).reshape(w, WINDOW)
            btp = jnp.pad(bt, ((1, 0), (0, 0)), constant_values=-1)
            btk = jnp.concatenate([btp[:w], btp[1:]], axis=1)
            sim = jnp.einsum('bhwid,bhwjd->bhwij', bq, bk)
            i = bt[:, :, None]
            j = btk[:, None, :]
            mask = (i < j) | (i > j + WINDOW) | (j == -1)
            sim = jnp.where(mask, -jnp.finfo(sim.dtype).max, sim)
            attn = jax.nn.softmax(sim, axis=-1)
            out = jnp.einsum('bhwij,bhwjd->bhwid', attn, bv)
            return out.reshape(b, h, n, d)

        def _layer(x, wqkv, qs, ksc, wo, lg, lb, w1, b1, w2, b2):
            b, n, _ = x.shape
            h = shift_token(x)
            qkv = h @ wqkv
            q, k, v = jnp.split(qkv, 3, axis=-1)
            to_heads = lambda t: t.reshape(b, n, HEADS, DIM_HEAD).transpose(0, 2, 1, 3)
            q, k, v = (to_heads(q), to_heads(k), to_heads(v))
            q = l2norm(q) * qs
            k = l2norm(k) * ksc
            q, k = rotary_xpos(q, k)
            o = local_attention(q, k, v)
            o = o.transpose(0, 2, 1, 3).reshape(b, n, INNER)
            x = x + o @ wo
            h = shift_token(x)
            mu = h.mean(-1, keepdims=True)
            var = h.var(-1, keepdims=True)
            h = (h - mu) / jnp.sqrt(var + 1e-05) * lg + lb
            h = h @ w1 + b1
            a, g = jnp.split(h, 2, axis=-1)
            h = a * jax.nn.gelu(g, approximate=False)
            x = x + h @ w2 + b2
            return x
        key = jax.random.key(seed)
        ks = jax.random.split(key, 6)
        return {'x': jax.random.normal(ks[0], (B, N, DIM), jnp.float32), 'wqkv': jax.random.normal(ks[1], (DEPTH, DIM, 3 * INNER), jnp.float32) * 0.02, 'q_scale': jnp.ones((DEPTH, DIM_HEAD), jnp.float32), 'k_scale': jnp.ones((DEPTH, DIM_HEAD), jnp.float32), 'wo': jax.random.normal(ks[2], (DEPTH, INNER, DIM), jnp.float32) * 0.02, 'ln_g': jnp.ones((DEPTH, DIM), jnp.float32), 'ln_b': jnp.zeros((DEPTH, DIM), jnp.float32), 'w1': jax.random.normal(ks[3], (DEPTH, DIM, 2 * HID), jnp.float32) * 0.02, 'b1': jnp.zeros((DEPTH, 2 * HID), jnp.float32), 'w2': jax.random.normal(ks[4], (DEPTH, HID, DIM), jnp.float32) * 0.02, 'b2': jnp.zeros((DEPTH, DIM), jnp.float32)}
    _L0_ffn_all = _L0_ffn_setup()
    _L0_ffn_in = {k: v for k, v in _L0_ffn_all.items() if k in ('wqkv', 'q_scale', 'k_scale', 'wo', 'ln_g', 'ln_b', 'w1', 'b1', 'w2', 'b2')}
    del _L0_ffn_all
    return {'x': x, 'ctx_1024': ctx_1024, 'L0_xattn_wq': _L0_xattn_in['wq'], 'L0_xattn_bq': _L0_xattn_in['bq'], 'L0_xattn_wk': _L0_xattn_in['wk'], 'L0_xattn_bk': _L0_xattn_in['bk'], 'L0_xattn_wv': _L0_xattn_in['wv'], 'L0_xattn_bv': _L0_xattn_in['bv'], 'L0_ffn_wqkv': _L0_ffn_in['wqkv'], 'L0_ffn_q_scale': _L0_ffn_in['q_scale'], 'L0_ffn_k_scale': _L0_ffn_in['k_scale'], 'L0_ffn_wo': _L0_ffn_in['wo'], 'L0_ffn_ln_g': _L0_ffn_in['ln_g'], 'L0_ffn_ln_b': _L0_ffn_in['ln_b'], 'L0_ffn_w1': _L0_ffn_in['w1'], 'L0_ffn_b1': _L0_ffn_in['b1'], 'L0_ffn_w2': _L0_ffn_in['w2'], 'L0_ffn_b2': _L0_ffn_in['b2']}

def reference(x, ctx_1024, L0_xattn_wq, L0_xattn_bq, L0_xattn_wk, L0_xattn_bk, L0_xattn_wv, L0_xattn_bv, L0_ffn_wqkv, L0_ffn_q_scale, L0_ffn_k_scale, L0_ffn_wo, L0_ffn_ln_g, L0_ffn_ln_b, L0_ffn_w1, L0_ffn_b1, L0_ffn_w2, L0_ffn_b2):
    import jax
    import jax.numpy as jnp

    def _L0_xattn_ref(q, k, v, wq, bq, wk, bk, wv, bv):
        import jax, jax.numpy as jnp
        import numpy as np
        EMBED = 256
        HEADS = 16
        HIDDEN = 256
        HEAD_DIM = EMBED // HEADS
        B = q.shape[0]

        def split_heads(x):
            return x.reshape(B, -1, HEADS, HEAD_DIM).transpose(0, 2, 1, 3)
        qh = split_heads(q @ wq + bq)
        kh = split_heads(k @ wk + bk)
        vh = split_heads(v @ wv + bv)
        scale = 1.0 / np.sqrt(HEAD_DIM).astype(np.float32)
        scores = jnp.einsum('bhqd,bhkd->bhqk', qh, kh) * scale
        probs = jax.nn.softmax(scores, axis=-1)
        out = jnp.einsum('bhqk,bhkd->bhqd', probs, vh)
        return out.transpose(0, 2, 1, 3).reshape(B, -1, EMBED)

    def _L0_ffn_ref(x, wqkv, q_scale, k_scale, wo, ln_g, ln_b, w1, b1, w2, b2):
        import jax, jax.numpy as jnp
        import numpy as np
        DIM = 256
        DEPTH = 2
        HEADS = 8
        DIM_HEAD = 64
        WINDOW = 128
        INNER = HEADS * DIM_HEAD
        HID = int(DIM * 4 * 2 / 3)
        B, N = (2, 2048)
        QK_SCALE = 8.0

        def shift_token(t):
            t1, t2 = jnp.split(t, 2, axis=-1)
            t2 = jnp.pad(t2, ((0, 0), (1, 0), (0, 0)))[:, :-1]
            return jnp.concatenate([t1, t2], axis=-1)

        def l2norm(t):
            return t / jnp.clip(jnp.linalg.norm(t, axis=-1, keepdims=True), 1e-12)

        def rotate_half(x):
            x1, x2 = jnp.split(x, 2, axis=-1)
            return jnp.concatenate([-x2, x1], axis=-1)

        def rotary_xpos(q, k):
            n = q.shape[-2]
            half_idx = jnp.arange(0, DIM_HEAD, 2, dtype=jnp.float32)
            inv_freq = 1.0 / 10000.0 ** (half_idx / DIM_HEAD)
            t = jnp.arange(n, dtype=jnp.float32)
            freqs = t[:, None] * inv_freq[None, :]
            freqs = jnp.concatenate([freqs, freqs], axis=-1)
            base = (half_idx + 0.4 * DIM_HEAD) / (1.4 * DIM_HEAD)
            power = (t - n // 2) / float(WINDOW // 2)
            scale = base[None, :] ** power[:, None]
            scale = jnp.concatenate([scale, scale], axis=-1)
            cos, sin = (jnp.cos(freqs), jnp.sin(freqs))
            q = q * cos * scale + rotate_half(q) * sin * scale
            k = k * cos / scale + rotate_half(k) * sin / scale
            return (q, k)

        def local_attention(q, k, v):
            b, h, n, d = q.shape
            w = n // WINDOW
            bq = q.reshape(b, h, w, WINDOW, d) * QK_SCALE
            bk = k.reshape(b, h, w, WINDOW, d)
            bv = v.reshape(b, h, w, WINDOW, d)

            def look_around(t):
                p = jnp.pad(t, ((0, 0), (0, 0), (1, 0), (0, 0), (0, 0)))
                return jnp.concatenate([p[:, :, :w], p[:, :, 1:]], axis=3)
            bk, bv = (look_around(bk), look_around(bv))
            bt = jnp.arange(n).reshape(w, WINDOW)
            btp = jnp.pad(bt, ((1, 0), (0, 0)), constant_values=-1)
            btk = jnp.concatenate([btp[:w], btp[1:]], axis=1)
            sim = jnp.einsum('bhwid,bhwjd->bhwij', bq, bk)
            i = bt[:, :, None]
            j = btk[:, None, :]
            mask = (i < j) | (i > j + WINDOW) | (j == -1)
            sim = jnp.where(mask, -jnp.finfo(sim.dtype).max, sim)
            attn = jax.nn.softmax(sim, axis=-1)
            out = jnp.einsum('bhwij,bhwjd->bhwid', attn, bv)
            return out.reshape(b, h, n, d)

        def _layer(x, wqkv, qs, ksc, wo, lg, lb, w1, b1, w2, b2):
            b, n, _ = x.shape
            h = shift_token(x)
            qkv = h @ wqkv
            q, k, v = jnp.split(qkv, 3, axis=-1)
            to_heads = lambda t: t.reshape(b, n, HEADS, DIM_HEAD).transpose(0, 2, 1, 3)
            q, k, v = (to_heads(q), to_heads(k), to_heads(v))
            q = l2norm(q) * qs
            k = l2norm(k) * ksc
            q, k = rotary_xpos(q, k)
            o = local_attention(q, k, v)
            o = o.transpose(0, 2, 1, 3).reshape(b, n, INNER)
            x = x + o @ wo
            h = shift_token(x)
            mu = h.mean(-1, keepdims=True)
            var = h.var(-1, keepdims=True)
            h = (h - mu) / jnp.sqrt(var + 1e-05) * lg + lb
            h = h @ w1 + b1
            a, g = jnp.split(h, 2, axis=-1)
            h = a * jax.nn.gelu(g, approximate=False)
            x = x + h @ w2 + b2
            return x
        for l in range(DEPTH):
            x = _layer(x, wqkv[l], q_scale[l], k_scale[l], wo[l], ln_g[l], ln_b[l], w1[l], b1[l], w2[l], b2[l])
        return x
    x = x + _L0_xattn_ref(_layernorm(x, axis=-1), ctx_1024, ctx_1024, L0_xattn_wq, L0_xattn_bq, L0_xattn_wk, L0_xattn_bk, L0_xattn_wv, L0_xattn_bv)
    x = x + _L0_ffn_ref(_layernorm(x, axis=-1), L0_ffn_wqkv, L0_ffn_q_scale, L0_ffn_k_scale, L0_ffn_wo, L0_ffn_ln_g, L0_ffn_ln_b, L0_ffn_w1, L0_ffn_b1, L0_ffn_w2, L0_ffn_b2)
    return x

_drawn_inputs = setup_inputs


def setup_inputs(seed=0):
    import zlib

    import numpy as np

    out = dict(_drawn_inputs(seed))
    spreads = {'L0_ffn_q_scale': (1.0, 0.6),
     'L0_ffn_k_scale': (1.0, 0.6),
     'L0_ffn_ln_g': (1.0, 0.6),
     'L0_ffn_ln_b': (0.0, 0.8),
     'L0_ffn_b1': (0.0, 0.8),
     'L0_ffn_b2': (0.0, 0.1)}
    factors = {'L0_xattn_bq': 4.752, 'L0_xattn_bk': 8.0}
    for name, (base, spread) in spreads.items():
        noise = np.random.default_rng([zlib.crc32(name.encode()), seed]).standard_normal(out[name].shape)
        drawn = base * np.exp(spread * noise) if base else spread * noise
        out[name] = jnp.asarray(drawn.astype(out[name].dtype))
    for name, factor in factors.items():
        out[name] = (out[name] * factor).astype(out[name].dtype)
    return out
```

```python
from contextlib import ExitStack

import concourse.bass as bass
import concourse.mybir as mybir
import numpy as np

ALU = mybir.AluOpType
ACT = mybir.ActivationFunctionType
F32 = mybir.dt.float32
F32R = mybir.dt.float32r
BF16 = mybir.dt.bfloat16
I32 = mybir.dt.int32
AX_X = mybir.AxisListType.X

P = 128
B, N, D = 8, 256, 256
T = N // P
KD = D // P
PAIRS = B // 2
XH, XD = 16, D // 16
LAYERS = 2
H, HD = 8, 64
INNER = H * HD
HP = INNER // P
WINDOW = 128
HID = int(D * 4 * 2 / 3)
J = -(-HID // P)
HID_LAST = HID - (J - 1) * P
ROUNDS = LAYERS * PAIRS
VW = 32
PART_PAIRS = ((0, 0), (0, 1), (0, 2), (1, 0), (1, 1), (1, 2), (2, 0), (2, 1))
MASKED = -1e30
GAP = 2
SLOTS = 3
EPS = 1e-5
NORM_FLOOR = 1e-12


def constants():
    half = np.arange(0, HD, 2, dtype=np.float32)
    inv = (1.0 / np.float32(10000.0) ** (half / np.float32(HD))).astype(np.float32)
    t = np.arange(N, dtype=np.float32)
    f = (t[:, None] * inv[None, :]).astype(np.float32)
    f = np.concatenate([f, f], 1).astype(np.float64)
    base = (half + np.float32(0.4 * HD)) / np.float32(1.4 * HD)
    power = (t - N // 2) / np.float32(WINDOW // 2)
    s = (base[None, :].astype(np.float32) ** power[:, None].astype(np.float32)).astype(np.float64)
    s = np.concatenate([s, s], 1)
    sign = np.where(np.arange(HD) < HD // 2, -1.0, 1.0)[None, :]
    rot = np.stack([np.stack([np.cos(f) * s * 8, np.sin(f) * sign * s * 8]),
                    np.stack([np.cos(f) / s, np.sin(f) * sign / s])]).astype(np.float32)
    i, j = np.arange(N)[:, None], np.arange(N)[None, :]
    off = (i < j) | (i > j + WINDOW) | ((i < WINDOW) & (j >= WINDOW))
    mask = np.where(off, MASKED, 0.0).astype(np.float32)
    maskq = mask.reshape(T, P, N).transpose(1, 0, 2)
    maskk = mask.T.reshape(T, P, N).transpose(1, 0, 2)
    masks = np.stack([maskq, maskk], 1)
    sel = np.zeros((P, XH, P), np.float32)
    for h in range(XH):
        sel[h, h] = sel[32 + h, h] = 1.0
    ones = np.zeros((P, 2, 32), np.float32)
    ones[:, 0, 0:16] = 1.0
    ones[:, 1, 16:32] = 1.0
    spread = np.zeros((P, HP, P), np.float32)
    for h in range(H):
        spread[32 * (h % 4) + 16 * (h // 4), h // 2, HD * (h % 2):HD * (h % 2) + HD] = 1.0
    return {"c_rot": rot, "c_masks": masks, "c_sel": sel, "c_ones": ones, "c_spread": spread,
            "c_ident": np.eye(P, dtype=np.float32)}


class Signal:

    def __init__(self, sem, per_round, by=1):
        self.sem, self.per_round, self.by = sem, per_round, by

    def of(self, n, k):
        return self.sem, (n * self.per_round + (self.per_round + k)) * self.by

    def before(self, n, k):
        return self.sem, (n * self.per_round + k) * self.by


def place(order):
    turn, inside = {}, {}
    for ring, unit in order:
        k = ring[turn.get(ring, 0) % len(ring)]
        turn[ring] = turn.get(ring, 0) + 1
        inside.setdefault(k, []).append(unit)
    at = {}
    for k, units in inside.items():
        for i, unit in enumerate(units):
            at[unit] = (k, i + 1, units[i - 1], i > 0)
    return at, {k: len(u) for k, u in inside.items()}


def cross_attention(nc, io, dram):
    SCHEDULE = [("ln", 0), ("ln", 1), ("turn", 0), ("turn", 1), ("proj", 0), ("proj", 1), ("max", 0),
                ("max", 1), ("attend", 0), ("out", 0), ("attend", 1), ("out", 1)]
    ring, own = (0, 1, 2, 3, 4, 5), (6, 7)
    order = []
    for stage, b in SCHEDULE:
        if stage == "turn":
            order += [(ring, ("cT", b)), (ring, ("xT", b))]
        if stage == "proj":
            order += [(ring, (c, b)) for c in "kqv"]
        if stage == "max":
            order += [(ring, ("s", b, h)) for h in range(XH)] + [(ring, ("mT", b))]
        if stage == "attend":
            order += [(ring, ("e", b, h)) for h in range(XH)] + [(own, ("pv", b, g)) for g in range(2)]
        if stage == "out":
            order += [(ring, ("o", b, t)) for t in range(T)]
    units, per_bank = place(order)
    signals = []
    ctx = ExitStack()
    with ctx:
        def sb(name, shape, dt):
            return ctx.enter_context(nc.sbuf_tensor("x_" + name, shape, dt))

        def signal(name, per_round, by=1):
            signals.append(Signal(ctx.enter_context(nc.semaphore("x_" + name)), per_round, by))
            return signals[-1]

        def sem(name):
            return ctx.enter_context(nc.semaphore("x_" + name))

        psum = [ctx.enter_context(nc.psum_tensor(f"x_ps{i}", [P, 512], F32)) for i in range(8)]
        ident = sb("ident", [P, P], F32)
        sel_f = sb("sel_f", [P, XH, P], F32)
        sel = sb("sel", [P, XH, P], BF16)
        wraw = sb("wraw", [P, 3, KD, D], F32)
        whi = sb("whi", [P, 3, KD, D], F32R)
        wlo = sb("wlo", [P, 3, KD, D], F32R)
        bqk = sb("bqk", [P, 2, KD], F32)
        bv = sb("bv", [P, D], F32)
        mhalf = sb("mhalf", [P, T], F32)
        xin = sb("xin", [P, 2, T, D], F32)
        cin = sb("cin", [P, 2, T, D], F32)
        stats = sb("stats", [P, 2, 2, T, 6], F32)
        mv = sb("mv", [P, 2, 2, T, 2], F32)
        veps = sb("veps", [P, 2, 2, T], F32)
        eps = sb("eps", [P, T], F32)
        carrier = sb("carrier", [P, T], F32)
        rstd = sb("rstd", [P, 2, 2, T], F32)
        xn = sb("xn", [P, 2, T, D], F32)
        hi = sb("hi", [P, 2, 2, KD, N], F32R)
        lo = sb("lo", [P, 2, 2, KD, N], F32R)
        qk = sb("qk", [P, 2, 2, KD, N], F32)
        rest = sb("rest", [P, 2, 2, KD, N], F32)
        parts = sb("parts", [P, 2, 2, 3, KD, N], BF16)
        stack = sb("stack", [P, 2, 2, XH, N], BF16)
        va = sb("va", [P, 2, T, XH, VW], F32)
        nm = sb("nm", [P, 2, T, XH], F32)
        mrow = sb("mrow", [P, 2, N], BF16)
        probs = sb("probs", [P, SLOTS, T * N], F32)
        oT = sb("oT", [P, 2, 4, N], F32)
        rden = sb("rden", [P, 2, T, XH], F32)
        x1 = sb("x1", [P, 2, T, D], F32)
        y = sb("y", [P, 2, T, D], F32)

        consts_in, sel_cast = sem("consts_in"), sem("sel_cast")
        whi_ready, wlo_ready, set_up = sem("whi_ready"), sem("wlo_ready"), sem("set_up")
        filled = {k: signal(f"filled{k}", m) for k, m in per_bank.items()}
        x_in = [signal(f"x_in{b}", 1, 16) for b in range(2)]
        c_in = [signal(f"c_in{b}", 1, 16) for b in range(2)]
        stats_ready, var_ready = signal("stats_ready", 4), signal("var_ready", 4)
        eps_added, rstd_ready = signal("eps_added", 4), signal("rstd_ready", 4)
        xn_ready = signal("xn_ready", 2)
        hi_ready, lo_ready = signal("hi_ready", 4), signal("lo_ready", 4)
        qk_ready, p1_ready, rest_ready = signal("qk_ready", 4), signal("p1_ready", 4), signal("rest_ready", 4)
        p2_ready, p3_ready = signal("p2_ready", 4), signal("p3_ready", 4)
        v_ready = signal("v_ready", 2)
        parts_out = [signal(f"parts_out{b}", 2, 16) for b in range(2)]
        stacks_in = [signal(f"stacks_in{b}", 2 * len(PART_PAIRS), 16) for b in range(2)]
        max_ready = signal("max_ready", 2 * XH)
        m1_ready, m2_ready = signal("m1_ready", 2), signal("m2_ready", 2)
        probs_ready, probs_used = signal("probs_ready", 2 * XH), signal("probs_used", 2 * XH)
        oT_ready = signal("oT_ready", 4)
        rden_ready, att_ready, x1_ready = signal("rden_ready", 4), signal("att_ready", 4), signal("x1_ready", 4)
        y_ready = signal("y_ready", 2)
        x1_out = [signal(f"x1_out{b}", 1, 16) for b in range(2)]
        y_out = [signal(f"y_out{b}", 1, 16) for b in range(2)]

        reader = {
            "cT": lambda b: (lo_ready, 2 * b + 1), "xT": lambda b: (lo_ready, 2 * b + 2),
            "k": lambda b: (qk_ready, 2 * b + 1), "q": lambda b: (qk_ready, 2 * b + 2),
            "v": lambda b: (v_ready, b + 1),
            "s": lambda b, h: (max_ready, XH * b + h + 1), "mT": lambda b: (m2_ready, b + 1),
            "e": lambda b, h: (probs_ready, XH * b + h + 1), "pv": lambda b, g: (oT_ready, 2 * b + g + 1),
            "o": lambda b, t: (att_ready, T * b + t + 1),
        }

        def bank(unit):
            return psum[units[unit][0]]

        def full(n, unit):
            return filled[units[unit][0]].of(n, units[unit][1])

        def fills(unit):
            return filled[units[unit][0]].sem

        def emptied(n, unit):
            _, _, last, same_round = units[unit]
            by, k = reader[last[0]](*last[1:])
            return by.of(n, k) if same_round else by.before(n, k)

        for s in signals:
            nc.sync.sem_inc(s.sem, s.per_round * s.by)

        block = ctx.enter_context(nc.Block())

        @block.sync
        def _(sp):
            sp.dma_start(ident[:, :], io["c_ident"]).then_inc(consts_in, 16)
            sp.dma_start(sel_f[:, :, :], io["c_sel"]).then_inc(consts_in, 16)
            for c, w in enumerate(("wk", "wq", "wv")):
                sp.dma_start(wraw[:, c], io[w].rearrange("(k p) n -> p k n", p=P)).then_inc(consts_in, 16)
            for c, w in enumerate(("bk", "bq")):
                sp.dma_start(bqk[:, c], io[w].rearrange("(k p) -> p k", p=P),
                             allow_slow_non_contiguous=True).then_inc(consts_in, 16)
            sp.dma_start(bv[:, :], io["bv"].partition_broadcast(P)).then_inc(consts_in, 16)

            with sp.Fori(0, PAIRS) as n:
                for b in range(2):
                    sp.wait_ge(*x1_ready.before(n, T * (b + 1)))
                    sp.dma_start(xin[:, b], io["x"][n * 2 + b].rearrange("(t p) d -> p t d", p=P)).then_inc(x_in[b].sem, 16)
                    sp.dma_start(cin[:, b], io["ctx"][n * 2 + b].rearrange("(t p) d -> p t d", p=P)).then_inc(c_in[b].sem, 16)
                for b in range(2):
                    sp.wait_ge(*p3_ready.of(n, 2 * b + 2))
                    for c in range(2):
                        sp.dma_start(dram["parts"][b, c].rearrange("s (k p) t -> p s k t", p=P),
                                     parts[:, b, c]).then_inc(parts_out[b].sem, 16)
                    sp.wait_ge(*parts_out[b].of(n, 2))
                    for c in range(2):
                        for g, pair in enumerate(PART_PAIRS):
                            sp.dma_start(stack[XD * g:XD * (g + 1), b, c],
                                         dram["parts"][b, c, pair[c]].rearrange("(h r) t -> r h t", r=XD)
                                         ).then_inc(stacks_in[b].sem, 16)
                for b in range(2):
                    sp.wait_ge(*x1_ready.of(n, T * (b + 1)))
                    sp.dma_start(dram["x1"][n * 2 + b].rearrange("(t p) d -> p t d", p=P), x1[:, b]).then_inc(x1_out[b].sem, 16)
                    sp.wait_ge(*y_ready.of(n, b + 1))
                    sp.dma_start(dram["y"][n * 2 + b].rearrange("(t p) d -> p t d", p=P), y[:, b]).then_inc(y_out[b].sem, 16)
            for b in range(2):
                sp.wait_ge(*x1_out[b].of(PAIRS - 1, 1))
                sp.wait_ge(*y_out[b].of(PAIRS - 1, 1))

        @block.tensor
        def _(pe):
            pe.wait_ge(consts_in, 16 * 8)
            pe.wait_ge(sel_cast, 1)
            pe.wait_ge(whi_ready, 1)
            pe.wait_ge(wlo_ready, 1)
            pe.wait_ge(set_up, 5)

            with pe.Fori(0, PAIRS) as n:
                for stage, b in SCHEDULE:
                    if stage == "turn":
                        for s, (kind, src) in enumerate((("cT", cin), ("xT", xn))):
                            if kind == "cT":
                                pe.wait_ge(*c_in[b].of(n, 1))
                            else:
                                pe.wait_ge(*xn_ready.of(n, b + 1))
                            pe.wait_ge(*emptied(n, (kind, b)))
                            for d in range(KD):
                                for t in range(T):
                                    mm = pe.transpose(bank((kind, b))[:, d * N + t * P:d * N + (t + 1) * P],
                                                      src[:, b, t, d * P:(d + 1) * P], ident[:, :])
                            mm.then_inc(fills((kind, b)), 1)
                    if stage == "proj":
                        pe.wait_ge(*lo_ready.of(n, 2 * b + 2))
                        for w, c in enumerate("kqv"):
                            s = 1 if c == "q" else 0
                            pe.wait_ge(*emptied(n, (c, b)))
                            for m in range(2):
                                for i, (a, z) in enumerate(((hi, whi), (hi, wlo), (lo, whi))):
                                    for d in range(KD):
                                        at, wt = a[:, b, s, d], z[:, w, d]
                                        if c == "v":
                                            fixed, moving = at[:, m * P:(m + 1) * P], wt
                                        else:
                                            fixed, moving = wt[:, m * P:(m + 1) * P], at
                                        mm = pe.matmul(bank((c, b))[:, m * N:(m + 1) * N], fixed, moving,
                                                       start=(i == 0 and d == 0), stop=(i == 2 and d == KD - 1))
                            mm.then_inc(fills((c, b)), 1)
                    if stage == "max":
                        pe.wait_ge(*stacks_in[b].of(n, 2 * len(PART_PAIRS)))
                        for h in range(XH):
                            pe.wait_ge(*emptied(n, ("s", b, h)))
                            for t in range(T):
                                mm = pe.matmul(bank(("s", b, h))[:, t * N:(t + 1) * N], stack[:, b, 1, h, t * P:(t + 1) * P],
                                               stack[:, b, 0, h, :], start=True, stop=True)
                            mm.then_inc(fills(("s", b, h)), 1)
                        pe.wait_ge(*max_ready.of(n, XH * (b + 1)))
                        pe.wait_ge(*emptied(n, ("mT", b)))
                        for t in range(T):
                            mm = pe.transpose(bank(("mT", b))[0:XH, t * P:(t + 1) * P], nm[:, b, t, :], ident[:, :])
                        mm.then_inc(fills(("mT", b)), 1)
                    if stage == "attend":
                        def scores(h):
                            pe.wait_ge(*emptied(n, ("e", b, h)))
                            for k in range(T):
                                to = bank(("e", b, h))[:, k * N:(k + 1) * N]
                                pe.matmul(to, stack[:, b, 0, h, k * P:(k + 1) * P], stack[:, b, 1, h, :],
                                          start=True, stop=False)
                                mm = pe.matmul(to, sel[:, h, :], mrow[:, b, :], start=False, stop=True)
                            mm.then_inc(fills(("e", b, h)), 1)

                        def values(h):
                            g, c, q = h // 8, h // 4 % 2, VW * (h % 4)
                            if h % 8 == 0:
                                pe.wait_ge(*emptied(n, ("pv", b, g)))
                            pe.wait_ge(*probs_ready.of(n, XH * b + h + 1))
                            for k in range(T):
                                mm = pe.matmul(bank(("pv", b, g))[q:q + VW, c * N:(c + 1) * N], va[:, b, k, h, :],
                                               probs[:, (XH * b + h) % SLOTS, k * N:(k + 1) * N],
                                               start=(k == 0), stop=(k == T - 1))
                            mm.then_inc(probs_used.sem, 1)

                        pe.wait_ge(*m2_ready.of(n, b + 1))
                        pe.wait_ge(*v_ready.of(n, b + 1))
                        scores(0)
                        scores(1)
                        for h in range(XH):
                            if h + 2 < XH:
                                scores(h + 2)
                            values(h)
                    if stage == "out":
                        pe.wait_ge(*oT_ready.of(n, 2 * b + 2))
                        for t in range(T):
                            pe.wait_ge(*emptied(n, ("o", b, t)))
                            for g in range(4):
                                mm = pe.transpose(bank(("o", b, t))[:, g * P:(g + 1) * P],
                                                  oT[:, b, g, t * P:(t + 1) * P], ident[:, :])
                            mm.then_inc(fills(("o", b, t)), 1)

        @block.scalar
        def _(act):
            act.wait_ge(consts_in, 16 * 8)
            act.activation(sel[:, :, :], sel_f[:, :, :], ACT.Copy).then_inc(sel_cast, 1)
            act.activation(whi[:, :, :, :], wraw[:, :, :, :], ACT.Copy).then_inc(whi_ready, 1)
            act.wait_ge(set_up, 5)

            with act.Fori(0, PAIRS) as n:
                for stage, b in SCHEDULE:
                    if stage == "turn":
                        for s, kind in enumerate(("cT", "xT")):
                            act.wait_ge(*full(n, (kind, b)))
                            act.activation(hi[:, b, s], bank((kind, b))[:, :].rearrange("p (k t) -> p k t", k=KD),
                                           ACT.Copy).then_inc(hi_ready.sem, 1)
                    if stage == "proj":
                        for c in range(2):
                            act.wait_ge(*qk_ready.of(n, 2 * b + c + 1))
                            act.activation(parts[:, b, c, 0], qk[:, b, c], ACT.Copy).then_inc(p1_ready.sem, 1)
                        for c in range(2):
                            act.wait_ge(*rest_ready.of(n, 2 * b + c + 1))
                            act.activation(parts[:, b, c, 1], rest[:, b, c], ACT.Copy).then_inc(p2_ready.sem, 1)
                    if stage == "max":
                        act.wait_ge(*full(n, ("mT", b)))
                        act.activation(mrow[0:XH, b, :], bank(("mT", b))[0:XH, 0:N], ACT.Copy).then_inc(m1_ready.sem, 1)
                    if stage == "attend":
                        def output(g):
                            act.wait_ge(*probs_used.of(n, XH * b + 8 * (g + 1)))
                            act.activation(oT[:, b, 2 * g:2 * g + 2],
                                           bank(("pv", b, g))[:, :].rearrange("p (g t) -> p g t", g=2),
                                           ACT.Copy).then_inc(oT_ready.sem, 1)

                        for h in range(XH):
                            i = XH * b + h
                            act.wait_ge(*full(n, ("e", b, h)))
                            act.wait_ge(*(probs_used.of(n, i + 1 - SLOTS) if i >= SLOTS
                                          else probs_used.before(n, 2 * XH + i + 1 - SLOTS)))
                            act.activation(probs[:, i % SLOTS, :], bank(("e", b, h))[:, :],
                                           ACT.Exp).then_inc(probs_ready.sem, 1)
                            if h == 8 + SLOTS:
                                output(0)
                        output(1)

        @block.gpsimd
        def _(pool):
            pool.memset(mhalf[:, :], -0.5).then_inc(set_up, 1)
            pool.memset(eps[:, :], EPS).then_inc(set_up, 1)
            pool.memset(mrow[:, :, :], 0.0).then_inc(set_up, 1)
            pool.memset(va[:, :, :, :, XD:VW], 0.0).then_inc(set_up, 1)
            pool.wait_ge(set_up, 4)
            pool.memset(va[:, :, :, :, XD:XD + 1], 1.0).then_inc(set_up, 1)

            with pool.Fori(0, PAIRS) as n:
                for stage, b in SCHEDULE:
                    if stage in ("ln", "out"):
                        s = 0 if stage == "ln" else 1
                        k = b + 1 if s == 0 else b + 3
                        pool.wait_ge(*var_ready.of(n, k))
                        pool.tensor_tensor(veps[:, b, s], mv[:, b, s, :, 1], eps[:, :], ALU.add).then_inc(eps_added.sem, 1)
                        pool.wait_ge(*eps_added.of(n, k))
                        pool.tensor_tensor(rstd[:, b, s], veps[:, b, s], mhalf[:, :], ALU.pow).then_inc(rstd_ready.sem, 1)
                    if stage == "proj":
                        for c in range(2):
                            pool.wait_ge(*p2_ready.of(n, 2 * b + c + 1))
                            pool.tensor_tensor(parts[:, b, c, 2], rest[:, b, c], parts[:, b, c, 1],
                                               ALU.subtract).then_inc(p3_ready.sem, 1)

        @block.vector
        def _(dve):
            dve.wait_ge(whi_ready, 1)
            dve.tensor_tensor(wlo[:, :, :, :], wraw[:, :, :, :], whi[:, :, :, :].bitcast(F32),
                              ALU.subtract).then_inc(wlo_ready, 1)
            dve.wait_ge(set_up, 5)

            def layernorm(n, b, s, src, dst, ready):
                k = b + 1 if s == 0 else b + 3
                for t in range(T):
                    last = dve.bn_stats(stats[:, b, s, t], src[:, b, t])
                last.then_inc(stats_ready.sem, 1)
                dve.wait_ge(*stats_ready.of(n, k))
                dve.tensor_copy(carrier[:, :], stats[:, b, s, :, 0])
                for t in range(T):
                    last = dve.bn_aggr(mv[:, b, s, t], stats[:, b, s, t])
                last.then_inc(var_ready.sem, 1)
                dve.wait_ge(*rstd_ready.of(n, k))
                for t in range(T):
                    last = dve.tensor_scalar(dst[:, b, t], src[:, b, t], mv[:, b, s, t, 0:1], rstd[:, b, s, t:t + 1],
                                             ALU.subtract, ALU.mult)
                last.then_inc(ready.sem, 1)

            with dve.Fori(0, PAIRS) as n:
                for stage, b in SCHEDULE:
                    if stage == "ln":
                        dve.wait_ge(*x_in[b].of(n, 1))
                        layernorm(n, b, 0, xin, xn, xn_ready)
                    if stage == "turn":
                        for s, kind in enumerate(("cT", "xT")):
                            dve.wait_ge(*hi_ready.of(n, 2 * b + s + 1))
                            dve.tensor_tensor(lo[:, b, s], bank((kind, b))[:, :].rearrange("p (k t) -> p k t", k=KD),
                                              hi[:, b, s].bitcast(F32), ALU.subtract).then_inc(lo_ready.sem, 1)
                    if stage == "proj":
                        for c, kind in enumerate("kq"):
                            dve.wait_ge(*full(n, (kind, b)))
                            for m in range(KD):
                                last = dve.tensor_scalar(qk[:, b, c, m], bank((kind, b))[:, m * N:(m + 1) * N],
                                                         bqk[:, c, m:m + 1], XD ** -0.5 if kind == "q" else 1.0,
                                                         ALU.add, ALU.mult)
                            last.then_inc(qk_ready.sem, 1)
                        for c in range(2):
                            dve.wait_ge(*p1_ready.of(n, 2 * b + c + 1))
                            dve.tensor_tensor(rest[:, b, c], qk[:, b, c], parts[:, b, c, 0],
                                              ALU.subtract).then_inc(rest_ready.sem, 1)
                        dve.wait_ge(*full(n, ("v", b)))
                        for t in range(T):
                            last = dve.tensor_tensor(va[:, b, t, :, 0:XD],
                                                     bank(("v", b))[:, t * N:(t + 1) * N].rearrange("p (h r) -> p h r", r=XD),
                                                     bv[:, :].rearrange("p (h r) -> p h r", r=XD), ALU.add)
                        last.then_inc(v_ready.sem, 1)
                    if stage == "max":
                        for h in range(XH):
                            dve.wait_ge(*full(n, ("s", b, h)))
                            dve.tensor_reduce(nm[:, b, :, h], bank(("s", b, h))[:, :].rearrange("p (t k) -> p t k", t=T),
                                              AX_X, ALU.max, negate=True).then_inc(max_ready.sem, 1)
                        dve.wait_ge(*m1_ready.of(n, b + 1))
                        dve.tensor_tensor(mrow[32:32 + XH, b, :], bank(("mT", b))[0:XH, 0:N], mrow[0:XH, b, :],
                                          ALU.subtract).then_inc(m2_ready.sem, 1)
                    if stage == "out":
                        for t in range(T):
                            k = T * b + t + 1
                            o = bank(("o", b, t))[:, :].rearrange("p (h r) -> p h r", r=VW)
                            dve.wait_ge(*full(n, ("o", b, t)))
                            dve.reciprocal(rden[:, b, t], o[:, :, XD]).then_inc(rden_ready.sem, 1)
                            dve.wait_ge(*rden_ready.of(n, k))
                            if t == 0:
                                dve.wait_ge(*x1_out[b].before(n, 1))
                            dve.tensor_tensor(x1[:, b, t].rearrange("p (h r) -> p h r", r=XD), o[:, :, 0:XD],
                                              rden[:, b, t].unsqueeze(2).to_broadcast([P, XH, XD]),
                                              ALU.mult).then_inc(att_ready.sem, 1)
                            dve.wait_ge(*att_ready.of(n, k))
                            dve.tensor_tensor(x1[:, b, t], x1[:, b, t], xin[:, b, t], ALU.add).then_inc(x1_ready.sem, 1)
                        dve.wait_ge(*x1_ready.of(n, T * (b + 1)))
                        dve.wait_ge(*y_out[b].before(n, 1))
                        layernorm(n, b, 1, x1, y, y_ready)


def layers(nc, io, dram, out):
    SCHEDULE = [("turn", 0), ("turn", 1), ("qkv", 0), ("qkv", 1), ("qkT", 0), ("max", 0), ("attend", 0),
                ("qkT", 1), ("share", 0), ("max", 1), ("wo", 0), ("attend", 1), ("hturn", 0), ("w1a", 0),
                ("share", 1), ("w1b", 0), ("wo", 1), ("w2", 0), ("hturn", 1), ("w1a", 1), ("w1b", 1), ("w2", 1)]
    HALVES = {"w1a": range(0, J // 2), "w1b": range(J // 2, J)}
    ring, sums, own = (0, 1, 2, 3, 4), (5,), (6, 7)
    order = []
    for stage, b in SCHEDULE:
        if stage == "turn":
            order += [(ring, ("yT", b))]
        if stage == "qkv":
            order += [(ring, ("qkv", b, t, c)) for t in range(T) for c in range(3)]
        if stage == "qkT":
            order += [(ring, ("qkT", b, g, c)) for g in range(2) for c in range(2)]
        if stage == "max":
            order += [(ring, ("s", b, h)) for h in range(H)] + [(ring, ("mT", b))]
        if stage == "attend":
            order += [(ring, ("e", b, h)) for h in range(H)]
            order += [(own, ("pv", b, g)) for g in range(2)] + [(sums, ("sum", b))]
        if stage == "share":
            order += [(ring, ("share", b, g)) for g in range(2)]
        if stage == "wo":
            order += [(ring, ("wo", b))]
        if stage == "hturn":
            order += [(ring, ("hT", b))]
        if stage in HALVES:
            order += [(ring, ("w1", b, j)) for j in HALVES[stage]]
        if stage == "w2":
            order += [(ring, ("w2", b))]
    units, per_bank = place(order)
    signals = []
    ctx = ExitStack()
    with ctx:
        def sb(name, shape, dt):
            return ctx.enter_context(nc.sbuf_tensor("l_" + name, shape, dt))

        def signal(name, per_round, by=1):
            signals.append(Signal(ctx.enter_context(nc.semaphore("l_" + name)), per_round, by))
            return signals[-1]

        def sem(name):
            return ctx.enter_context(nc.semaphore("l_" + name))

        psum = [ctx.enter_context(nc.psum_tensor(f"l_ps{i}", [P, 512], F32)) for i in range(8)]
        ident = sb("ident", [P, P], F32)
        ident_b = sb("ident_b", [P, P], BF16)
        masks = sb("masks", [P, 2, T, N], BF16)
        sel = sb("sel", [P, H, P], BF16)
        ones = sb("ones", [P, 2, 32], F32)
        spread = sb("spread", [P, HP, P], F32R)
        turns = sb("turns", [P, 2, 2, T, HD], F32)
        mhalf = sb("mhalf", [P, H], F32)
        zero_row = sb("zero_row", [1, P], F32)
        scale = sb("scale", [P, 2, 2, HD], F32)
        table = sb("table", [P, 2, 2, T, HD], F32)
        wqkv = [sb("wqkv" + s, [P, KD, 3 * INNER], F32R) for s in ("hi", "lo")]
        wo = [sb("wo" + s, [P, HP, D], F32R) for s in ("hi", "lo")]
        w1 = [sb("w1" + s, [P, KD, 2 * HID + P - HID_LAST], F32R) for s in ("hi", "lo")]
        w2 = [sb("w2" + s, [P, J, D], F32R) for s in ("hi", "lo")]
        b1 = sb("b1", [P, 2, J], F32)
        b2 = sb("b2", [P, D], F32)
        ln = sb("ln", [P, 2, KD], F32)
        yn = sb("yn", [P, 2, T, D], F32)
        y1 = sb("y1", [P, 2, T, D], F32)
        h = sb("h", [P, 2, T, D], F32)
        x1 = sb("x1", [P, 2, T, D], F32)
        flat = [sb("yT" + s, [P, 2, 2 * (N + GAP)], F32R) for s in ("hi", "lo")]
        rot = sb("rot", [P, 10, INNER], F32)
        sq = sb("sq", [P, 2, INNER], F32)
        ssq = sb("ssq", [P, 2, T, 2, H], F32)
        rnorm = sb("rnorm", [P, 2, T, 2, H], F32)
        q = [sb("q" + s, [P, 2, HP, 2, N], F32R) for s in ("hi", "lo")]
        k = [sb("k" + s, [P, 2, HP, N], F32R) for s in ("hi", "lo")]
        v = sb("v", [P, 2, T, INNER], F32)
        nm = sb("nm", [P, 2, T, H], F32)
        mrow = sb("mrow", [P, 2, N], BF16)
        probs = sb("probs", [P, SLOTS, N + P], F32)
        share = [sb("share" + s, [P, N], dt) for s, dt in (("", F32), ("hi", F32R), ("lo", F32R))]
        stats = sb("stats", [P, 2, T, 6], F32)
        mv = sb("mv", [P, 2, T, 2], F32)
        veps = sb("veps", [P, 2, T], F32)
        eps = sb("eps", [P, T], F32)
        carrier = sb("carrier", [P, T], F32)
        rstd = sb("rstd", [P, 2, T], F32)
        u = [sb("u" + s, [P, J, N], F32R) for s in ("hi", "lo")]
        uf = sb("uf", [P, 2, N], F32)
        z = sq[:, 0]
        gate = sq[:, 1].rearrange("p (s t) -> p s t", s=2)

        consts_in, consts_cast, set_up = sem("consts_in"), sem("consts_cast"), sem("set_up")
        raw_a, raw_b = signal("raw_a", 2, 16), signal("raw_b", 3, 16)
        small_in = signal("small_in", 13, 16)
        table_ready = signal("table_ready", 1)
        hi_a, lo_a, hi_b, lo_b = signal("hi_a", 1), signal("lo_a", 1), signal("hi_b", 1), signal("lo_b", 1)
        filled = {i: signal(f"filled{i}", m) for i, m in per_bank.items()}
        y_in = [signal(f"y_in{b}", 1, 16) for b in range(2)]
        x1_in = [signal(f"x1_in{b}", 1, 16) for b in range(2)]
        yT_hi, yT_lo = signal("yT_hi", 2), signal("yT_lo", 2)
        sq_ready, ssq_sum, ssq_ready = signal("sq_ready", 8), signal("ssq_sum", 8), signal("ssq_ready", 8)
        terms_ready, norm_ready, sum_ready = signal("terms_ready", 8), signal("norm_ready", 8), signal("sum_ready", 8)
        qk_ready, v_ready = signal("qk_ready", 8), signal("v_ready", 4)
        turned_hi, turned_lo = signal("turned_hi", 8), signal("turned_lo", 8)
        max_ready = signal("max_ready", 2 * H)
        m1_ready, m2_ready = signal("m1_ready", 2), signal("m2_ready", 2)
        probs_ready, probs_used = signal("probs_ready", 2 * H), signal("probs_used", 2 * H)
        o_ready = signal("o_ready", 4)
        share_ready, share_hi, share_lo = signal("share_ready", 2), signal("share_hi", 2), signal("share_lo", 2)
        divided, o_hi, o_lo = signal("divided", 4), signal("o_hi", 4), signal("o_lo", 4)
        y1_ready = signal("y1_ready", 2)
        shifted = [signal(f"shifted{b}", 5, 16) for b in range(2)]
        stats_ready, var_ready = signal("stats_ready", 2), signal("var_ready", 2)
        eps_added, rstd_ready = signal("eps_added", 2), signal("rstd_ready", 2)
        h_ready, z_ready, z_hi, z_lo = signal("h_ready", 2), signal("z_ready", 2), signal("z_hi", 2), signal("z_lo", 2)
        y1b_ready = signal("y1b_ready", 2)
        gate_ready, uf_ready = signal("gate_ready", 2 * J), signal("uf_ready", 2 * J)
        u_hi, u_lo = signal("u_hi", 2 * J), signal("u_lo", 2 * J)
        y2_ready, out_ready = signal("y2_ready", 2), signal("out_ready", 2)
        y_out = [signal(f"y_out{b}", 1, 16) for b in range(2)]
        out_out = [signal(f"out_out{b}", 1, 16) for b in range(2)]

        reader = {
            "yT": lambda b: (yT_lo, b + 1),
            "qkv": lambda b, t, c: (terms_ready, 4 * b + 2 * t + c + 1) if c < 2 else (v_ready, T * b + t + 1),
            "qkT": lambda b, g, c: (turned_lo, 4 * b + 2 * g + c + 1),
            "s": lambda b, head: (max_ready, H * b + head + 1), "mT": lambda b: (m2_ready, b + 1),
            "e": lambda b, head: (probs_ready, H * b + head + 1),
            "pv": lambda b, g: (o_ready, 2 * b + g + 1), "sum": lambda b: (share_ready, b + 1),
            "share": lambda b, g: (divided, 2 * b + g + 1), "wo": lambda b: (y1_ready, b + 1),
            "hT": lambda b: (z_ready, b + 1), "w1": lambda b, j: (uf_ready, J * b + j + 1),
            "w2": lambda b: (y2_ready, b + 1),
        }

        def bank(*unit):
            return psum[units[unit][0]]

        def full(n, *unit):
            return filled[units[unit][0]].of(n, units[unit][1])

        def fills(*unit):
            return filled[units[unit][0]].sem

        def emptied(n, *unit):
            _, _, last, same_round = units[unit]
            by, m = reader[last[0]](*last[1:])
            return by.of(n, m) if same_round else by.before(n, m)

        def halves(tile, b):
            return tile[:, b].rearrange("p (d c) -> p d c", d=2)[:, :, 0:N]

        products = ((0, 0), (0, 1), (1, 0))

        for s in signals:
            nc.sync.sem_inc(s.sem, s.per_round * s.by)

        block = ctx.enter_context(nc.Block())

        @block.sync
        def _(sp):
            sp.dma_start(ident[:, :], io["c_ident"]).then_inc(consts_in, 16)
            sp.dma_start(ones[:, :, :], io["c_ones"]).then_inc(consts_in, 16)
            for c in range(2):
                for s in range(2):
                    sp.dma_start(turns[:, c, s], io["c_rot"][c, s].rearrange("(t p) d -> p t d", p=P)).then_inc(consts_in, 16)
            sp.dma_start(rot[:, 0:2].rearrange("p a (t n) -> p a t n", t=T), io["c_masks"]).then_inc(consts_in, 16)
            sp.dma_start(rot[:, 2:4].rearrange("p a (h c) -> p (a h) c", c=P), io["c_sel"][:, 0:H]).then_inc(consts_in, 16)
            sp.dma_start(rot[:, 4].rearrange("p (h c) -> p h c", c=P), io["c_spread"]).then_inc(consts_in, 16)
            sp.wait_ge(consts_cast, 4)

            with sp.Fori(0, LAYERS) as l:
                sp.wait_ge(*y2_ready.before(l * PAIRS, 2))
                raw = rot[:, :, :].rearrange("p a c -> p (a c)")
                nq = KD * 3 * INNER
                sp.dma_start(raw[:, 0:nq].rearrange("p (k n) -> p k n", k=KD),
                             io["wqkv"][l].rearrange("(k p) n -> p k n", p=P)).then_inc(raw_a.sem, 16)
                sp.dma_start(raw[:, nq:nq + HP * D].rearrange("p (k n) -> p k n", k=HP),
                             io["wo"][l].rearrange("(k p) n -> p k n", p=P)).then_inc(raw_a.sem, 16)
                half = HD // 2
                for c, name in enumerate(("q_scale", "k_scale")):
                    src = io[name][l]
                    sp.dma_start(scale[:, c, 0], src.partition_broadcast(P)).then_inc(small_in.sem, 16)
                    sp.dma_start(scale[:, c, 1, 0:half], src[half:HD].partition_broadcast(P)).then_inc(small_in.sem, 16)
                    sp.dma_start(scale[:, c, 1, half:HD], src[0:half].partition_broadcast(P)).then_inc(small_in.sem, 16)
                for c in range(2):
                    src = io["b1"][l][c * HID:(c + 1) * HID]
                    m = (J - 1) * P
                    sp.dma_start(b1[:, c, 0:J - 1], src[0:m].rearrange("(j p) -> p j", p=P),
                                 allow_slow_non_contiguous=True).then_inc(small_in.sem, 16)
                    sp.dma_start(b1[0:HID_LAST, c, J - 1:J], src[m:HID].rearrange("(p j) -> p j", j=1),
                                 allow_slow_non_contiguous=True).then_inc(small_in.sem, 16)
                sp.dma_start(b2[:, :], io["b2"][l].partition_broadcast(P)).then_inc(small_in.sem, 16)
                for c, name in enumerate(("ln_g", "ln_b")):
                    sp.dma_start(ln[:, c], io[name][l].rearrange("(k p) -> p k", p=P),
                                 allow_slow_non_contiguous=True).then_inc(small_in.sem, 16)
                sp.wait_ge(*lo_a.of(l, 1))
                n1 = KD * 2 * HID
                sp.dma_start(raw[:, 0:n1].rearrange("p (k n) -> p k n", k=KD),
                             io["w1"][l].rearrange("(k p) n -> p k n", p=P)).then_inc(raw_b.sem, 16)
                sp.dma_start(raw[:, n1:n1 + (J - 1) * D].rearrange("p (k n) -> p k n", k=J - 1),
                             io["w2"][l, 0:(J - 1) * P].rearrange("(k p) n -> p k n", p=P)).then_inc(raw_b.sem, 16)
                sp.dma_start(raw[0:HID_LAST, n1 + (J - 1) * D:n1 + J * D], io["w2"][l, (J - 1) * P:HID]).then_inc(raw_b.sem, 16)

                with sp.Fori(0, PAIRS) as i:
                    n = l * PAIRS + i
                    for b in range(2):
                        sp.wait_ge(*y1_ready.before(n, b + 1))
                        sp.dma_start(yn[:, b], dram["y"][i * 2 + b].rearrange("(t p) d -> p t d", p=P)).then_inc(y_in[b].sem, 16)
                        sp.wait_ge(*out_out[b].before(n, 1))
                        sp.dma_start(x1[:, b], dram["x1"][i * 2 + b].rearrange("(t p) d -> p t d", p=P)).then_inc(x1_in[b].sem, 16)
                    for stage, b in SCHEDULE:
                        if stage == "wo":
                            sp.wait_ge(*y1_ready.of(n, b + 1))
                            sp.wait_ge(*y_out[b].before(n, 1))
                            s = shifted[b].sem
                            sp.dma_start(h[:, b, :, 0:P], y1[:, b, :, 0:P]).then_inc(s, 16)
                            sp.dma_start(h[1:113, b, :, P:D], y1[0:112, b, :, P:D]).then_inc(s, 16)
                            sp.dma_start(h[113:P, b, :, P:D], y1[112:P - 1, b, :, P:D]).then_inc(s, 16)
                            sp.dma_start(h[0:1, b, 1, P:D], y1[P - 1:P, b, 0, P:D]).then_inc(s, 16)
                            sp.dma_start(h[0:1, b, 0, P:D], zero_row[:, :]).then_inc(s, 16)
                        if stage == "w2":
                            sp.wait_ge(*y2_ready.of(n, b + 1))
                            sp.dma_start(dram["y"][i * 2 + b].rearrange("(t p) d -> p t d", p=P), h[:, b]).then_inc(y_out[b].sem, 16)
                            sp.wait_ge(*out_ready.of(n, b + 1))
                            sp.dma_start(out[i * 2 + b].rearrange("(t p) d -> p t d", p=P), x1[:, b]).then_inc(out_out[b].sem, 16)
            for b in range(2):
                sp.wait_ge(*y_out[b].of(ROUNDS - 1, 1))
                sp.wait_ge(*out_out[b].of(ROUNDS - 1, 1))

        @block.tensor
        def _(pe):
            pe.wait_ge(consts_cast, 4)
            pe.wait_ge(consts_in, 16 * 9)
            pe.wait_ge(set_up, 14)

            def start_of(kind, b, d):
                return 0 if d == 0 else N + GAP - (1 if kind == "y" else 0)

            with pe.Fori(0, LAYERS) as l:
                with pe.Fori(0, PAIRS) as i:
                    n = l * PAIRS + i
                    for stage, b in SCHEDULE:
                        if stage in ("turn", "hturn"):
                            kind, src = ("yT", yn) if stage == "turn" else ("hT", h)
                            if stage == "turn":
                                pe.wait_ge(*y_in[b].of(n, 1))
                            else:
                                pe.wait_ge(*h_ready.of(n, b + 1))
                            pe.wait_ge(*emptied(n, kind, b))
                            for d in range(KD):
                                for t in range(T):
                                    mm = pe.transpose(bank(kind, b)[:, d * N + t * P:d * N + (t + 1) * P],
                                                      src[:, b, t, d * P:(d + 1) * P], ident[:, :])
                            mm.then_inc(fills(kind, b), 1)
                        if stage == "qkv":
                            if b == 0:
                                pe.wait_ge(*lo_a.of(l, 1))
                            pe.wait_ge(*yT_lo.of(n, b + 1))
                            for t in range(T):
                                for c in range(3):
                                    pe.wait_ge(*emptied(n, "qkv", b, t, c))
                                    for e, (x, w) in enumerate(products):
                                        for d in range(KD):
                                            at = start_of("y", b, d) + t * P
                                            mm = pe.matmul(bank("qkv", b, t, c)[:, :], flat[x][:, b, at:at + P],
                                                           wqkv[w][:, d, c * INNER:(c + 1) * INNER],
                                                           start=(e == 0 and d == 0), stop=(e == 2 and d == KD - 1))
                                    mm.then_inc(fills("qkv", b, t, c), 1)
                        if stage == "qkT":
                            pe.wait_ge(*qk_ready.of(n, 4 * b + 4))
                            for g in range(2):
                                for c in range(2):
                                    pe.wait_ge(*emptied(n, "qkT", b, g, c))
                                    for pr in range(2):
                                        for t in range(T):
                                            at = (2 * g + pr) * P
                                            mm = pe.transpose(bank("qkT", b, g, c)[:, pr * N + t * P:pr * N + (t + 1) * P],
                                                              rot[:, 4 * b + 2 * t + c, at:at + P], ident[:, :])
                                    mm.then_inc(fills("qkT", b, g, c), 1)
                        if stage == "max":
                            for head in range(H):
                                pr, par = head // 2, head % 2
                                if head % 4 == 0:
                                    pe.wait_ge(*turned_hi.of(n, 4 * b + 2 * (head // 4) + 2))
                                pe.wait_ge(*emptied(n, "s", b, head))
                                for t in range(T):
                                    to = bank("s", b, head)[:, t * N:(t + 1) * N]
                                    pe.matmul(to, q[0][:, b, pr, par, t * P:(t + 1) * P], k[0][:, b, pr, :],
                                              start=True, stop=False)
                                    mm = pe.matmul(to, ident_b[:, :], masks[:, 0, t, :], start=False, stop=True)
                                mm.then_inc(fills("s", b, head), 1)
                            pe.wait_ge(*max_ready.of(n, H * (b + 1)))
                            pe.wait_ge(*emptied(n, "mT", b))
                            for t in range(T):
                                mm = pe.transpose(bank("mT", b)[0:H, t * P:(t + 1) * P], nm[:, b, t, :], ident[:, :])
                            mm.then_inc(fills("mT", b), 1)
                        if stage == "attend":
                            def scores(head):
                                pr, par = head // 2, head % 2
                                pe.wait_ge(*emptied(n, "e", b, head))
                                for t in range(T):
                                    to = bank("e", b, head)[:, t * N:N + t * P]
                                    for e, (x, y) in enumerate(products):
                                        pe.matmul(to, k[y][:, b, pr, t * P:(t + 1) * P], q[x][:, b, pr, par, t * P:N],
                                                  start=(e == 0), stop=False)
                                    pe.matmul(to, ident_b[:, :], masks[:, 1, t, t * P:N], start=False, stop=False)
                                    mm = pe.matmul(to, sel[:, head, :], mrow[:, b, t * P:N], start=False, stop=True)
                                mm.then_inc(fills("e", b, head), 1)

                            def values(head):
                                g, pr, par, r = head // 4, head // 2 % 2, head % 2, 32 * (head % 4)
                                if head % 4 == 0:
                                    pe.wait_ge(*emptied(n, "pv", b, g))
                                if head == 0:
                                    pe.wait_ge(*emptied(n, "sum", b))
                                pe.wait_ge(*probs_ready.of(n, H * b + head + 1))
                                p = probs[:, (H * b + head) % SLOTS]
                                for t in range(T):
                                    pe.matmul(bank("pv", b, g)[HD * par:HD * (par + 1), pr * N + t * P:(pr + 1) * N],
                                              v[:, b, t, head * HD:(head + 1) * HD], p[:, t * N:N + t * P],
                                              start=(t == 0), stop=(t == T - 1), skip_group_check=True)
                                for t in range(T):
                                    mm = pe.matmul(bank("sum", b)[r:r + 32, t * P:N], ones[:, head // 4, :],
                                                   p[:, t * N:N + t * P], start=(t == 0 and head < 4),
                                                   stop=(t == T - 1 and head >= 4), skip_group_check=True)
                                mm.then_inc(probs_used.sem, 1)

                            pe.wait_ge(*turned_lo.of(n, 4 * b + 4))
                            pe.wait_ge(*m2_ready.of(n, b + 1))
                            pe.wait_ge(*v_ready.of(n, T * (b + 1)))
                            scores(0)
                            scores(1)
                            for head in range(H):
                                if head + 2 < H:
                                    scores(head + 2)
                                values(head)
                        if stage == "share":
                            pe.wait_ge(*share_lo.of(n, b + 1))
                            for g in range(2):
                                pe.wait_ge(*emptied(n, "share", b, g))
                                for pr in range(2):
                                    for e in range(2):
                                        mm = pe.matmul(bank("share", b, g)[:, pr * N:(pr + 1) * N],
                                                       spread[:, 2 * g + pr, :], share[1 + e][:, :],
                                                       start=(e == 0), stop=(e == 1))
                                mm.then_inc(fills("share", b, g), 1)
                        if stage == "wo":
                            pe.wait_ge(*o_lo.of(n, 2 * b + 2))
                            pe.wait_ge(*emptied(n, "wo", b))
                            for t in range(T):
                                for e, (x, w) in enumerate(products):
                                    for p in range(HP):
                                        mm = pe.matmul(bank("wo", b)[:, t * D:(t + 1) * D],
                                                       k[x][:, b, p, t * P:(t + 1) * P], wo[w][:, p, :],
                                                       start=(e == 0 and p == 0), stop=(e == 2 and p == HP - 1))
                            mm.then_inc(fills("wo", b), 1)
                        if stage in HALVES:
                            if b == 0 and stage == "w1a":
                                pe.wait_ge(*lo_b.of(l, 1))
                            pe.wait_ge(*z_lo.of(n, b + 1))
                            for j in HALVES[stage]:
                                pe.wait_ge(*emptied(n, "w1", b, j))
                                for a in range(2):
                                    for e, (w, x) in enumerate(products):
                                        for d in range(KD):
                                            at, c = start_of("h", b, d), a * HID + j * P
                                            mm = pe.matmul(bank("w1", b, j)[:, a * N:(a + 1) * N], w1[w][:, d, c:c + P],
                                                           flat[x][:, b, at:at + N],
                                                           start=(e == 0 and d == 0), stop=(e == 2 and d == KD - 1))
                                mm.then_inc(fills("w1", b, j), 1)
                        if stage == "w2":
                            pe.wait_ge(*u_lo.of(n, J * (b + 1)))
                            pe.wait_ge(*emptied(n, "w2", b))
                            for t in range(T):
                                for e, (x, w) in enumerate(products):
                                    for j in range(J):
                                        mm = pe.matmul(bank("w2", b)[:, t * D:(t + 1) * D], u[x][:, j, t * P:(t + 1) * P],
                                                       w2[w][:, j, :], start=(e == 0 and j == 0),
                                                       stop=(e == 2 and j == J - 1))
                            mm.then_inc(fills("w2", b), 1)

        @block.scalar
        def _(act):
            act.wait_ge(consts_in, 16 * 9)
            act.activation(ident_b[:, :], ident[:, :], ACT.Copy).then_inc(consts_cast, 1)
            act.activation(masks[:, :, :, :], rot[:, 0:2].rearrange("p a (t n) -> p a t n", t=T), ACT.Copy).then_inc(consts_cast, 1)
            act.activation(sel[:, :, :], rot[:, 2:4].rearrange("p a (h c) -> p (a h) c", c=P), ACT.Copy).then_inc(consts_cast, 1)
            act.activation(spread[:, :, :], rot[:, 4].rearrange("p (h c) -> p h c", c=P), ACT.Copy).then_inc(consts_cast, 1)
            act.wait_ge(set_up, 14)
            raw = rot[:, :, :].rearrange("p a c -> p (a c)")
            nq, n1 = KD * 3 * INNER, KD * 2 * HID

            with act.Fori(0, LAYERS) as l:
                act.wait_ge(*raw_a.of(l, 2))
                act.activation(wqkv[0][:, :, :], raw[:, 0:nq].rearrange("p (k n) -> p k n", k=KD), ACT.Copy)
                act.activation(wo[0][:, :, :], raw[:, nq:nq + HP * D].rearrange("p (k n) -> p k n", k=HP),
                               ACT.Copy).then_inc(hi_a.sem, 1)
                act.wait_ge(*raw_b.of(l, 3))
                act.activation(w1[0][:, :, 0:2 * HID], raw[:, 0:n1].rearrange("p (k n) -> p k n", k=KD), ACT.Copy)
                act.activation(w2[0][:, 0:J - 1], raw[:, n1:n1 + (J - 1) * D].rearrange("p (k n) -> p k n", k=J - 1), ACT.Copy)
                act.activation(w2[0][0:HID_LAST, J - 1], raw[0:HID_LAST, n1 + (J - 1) * D:n1 + J * D],
                               ACT.Copy).then_inc(hi_b.sem, 1)

                with act.Fori(0, PAIRS) as i:
                    n = l * PAIRS + i
                    for stage, b in SCHEDULE:
                        if stage == "turn":
                            act.wait_ge(*full(n, "yT", b))
                            act.activation(halves(flat[0], b), bank("yT", b)[:, :].rearrange("p (d t) -> p d t", d=KD),
                                           ACT.Copy).then_inc(yT_hi.sem, 1)
                        if stage == "qkv":
                            for t in range(T):
                                for c in range(2):
                                    m = 4 * b + 2 * t + c + 1
                                    act.wait_ge(*full(n, "qkv", b, t, c))
                                    act.wait_ge(*(ssq_sum.of(n, m - 2) if m > 2 else ssq_sum.before(n, 8 + m - 2)))
                                    act.activation(sq[:, c], bank("qkv", b, t, c)[:, :], ACT.Square).then_inc(sq_ready.sem, 1)
                                act.wait_ge(*full(n, "qkv", b, t, 2))
                                act.activation(v[:, b, t], bank("qkv", b, t, 2)[:, :], ACT.Copy).then_inc(v_ready.sem, 1)
                        if stage == "qkT":
                            for g in range(2):
                                for c in range(2):
                                    act.wait_ge(*full(n, "qkT", b, g, c))
                                    src = bank("qkT", b, g, c)[:, :].rearrange("p (r t) -> p r t", r=2)
                                    if c == 0:
                                        for par in range(2):
                                            rows = slice(HD * par, HD * (par + 1))
                                            last = act.activation(q[0][rows, b, 2 * g:2 * g + 2, par], src[rows], ACT.Copy)
                                    else:
                                        last = act.activation(k[0][:, b, 2 * g:2 * g + 2], src, ACT.Copy)
                                    last.then_inc(turned_hi.sem, 1)
                        if stage == "max":
                            act.wait_ge(*full(n, "mT", b))
                            act.activation(mrow[0:H, b, :], bank("mT", b)[0:H, 0:N], ACT.Copy).then_inc(m1_ready.sem, 1)
                        if stage == "attend":
                            def output(g):
                                act.wait_ge(*probs_used.of(n, H * b + 4 * (g + 1)))
                                act.activation(v[:, b, :, g * N:(g + 1) * N],
                                               bank("pv", b, g)[:, :].rearrange("p (r t) -> p r t", r=2),
                                               ACT.Copy).then_inc(o_ready.sem, 1)

                            for head in range(H):
                                m = H * b + head
                                act.wait_ge(*full(n, "e", b, head))
                                act.wait_ge(*(probs_used.of(n, m + 1 - SLOTS) if m >= SLOTS
                                              else probs_used.before(n, 2 * H + m + 1 - SLOTS)))
                                act.activation(probs[:, m % SLOTS, :], bank("e", b, head)[:, 0:N + P],
                                               ACT.Exp).then_inc(probs_ready.sem, 1)
                                if head == 3 + SLOTS:
                                    output(0)
                            output(1)
                        if stage == "attend":
                            act.wait_ge(*share_ready.of(n, b + 1))
                            act.activation(share[1][:, :], share[0][:, :], ACT.Copy).then_inc(share_hi.sem, 1)
                        if stage == "share":
                            for g in range(2):
                                act.wait_ge(*divided.of(n, 2 * b + g + 1))
                                act.activation(k[0][:, b, 2 * g:2 * g + 2], v[:, b, :, g * N:(g + 1) * N],
                                               ACT.Copy).then_inc(o_hi.sem, 1)
                        if stage == "hturn":
                            act.wait_ge(*z_ready.of(n, b + 1))
                            act.activation(halves(flat[0], b), z.rearrange("p (d t) -> p d t", d=KD), ACT.Copy).then_inc(z_hi.sem, 1)
                        if stage in HALVES:
                            def rows(j):
                                return P if j < J - 1 else HID_LAST

                            def gelu(j):
                                m, r = J * b + j + 1, rows(j)
                                if m == 1:
                                    act.wait_ge(*small_in.of(l, 13))
                                act.wait_ge(*full(n, "w1", b, j))
                                act.wait_ge(*(uf_ready.of(n, m - 2) if m > 2 else uf_ready.before(n, 2 * J + m - 2)))
                                act.activation(gate[0:r, j % 2], bank("w1", b, j)[0:r, N:2 * N], ACT.Gelu,
                                               bias=b1[0:r, 1, j:j + 1]).then_inc(gate_ready.sem, 1)

                            def high(j):
                                r = rows(j)
                                act.wait_ge(*uf_ready.of(n, J * b + j + 1))
                                act.activation(u[0][0:r, j], uf[0:r, j % 2], ACT.Copy).then_inc(u_hi.sem, 1)

                            js = list(HALVES[stage])
                            gelu(js[0])
                            for j in js[1:]:
                                gelu(j)
                                high(j - 1)
                            high(js[-1])

        @block.gpsimd
        def _(pool):
            for i in range(2):
                pool.memset(q[i][:, :, :, :, :].bitcast(F32), 0.0).then_inc(set_up, 1)
                pool.memset(flat[i][:, :, :].bitcast(F32), 0.0).then_inc(set_up, 1)
                pool.memset(u[i][:, J - 1].bitcast(F32), 0.0).then_inc(set_up, 1)
                pool.memset(w2[i][:, J - 1].bitcast(F32), 0.0).then_inc(set_up, 1)
                pool.memset(w1[i][:, :, 2 * HID:].bitcast(F32), 0.0).then_inc(set_up, 1)
            pool.memset(mrow[:, :, :], 0.0).then_inc(set_up, 1)
            pool.memset(zero_row[:, :], 0.0).then_inc(set_up, 1)
            pool.memset(mhalf[:, :], -0.5).then_inc(set_up, 1)
            pool.memset(eps[:, :], EPS).then_inc(set_up, 1)

            with pool.Fori(0, LAYERS) as l:
                with pool.Fori(0, PAIRS) as i:
                    n = l * PAIRS + i
                    for stage, b in SCHEDULE:
                        if stage == "qkv":
                            for t in range(T):
                                for c in range(2):
                                    m = 4 * b + 2 * t + c
                                    slot = rot[:, m].rearrange("p (h d) -> p h d", d=HD)
                                    pool.wait_ge(*ssq_ready.of(n, m + 1))
                                    pool.tensor_tensor(rnorm[:, b, t, c], ssq[:, b, t, c], mhalf[:, :], ALU.pow).then_inc(norm_ready.sem, 1)
                                    pool.wait_ge(*terms_ready.of(n, m + 1))
                                    pool.tensor_tensor(rot[:, m], rot[:, m], rot[:, 8 + m % 2], ALU.add).then_inc(sum_ready.sem, 1)
                                    pool.wait_ge(*norm_ready.of(n, m + 1))
                                    pool.wait_ge(*sum_ready.of(n, m + 1))
                                    pool.tensor_tensor(slot, slot, rnorm[:, b, t, c].unsqueeze(2).to_broadcast([P, H, HD]),
                                                       ALU.mult).then_inc(qk_ready.sem, 1)
                        if stage == "share":
                            for g in range(2):
                                pool.wait_ge(*o_hi.of(n, 2 * b + g + 1))
                                pool.tensor_tensor(k[1][:, b, 2 * g:2 * g + 2], v[:, b, :, g * N:(g + 1) * N],
                                                   k[0][:, b, 2 * g:2 * g + 2].bitcast(F32), ALU.subtract).then_inc(o_lo.sem, 1)
                        if stage == "wo":
                            pool.wait_ge(*var_ready.of(n, b + 1))
                            pool.tensor_tensor(veps[:, b], mv[:, b, :, 1], eps[:, :], ALU.add).then_inc(eps_added.sem, 1)
                            pool.wait_ge(*eps_added.of(n, b + 1))
                            pool.tensor_tensor(rstd[:, b], veps[:, b], mhalf[:, 0:T], ALU.pow).then_inc(rstd_ready.sem, 1)
                        if stage == "hturn":
                            if b == 0:
                                pool.wait_ge(*small_in.of(l, 13))
                            pool.wait_ge(*full(n, "hT", b))
                            for t in range(T):
                                last = pool.tensor_tensor(h[:, b, t], y1[:, b, t], b2[:, :], ALU.add)
                            last.then_inc(y1b_ready.sem, 1)
                        if stage in HALVES:
                            for j in HALVES[stage]:
                                r = P if j < J - 1 else HID_LAST
                                pool.wait_ge(*u_hi.of(n, J * b + j + 1))
                                pool.tensor_tensor(u[1][0:r, j], uf[0:r, j % 2], u[0][0:r, j].bitcast(F32),
                                                   ALU.subtract).then_inc(u_lo.sem, 1)

        @block.vector
        def _(dve):
            dve.wait_ge(set_up, 14)
            dve.wait_ge(consts_in, 16 * 9)
            raw = rot[:, :, :].rearrange("p a c -> p (a c)")
            nq, n1 = KD * 3 * INNER, KD * 2 * HID

            with dve.Fori(0, LAYERS) as l:
                dve.wait_ge(*hi_a.of(l, 1))
                dve.tensor_tensor(wqkv[1][:, :, :], raw[:, 0:nq].rearrange("p (k n) -> p k n", k=KD),
                                  wqkv[0][:, :, :].bitcast(F32), ALU.subtract)
                dve.tensor_tensor(wo[1][:, :, :], raw[:, nq:nq + HP * D].rearrange("p (k n) -> p k n", k=HP),
                                  wo[0][:, :, :].bitcast(F32), ALU.subtract).then_inc(lo_a.sem, 1)
                dve.wait_ge(*small_in.of(l, 13))
                for c in range(2):
                    for s in range(2):
                        last = dve.tensor_tensor(table[:, c, s], turns[:, c, s],
                                                 scale[:, c, s].unsqueeze(1).to_broadcast([P, T, HD]), ALU.mult)
                last.then_inc(table_ready.sem, 1)
                dve.wait_ge(*hi_b.of(l, 1))
                dve.tensor_tensor(w1[1][:, :, 0:2 * HID], raw[:, 0:n1].rearrange("p (k n) -> p k n", k=KD),
                                  w1[0][:, :, 0:2 * HID].bitcast(F32), ALU.subtract)
                dve.tensor_tensor(w2[1][:, 0:J - 1], raw[:, n1:n1 + (J - 1) * D].rearrange("p (k n) -> p k n", k=J - 1),
                                  w2[0][:, 0:J - 1].bitcast(F32), ALU.subtract)
                dve.tensor_tensor(w2[1][0:HID_LAST, J - 1], raw[0:HID_LAST, n1 + (J - 1) * D:n1 + J * D],
                                  w2[0][0:HID_LAST, J - 1].bitcast(F32), ALU.subtract).then_inc(lo_b.sem, 1)

                with dve.Fori(0, PAIRS) as i:
                    n = l * PAIRS + i
                    for stage, b in SCHEDULE:
                        if stage == "turn":
                            dve.wait_ge(*yT_hi.of(n, b + 1))
                            dve.tensor_tensor(halves(flat[1], b), bank("yT", b)[:, :].rearrange("p (d t) -> p d t", d=KD),
                                              halves(flat[0], b).bitcast(F32), ALU.subtract).then_inc(yT_lo.sem, 1)
                        if stage == "qkv":
                            for t in range(T):
                                for c in range(2):
                                    m = 4 * b + 2 * t + c
                                    src = bank("qkv", b, t, c)[:, :].rearrange("p (h d) -> p h d", d=HD)
                                    first = rot[:, m].rearrange("p (h d) -> p h d", d=HD)
                                    second = rot[:, 8 + m % 2].rearrange("p (h d) -> p h d", d=HD)
                                    half = HD // 2
                                    dve.wait_ge(*sq_ready.of(n, m + 1))
                                    dve.tensor_reduce(ssq[:, b, t, c], sq[:, c].rearrange("p (h d) -> p h d", d=HD),
                                                      AX_X, ALU.add).then_inc(ssq_sum.sem, 1)
                                    if m == 0:
                                        dve.wait_ge(*table_ready.of(l, 1))
                                    dve.tensor_tensor(first, src, table[:, c, 0, t].unsqueeze(1).to_broadcast([P, H, HD]), ALU.mult)
                                    dve.wait_ge(*(sum_ready.of(n, m - 1) if m >= 2 else sum_ready.before(n, 8 + m - 1)))
                                    dve.tensor_tensor(second[:, :, 0:half], src[:, :, half:HD],
                                                      table[:, c, 1, t, 0:half].unsqueeze(1).to_broadcast([P, H, half]), ALU.mult)
                                    dve.tensor_tensor(second[:, :, half:HD], src[:, :, 0:half],
                                                      table[:, c, 1, t, half:HD].unsqueeze(1).to_broadcast([P, H, half]),
                                                      ALU.mult).then_inc(terms_ready.sem, 1)
                                    dve.wait_ge(*ssq_sum.of(n, m + 1))
                                    dve.tensor_scalar(ssq[:, b, t, c], ssq[:, b, t, c], NORM_FLOOR ** 2, None,
                                                      ALU.max).then_inc(ssq_ready.sem, 1)
                        if stage == "qkT":
                            for g in range(2):
                                for c in range(2):
                                    dve.wait_ge(*turned_hi.of(n, 4 * b + 2 * g + c + 1))
                                    src = bank("qkT", b, g, c)[:, :].rearrange("p (r t) -> p r t", r=2)
                                    if c == 0:
                                        for par in range(2):
                                            rows = slice(HD * par, HD * (par + 1))
                                            last = dve.tensor_tensor(q[1][rows, b, 2 * g:2 * g + 2, par], src[rows],
                                                                     q[0][rows, b, 2 * g:2 * g + 2, par].bitcast(F32), ALU.subtract)
                                    else:
                                        last = dve.tensor_tensor(k[1][:, b, 2 * g:2 * g + 2], src,
                                                                 k[0][:, b, 2 * g:2 * g + 2].bitcast(F32), ALU.subtract)
                                    last.then_inc(turned_lo.sem, 1)
                        if stage == "max":
                            for head in range(H):
                                dve.wait_ge(*full(n, "s", b, head))
                                dve.tensor_reduce(nm[:, b, :, head], bank("s", b, head)[:, :].rearrange("p (t c) -> p t c", t=T),
                                                  AX_X, ALU.max, negate=True).then_inc(max_ready.sem, 1)
                            dve.wait_ge(*m1_ready.of(n, b + 1))
                            dve.tensor_tensor(mrow[32:32 + H, b, :], bank("mT", b)[0:H, 0:N], mrow[0:H, b, :],
                                              ALU.subtract).then_inc(m2_ready.sem, 1)
                        if stage == "attend":
                            dve.wait_ge(*probs_used.of(n, H * (b + 1)))
                            dve.reciprocal(share[0][:, :], bank("sum", b)[:, 0:N]).then_inc(share_ready.sem, 1)
                            dve.wait_ge(*share_hi.of(n, b + 1))
                            dve.tensor_tensor(share[2][:, :], share[0][:, :], share[1][:, :].bitcast(F32),
                                              ALU.subtract).then_inc(share_lo.sem, 1)
                        if stage == "share":
                            for g in range(2):
                                dve.wait_ge(*full(n, "share", b, g))
                                dve.wait_ge(*o_ready.of(n, 2 * b + g + 1))
                                o = v[:, b, :, g * N:(g + 1) * N]
                                dve.tensor_tensor(o, bank("share", b, g)[:, :].rearrange("p (r t) -> p r t", r=2), o,
                                                  ALU.mult).then_inc(divided.sem, 1)
                        if stage == "wo":
                            dve.wait_ge(*full(n, "wo", b))
                            dve.tensor_tensor(y1[:, b], bank("wo", b)[:, :].rearrange("p (t d) -> p t d", t=T), yn[:, b],
                                              ALU.add).then_inc(y1_ready.sem, 1)
                            dve.wait_ge(*shifted[b].of(n, 5))
                            for t in range(T):
                                last = dve.bn_stats(stats[:, b, t], h[:, b, t])
                            last.then_inc(stats_ready.sem, 1)
                            dve.wait_ge(*stats_ready.of(n, b + 1))
                            dve.tensor_copy(carrier[:, :], stats[:, b, :, 0])
                            for t in range(T):
                                last = dve.bn_aggr(mv[:, b, t], stats[:, b, t])
                            last.then_inc(var_ready.sem, 1)
                            dve.wait_ge(*rstd_ready.of(n, b + 1))
                            for t in range(T):
                                last = dve.tensor_scalar(h[:, b, t], h[:, b, t], mv[:, b, t, 0:1], rstd[:, b, t:t + 1],
                                                         ALU.subtract, ALU.mult)
                            last.then_inc(h_ready.sem, 1)
                        if stage == "hturn":
                            dve.wait_ge(*full(n, "hT", b))
                            for d in range(KD):
                                last = dve.tensor_scalar(z[:, d * N:(d + 1) * N], bank("hT", b)[:, d * N:(d + 1) * N],
                                                         ln[:, 0, d:d + 1], ln[:, 1, d:d + 1], ALU.mult, ALU.add)
                            last.then_inc(z_ready.sem, 1)
                            dve.wait_ge(*z_hi.of(n, b + 1))
                            dve.tensor_tensor(halves(flat[1], b), z.rearrange("p (d t) -> p d t", d=KD),
                                              halves(flat[0], b).bitcast(F32), ALU.subtract).then_inc(z_lo.sem, 1)
                        if stage in HALVES:
                            for j in HALVES[stage]:
                                m, r = J * b + j + 1, (P if j < J - 1 else HID_LAST)
                                dve.wait_ge(*gate_ready.of(n, m))
                                dve.wait_ge(*(u_lo.of(n, m - 2) if m > 2 else u_lo.before(n, 2 * J + m - 2)))
                                dve.scalar_tensor_tensor(uf[0:r, j % 2], bank("w1", b, j)[0:r, 0:N], b1[0:r, 0, j:j + 1],
                                                         gate[0:r, j % 2], ALU.add, ALU.mult).then_inc(uf_ready.sem, 1)
                        if stage == "w2":
                            dve.wait_ge(*full(n, "w2", b))
                            dve.wait_ge(*y1b_ready.of(n, b + 1))
                            dve.tensor_tensor(h[:, b], bank("w2", b)[:, :].rearrange("p (t d) -> p t d", t=T), h[:, b],
                                              ALU.add).then_inc(y2_ready.sem, 1)
                            dve.wait_ge(*y2_ready.of(n, b + 1))
                            dve.wait_ge(*x1_in[b].of(n, 1))
                            dve.tensor_tensor(x1[:, b], h[:, b], x1[:, b], ALU.add).then_inc(out_ready.sem, 1)


INPUTS = (("x", "x"), ("ctx", "ctx_1024"), ("wq", "L0_xattn_wq"), ("bq", "L0_xattn_bq"), ("wk", "L0_xattn_wk"),
          ("bk", "L0_xattn_bk"), ("wv", "L0_xattn_wv"), ("bv", "L0_xattn_bv"), ("wqkv", "L0_ffn_wqkv"),
          ("q_scale", "L0_ffn_q_scale"), ("k_scale", "L0_ffn_k_scale"), ("wo", "L0_ffn_wo"),
          ("ln_g", "L0_ffn_ln_g"), ("ln_b", "L0_ffn_ln_b"), ("w1", "L0_ffn_w1"), ("b1", "L0_ffn_b1"),
          ("w2", "L0_ffn_w2"), ("b2", "L0_ffn_b2"))


def build(nc, io, out):
    dram = {
        "parts": nc.dram_tensor("parts", (2, 2, 3, D, N), BF16).ap(),
        "x1": nc.dram_tensor("x1", (B, N, D), F32).ap(),
        "y": nc.dram_tensor("y", (B, N, D), F32).ap(),
    }
    cross_attention(nc, io, dram)
    layers(nc, io, dram, out)


def kernel(**inputs):
    import concourse.bacc as bacc
    from concourse.bass_utils import run_bass_kernel_spmd

    nc = bacc.Bacc("TRN2", target_bir_lowering=False, num_devices=1)
    arrays = {short: np.ascontiguousarray(inputs[name]) for short, name in INPUTS} | constants()
    io = {k: nc.dram_tensor("in_" + k, a.shape, mybir.dt.from_np(a.dtype), kind="ExternalInput").ap()
          for k, a in arrays.items()}
    out = nc.dram_tensor("out_dram", (B, N, D), F32, kind="ExternalOutput").ap()
    build(nc, io, out)
    r = run_bass_kernel_spmd(nc, [{"in_" + k: a for k, a in arrays.items()}], core_ids=[0])
    return r.results[0]["out_dram"]
```

```python
from contextlib import ExitStack

import concourse.bass as bass
import concourse.mybir as mybir
import numpy as np

ALU = mybir.AluOpType
ACT = mybir.ActivationFunctionType
F32 = mybir.dt.float32
F32R = mybir.dt.float32r
BF16 = mybir.dt.bfloat16
I32 = mybir.dt.int32
AX_X = mybir.AxisListType.X

P = 128
B, N, D = 8, 256, 256
T = N // P
KD = D // P
PAIRS = B // 2
XH, XD = 16, D // 16
LAYERS = 2
H, HD = 8, 64
INNER = H * HD
HP = INNER // P
WINDOW = 128
HID = int(D * 4 * 2 / 3)
J = -(-HID // P)
HID_LAST = HID - (J - 1) * P
ROUNDS = LAYERS * PAIRS
VW = 32
PART_PAIRS = ((0, 0), (0, 1), (0, 2), (1, 0), (1, 1), (1, 2), (2, 0), (2, 1))
MASKED = -1e30
GAP = 2
PAIRS_OF_TILES = 3
SLOTS = 3
EPS = 1e-5
NORM_FLOOR = 1e-12


def constants():
    half = np.arange(0, HD, 2, dtype=np.float32)
    inv = (1.0 / np.float32(10000.0) ** (half / np.float32(HD))).astype(np.float32)
    t = np.arange(N, dtype=np.float32)
    f = (t[:, None] * inv[None, :]).astype(np.float32)
    f = np.concatenate([f, f], 1).astype(np.float64)
    base = (half + np.float32(0.4 * HD)) / np.float32(1.4 * HD)
    power = (t - N // 2) / np.float32(WINDOW // 2)
    s = (base[None, :].astype(np.float32) ** power[:, None].astype(np.float32)).astype(np.float64)
    s = np.concatenate([s, s], 1)
    sign = np.where(np.arange(HD) < HD // 2, -1.0, 1.0)[None, :]
    rot = np.stack([np.stack([np.cos(f) * s * 8, np.sin(f) * sign * s * 8]),
                    np.stack([np.cos(f) / s, np.sin(f) * sign / s])]).astype(np.float32)
    i, j = np.arange(N)[:, None], np.arange(N)[None, :]
    off = (i < j) | (i > j + WINDOW) | ((i < WINDOW) & (j >= WINDOW))
    mask = np.where(off, MASKED, 0.0).astype(np.float32)
    mask = np.concatenate([mask[0:P, 0:P], mask[P:N, :]], 1)
    sel = np.zeros((P, XH, P), np.float32)
    for h in range(XH):
        sel[h, h] = sel[32 + h, h] = 1.0
    return {"c_rot": rot, "c_mask": mask, "c_sel": sel, "c_ident": np.eye(P, dtype=np.float32)}
class Signal:

    def __init__(self, sem, per_round, by=1):
        self.sem, self.per_round, self.by = sem, per_round, by

    def of(self, n, k):
        return self.sem, (n * self.per_round + (self.per_round + k)) * self.by

    def before(self, n, k):
        return self.sem, (n * self.per_round + k) * self.by


def place(order):
    turn, inside = {}, {}
    for ring, unit in order:
        k = ring[turn.get(ring, 0) % len(ring)]
        turn[ring] = turn.get(ring, 0) + 1
        inside.setdefault(k, []).append(unit)
    at = {}
    for k, units in inside.items():
        for i, unit in enumerate(units):
            at[unit] = (k, i + 1, units[i - 1], i > 0)
    return at, {k: len(u) for k, u in inside.items()}


def cross_attention(nc, io, dram):
    SCHEDULE = [("ln", 0), ("ln", 1), ("turn", 0), ("turn", 1), ("proj", 0), ("proj", 1), ("max", 0),
                ("max", 1), ("attend", 0), ("out", 0), ("attend", 1), ("out", 1)]
    ring, own = (0, 1, 2, 3, 4, 5), (6, 7)
    order = []
    for stage, b in SCHEDULE:
        if stage == "turn":
            order += [(ring, ("cT", b)), (ring, ("xT", b))]
        if stage == "proj":
            order += [(ring, (c, b)) for c in "kqv"]
        if stage == "max":
            order += [(ring, ("s", b, h)) for h in range(XH)] + [(ring, ("mT", b))]
        if stage == "attend":
            order += [(ring, ("e", b, h)) for h in range(XH)] + [(own, ("pv", b, g)) for g in range(2)]
        if stage == "out":
            order += [(ring, ("o", b, t)) for t in range(T)]
    units, per_bank = place(order)
    signals = []
    ctx = ExitStack()
    with ctx:
        def sb(name, shape, dt):
            return ctx.enter_context(nc.sbuf_tensor("x_" + name, shape, dt))

        def signal(name, per_round, by=1):
            signals.append(Signal(ctx.enter_context(nc.semaphore("x_" + name)), per_round, by))
            return signals[-1]

        def sem(name):
            return ctx.enter_context(nc.semaphore("x_" + name))

        psum = [ctx.enter_context(nc.psum_tensor(f"x_ps{i}", [P, 512], F32)) for i in range(8)]
        ident = sb("ident", [P, P], F32)
        sel_f = sb("sel_f", [P, XH, P], F32)
        sel = sb("sel", [P, XH, P], BF16)
        wraw = sb("wraw", [P, 3, KD, D], F32)
        whi = sb("whi", [P, 3, KD, D], F32R)
        wlo = sb("wlo", [P, 3, KD, D], F32R)
        bqk = sb("bqk", [P, 2, KD], F32)
        bv = sb("bv", [P, D], F32)
        mhalf = sb("mhalf", [P, T], F32)
        xin = sb("xin", [P, 2, T, D], F32)
        cin = sb("cin", [P, 2, T, D], F32)
        stats = sb("stats", [P, 2, 2, T, 6], F32)
        mv = sb("mv", [P, 2, 2, T, 2], F32)
        veps = sb("veps", [P, 2, 2, T], F32)
        eps = sb("eps", [P, T], F32)
        carrier = sb("carrier", [P, T], F32)
        rstd = sb("rstd", [P, 2, 2, T], F32)
        xn = sb("xn", [P, 2, T, D], F32)
        hi = sb("hi", [P, 2, 2, KD, N], F32R)
        lo = sb("lo", [P, 2, 2, KD, N], F32R)
        qk = sb("qk", [P, 2, 2, KD, N], F32)
        rest = sb("rest", [P, 2, 2, KD, N], F32)
        parts = sb("parts", [P, 2, 2, 3, KD, N], BF16)
        stack = sb("stack", [P, 2, 2, XH, N], BF16)
        va = sb("va", [P, 2, T, XH, VW], F32)
        nm = sb("nm", [P, 2, T, XH], F32)
        mrow = sb("mrow", [P, 2, N], BF16)
        probs = sb("probs", [P, SLOTS, T * N], F32)
        oT = sb("oT", [P, 2, 4, N], F32)
        rden = sb("rden", [P, 2, T, XH], F32)
        x1 = sb("x1", [P, 2, T, D], F32)
        y = sb("y", [P, 2, T, D], F32)

        consts_in, sel_cast = sem("consts_in"), sem("sel_cast")
        whi_ready, wlo_ready, set_up = sem("whi_ready"), sem("wlo_ready"), sem("set_up")
        filled = {k: signal(f"filled{k}", m) for k, m in per_bank.items()}
        x_in = [signal(f"x_in{b}", 1, 16) for b in range(2)]
        c_in = [signal(f"c_in{b}", 1, 16) for b in range(2)]
        stats_ready, var_ready = signal("stats_ready", 4), signal("var_ready", 4)
        eps_added, rstd_ready = signal("eps_added", 4), signal("rstd_ready", 4)
        xn_ready = signal("xn_ready", 2)
        hi_ready, lo_ready = signal("hi_ready", 4), signal("lo_ready", 4)
        qk_ready, p1_ready, rest_ready = signal("qk_ready", 4), signal("p1_ready", 4), signal("rest_ready", 4)
        p2_ready, p3_ready = signal("p2_ready", 4), signal("p3_ready", 4)
        v_ready = signal("v_ready", 2)
        parts_out = [signal(f"parts_out{b}", 2, 16) for b in range(2)]
        stacks_in = [signal(f"stacks_in{b}", 2 * len(PART_PAIRS), 16) for b in range(2)]
        max_ready = signal("max_ready", 2 * XH)
        m1_ready, m2_ready = signal("m1_ready", 2), signal("m2_ready", 2)
        probs_ready, probs_used = signal("probs_ready", 2 * XH), signal("probs_used", 2 * XH)
        oT_ready = signal("oT_ready", 4)
        rden_ready, att_ready, x1_ready = signal("rden_ready", 4), signal("att_ready", 4), signal("x1_ready", 4)
        y_ready = signal("y_ready", 2)
        x1_out = [signal(f"x1_out{b}", 1, 16) for b in range(2)]
        y_out = [signal(f"y_out{b}", 1, 16) for b in range(2)]

        reader = {
            "cT": lambda b: (lo_ready, 2 * b + 1), "xT": lambda b: (lo_ready, 2 * b + 2),
            "k": lambda b: (qk_ready, 2 * b + 1), "q": lambda b: (qk_ready, 2 * b + 2),
            "v": lambda b: (v_ready, b + 1),
            "s": lambda b, h: (max_ready, XH * b + h + 1), "mT": lambda b: (m2_ready, b + 1),
            "e": lambda b, h: (probs_ready, XH * b + h + 1), "pv": lambda b, g: (oT_ready, 2 * b + g + 1),
            "o": lambda b, t: (att_ready, T * b + t + 1),
        }

        def bank(unit):
            return psum[units[unit][0]]

        def full(n, unit):
            return filled[units[unit][0]].of(n, units[unit][1])

        def fills(unit):
            return filled[units[unit][0]].sem

        def emptied(n, unit):
            _, _, last, same_round = units[unit]
            by, k = reader[last[0]](*last[1:])
            return by.of(n, k) if same_round else by.before(n, k)

        for s in signals:
            nc.sync.sem_inc(s.sem, s.per_round * s.by)

        block = ctx.enter_context(nc.Block())

        @block.sync
        def _(sp):
            sp.dma_start(ident[:, :], io["c_ident"]).then_inc(consts_in, 16)
            sp.dma_start(sel_f[:, :, :], io["c_sel"]).then_inc(consts_in, 16)
            for c, w in enumerate(("wk", "wq", "wv")):
                sp.dma_start(wraw[:, c], io[w].rearrange("(k p) n -> p k n", p=P)).then_inc(consts_in, 16)
            for c, w in enumerate(("bk", "bq")):
                sp.dma_start(bqk[:, c], io[w].rearrange("(k p) -> p k", p=P),
                             allow_slow_non_contiguous=True).then_inc(consts_in, 16)
            sp.dma_start(bv[:, :], io["bv"].partition_broadcast(P)).then_inc(consts_in, 16)

            with sp.Fori(0, PAIRS) as n:
                for b in range(2):
                    sp.wait_ge(*x1_ready.before(n, T * (b + 1)))
                    sp.dma_start(xin[:, b], io["x"][n * 2 + b].rearrange("(t p) d -> p t d", p=P)).then_inc(x_in[b].sem, 16)
                    sp.dma_start(cin[:, b], io["ctx"][n * 2 + b].rearrange("(t p) d -> p t d", p=P)).then_inc(c_in[b].sem, 16)
                for b in range(2):
                    sp.wait_ge(*p3_ready.of(n, 2 * b + 2))
                    for c in range(2):
                        sp.dma_start(dram["parts"][b, c].rearrange("s (k p) t -> p s k t", p=P),
                                     parts[:, b, c]).then_inc(parts_out[b].sem, 16)
                    sp.wait_ge(*parts_out[b].of(n, 2))
                    for c in range(2):
                        for g, pair in enumerate(PART_PAIRS):
                            sp.dma_start(stack[XD * g:XD * (g + 1), b, c],
                                         dram["parts"][b, c, pair[c]].rearrange("(h r) t -> r h t", r=XD)
                                         ).then_inc(stacks_in[b].sem, 16)
                for b in range(2):
                    sp.wait_ge(*x1_ready.of(n, T * (b + 1)))
                    sp.dma_start(dram["x1"][n * 2 + b].rearrange("(t p) d -> p t d", p=P), x1[:, b]).then_inc(x1_out[b].sem, 16)
                    sp.wait_ge(*y_ready.of(n, b + 1))
                    sp.dma_start(dram["y"][n * 2 + b].rearrange("(t p) d -> p t d", p=P), y[:, b]).then_inc(y_out[b].sem, 16)
            for b in range(2):
                sp.wait_ge(*x1_out[b].of(PAIRS - 1, 1))
                sp.wait_ge(*y_out[b].of(PAIRS - 1, 1))

        @block.tensor
        def _(pe):
            pe.wait_ge(consts_in, 16 * 8)
            pe.wait_ge(sel_cast, 1)
            pe.wait_ge(whi_ready, 1)
            pe.wait_ge(wlo_ready, 1)
            pe.wait_ge(set_up, 5)

            with pe.Fori(0, PAIRS) as n:
                for stage, b in SCHEDULE:
                    if stage == "turn":
                        for s, (kind, src) in enumerate((("cT", cin), ("xT", xn))):
                            if kind == "cT":
                                pe.wait_ge(*c_in[b].of(n, 1))
                            else:
                                pe.wait_ge(*xn_ready.of(n, b + 1))
                            pe.wait_ge(*emptied(n, (kind, b)))
                            for d in range(KD):
                                for t in range(T):
                                    mm = pe.transpose(bank((kind, b))[:, d * N + t * P:d * N + (t + 1) * P],
                                                      src[:, b, t, d * P:(d + 1) * P], ident[:, :])
                            mm.then_inc(fills((kind, b)), 1)
                    if stage == "proj":
                        pe.wait_ge(*lo_ready.of(n, 2 * b + 2))
                        for w, c in enumerate("kqv"):
                            s = 1 if c == "q" else 0
                            pe.wait_ge(*emptied(n, (c, b)))
                            for m in range(2):
                                for i, (a, z) in enumerate(((hi, whi), (hi, wlo), (lo, whi))):
                                    for d in range(KD):
                                        at, wt = a[:, b, s, d], z[:, w, d]
                                        if c == "v":
                                            fixed, moving = at[:, m * P:(m + 1) * P], wt
                                        else:
                                            fixed, moving = wt[:, m * P:(m + 1) * P], at
                                        mm = pe.matmul(bank((c, b))[:, m * N:(m + 1) * N], fixed, moving,
                                                       start=(i == 0 and d == 0), stop=(i == 2 and d == KD - 1))
                            mm.then_inc(fills((c, b)), 1)
                    if stage == "max":
                        pe.wait_ge(*stacks_in[b].of(n, 2 * len(PART_PAIRS)))
                        for h in range(XH):
                            pe.wait_ge(*emptied(n, ("s", b, h)))
                            for t in range(T):
                                mm = pe.matmul(bank(("s", b, h))[:, t * N:(t + 1) * N], stack[:, b, 1, h, t * P:(t + 1) * P],
                                               stack[:, b, 0, h, :], start=True, stop=True)
                            mm.then_inc(fills(("s", b, h)), 1)
                        pe.wait_ge(*max_ready.of(n, XH * (b + 1)))
                        pe.wait_ge(*emptied(n, ("mT", b)))
                        for t in range(T):
                            mm = pe.transpose(bank(("mT", b))[0:XH, t * P:(t + 1) * P], nm[:, b, t, :], ident[:, :])
                        mm.then_inc(fills(("mT", b)), 1)
                    if stage == "attend":
                        def scores(h):
                            pe.wait_ge(*emptied(n, ("e", b, h)))
                            for k in range(T):
                                to = bank(("e", b, h))[:, k * N:(k + 1) * N]
                                pe.matmul(to, stack[:, b, 0, h, k * P:(k + 1) * P], stack[:, b, 1, h, :],
                                          start=True, stop=False)
                                mm = pe.matmul(to, sel[:, h, :], mrow[:, b, :], start=False, stop=True)
                            mm.then_inc(fills(("e", b, h)), 1)

                        def values(h):
                            g, c, q = h // 8, h // 4 % 2, VW * (h % 4)
                            if h % 8 == 0:
                                pe.wait_ge(*emptied(n, ("pv", b, g)))
                            pe.wait_ge(*probs_ready.of(n, XH * b + h + 1))
                            for k in range(T):
                                mm = pe.matmul(bank(("pv", b, g))[q:q + VW, c * N:(c + 1) * N], va[:, b, k, h, :],
                                               probs[:, (XH * b + h) % SLOTS, k * N:(k + 1) * N],
                                               start=(k == 0), stop=(k == T - 1))
                            mm.then_inc(probs_used.sem, 1)

                        pe.wait_ge(*m2_ready.of(n, b + 1))
                        pe.wait_ge(*v_ready.of(n, b + 1))
                        scores(0)
                        scores(1)
                        for h in range(XH):
                            if h + 2 < XH:
                                scores(h + 2)
                            values(h)
                    if stage == "out":
                        pe.wait_ge(*oT_ready.of(n, 2 * b + 2))
                        for t in range(T):
                            pe.wait_ge(*emptied(n, ("o", b, t)))
                            for g in range(4):
                                mm = pe.transpose(bank(("o", b, t))[:, g * P:(g + 1) * P],
                                                  oT[:, b, g, t * P:(t + 1) * P], ident[:, :])
                            mm.then_inc(fills(("o", b, t)), 1)

        @block.scalar
        def _(act):
            act.wait_ge(consts_in, 16 * 8)
            act.activation(sel[:, :, :], sel_f[:, :, :], ACT.Copy).then_inc(sel_cast, 1)
            act.activation(whi[:, :, :, :], wraw[:, :, :, :], ACT.Copy).then_inc(whi_ready, 1)
            act.wait_ge(set_up, 5)

            with act.Fori(0, PAIRS) as n:
                for stage, b in SCHEDULE:
                    if stage == "turn":
                        for s, kind in enumerate(("cT", "xT")):
                            act.wait_ge(*full(n, (kind, b)))
                            act.activation(hi[:, b, s], bank((kind, b))[:, :].rearrange("p (k t) -> p k t", k=KD),
                                           ACT.Copy).then_inc(hi_ready.sem, 1)
                    if stage == "proj":
                        for c in range(2):
                            act.wait_ge(*qk_ready.of(n, 2 * b + c + 1))
                            act.activation(parts[:, b, c, 0], qk[:, b, c], ACT.Copy).then_inc(p1_ready.sem, 1)
                        for c in range(2):
                            act.wait_ge(*rest_ready.of(n, 2 * b + c + 1))
                            act.activation(parts[:, b, c, 1], rest[:, b, c], ACT.Copy).then_inc(p2_ready.sem, 1)
                    if stage == "max":
                        act.wait_ge(*full(n, ("mT", b)))
                        act.activation(mrow[0:XH, b, :], bank(("mT", b))[0:XH, 0:N], ACT.Copy).then_inc(m1_ready.sem, 1)
                    if stage == "attend":
                        def output(g):
                            act.wait_ge(*probs_used.of(n, XH * b + 8 * (g + 1)))
                            act.activation(oT[:, b, 2 * g:2 * g + 2],
                                           bank(("pv", b, g))[:, :].rearrange("p (g t) -> p g t", g=2),
                                           ACT.Copy).then_inc(oT_ready.sem, 1)

                        for h in range(XH):
                            i = XH * b + h
                            act.wait_ge(*full(n, ("e", b, h)))
                            act.wait_ge(*(probs_used.of(n, i + 1 - SLOTS) if i >= SLOTS
                                          else probs_used.before(n, 2 * XH + i + 1 - SLOTS)))
                            act.activation(probs[:, i % SLOTS, :], bank(("e", b, h))[:, :],
                                           ACT.Exp).then_inc(probs_ready.sem, 1)
                            if h == 8 + SLOTS:
                                output(0)
                        output(1)

        @block.gpsimd
        def _(pool):
            pool.memset(mhalf[:, :], -0.5).then_inc(set_up, 1)
            pool.memset(eps[:, :], EPS).then_inc(set_up, 1)
            pool.memset(mrow[:, :, :], 0.0).then_inc(set_up, 1)
            pool.memset(va[:, :, :, :, XD:VW], 0.0).then_inc(set_up, 1)
            pool.wait_ge(set_up, 4)
            pool.memset(va[:, :, :, :, XD:XD + 1], 1.0).then_inc(set_up, 1)

            with pool.Fori(0, PAIRS) as n:
                for stage, b in SCHEDULE:
                    if stage in ("ln", "out"):
                        s = 0 if stage == "ln" else 1
                        k = b + 1 if s == 0 else b + 3
                        pool.wait_ge(*var_ready.of(n, k))
                        pool.tensor_tensor(veps[:, b, s], mv[:, b, s, :, 1], eps[:, :], ALU.add).then_inc(eps_added.sem, 1)
                        pool.wait_ge(*eps_added.of(n, k))
                        pool.tensor_tensor(rstd[:, b, s], veps[:, b, s], mhalf[:, :], ALU.pow).then_inc(rstd_ready.sem, 1)
                    if stage == "proj":
                        for c in range(2):
                            pool.wait_ge(*p2_ready.of(n, 2 * b + c + 1))
                            pool.tensor_tensor(parts[:, b, c, 2], rest[:, b, c], parts[:, b, c, 1],
                                               ALU.subtract).then_inc(p3_ready.sem, 1)

        @block.vector
        def _(dve):
            dve.wait_ge(whi_ready, 1)
            dve.tensor_tensor(wlo[:, :, :, :], wraw[:, :, :, :], whi[:, :, :, :].bitcast(F32),
                              ALU.subtract).then_inc(wlo_ready, 1)
            dve.wait_ge(set_up, 5)

            def layernorm(n, b, s, src, dst, ready):
                k = b + 1 if s == 0 else b + 3
                for t in range(T):
                    last = dve.bn_stats(stats[:, b, s, t], src[:, b, t])
                last.then_inc(stats_ready.sem, 1)
                dve.wait_ge(*stats_ready.of(n, k))
                dve.tensor_copy(carrier[:, :], stats[:, b, s, :, 0])
                for t in range(T):
                    last = dve.bn_aggr(mv[:, b, s, t], stats[:, b, s, t])
                last.then_inc(var_ready.sem, 1)
                dve.wait_ge(*rstd_ready.of(n, k))
                for t in range(T):
                    last = dve.tensor_scalar(dst[:, b, t], src[:, b, t], mv[:, b, s, t, 0:1], rstd[:, b, s, t:t + 1],
                                             ALU.subtract, ALU.mult)
                last.then_inc(ready.sem, 1)

            with dve.Fori(0, PAIRS) as n:
                for stage, b in SCHEDULE:
                    if stage == "ln":
                        dve.wait_ge(*x_in[b].of(n, 1))
                        layernorm(n, b, 0, xin, xn, xn_ready)
                    if stage == "turn":
                        for s, kind in enumerate(("cT", "xT")):
                            dve.wait_ge(*hi_ready.of(n, 2 * b + s + 1))
                            dve.tensor_tensor(lo[:, b, s], bank((kind, b))[:, :].rearrange("p (k t) -> p k t", k=KD),
                                              hi[:, b, s].bitcast(F32), ALU.subtract).then_inc(lo_ready.sem, 1)
                    if stage == "proj":
                        for c, kind in enumerate("kq"):
                            dve.wait_ge(*full(n, (kind, b)))
                            for m in range(KD):
                                last = dve.tensor_scalar(qk[:, b, c, m], bank((kind, b))[:, m * N:(m + 1) * N],
                                                         bqk[:, c, m:m + 1], XD ** -0.5 if kind == "q" else 1.0,
                                                         ALU.add, ALU.mult)
                            last.then_inc(qk_ready.sem, 1)
                        for c in range(2):
                            dve.wait_ge(*p1_ready.of(n, 2 * b + c + 1))
                            dve.tensor_tensor(rest[:, b, c], qk[:, b, c], parts[:, b, c, 0],
                                              ALU.subtract).then_inc(rest_ready.sem, 1)
                        dve.wait_ge(*full(n, ("v", b)))
                        for t in range(T):
                            last = dve.tensor_tensor(va[:, b, t, :, 0:XD],
                                                     bank(("v", b))[:, t * N:(t + 1) * N].rearrange("p (h r) -> p h r", r=XD),
                                                     bv[:, :].rearrange("p (h r) -> p h r", r=XD), ALU.add)
                        last.then_inc(v_ready.sem, 1)
                    if stage == "max":
                        for h in range(XH):
                            dve.wait_ge(*full(n, ("s", b, h)))
                            dve.tensor_reduce(nm[:, b, :, h], bank(("s", b, h))[:, :].rearrange("p (t k) -> p t k", t=T),
                                              AX_X, ALU.max, negate=True).then_inc(max_ready.sem, 1)
                        dve.wait_ge(*m1_ready.of(n, b + 1))
                        dve.tensor_tensor(mrow[32:32 + XH, b, :], bank(("mT", b))[0:XH, 0:N], mrow[0:XH, b, :],
                                          ALU.subtract).then_inc(m2_ready.sem, 1)
                    if stage == "out":
                        for t in range(T):
                            k = T * b + t + 1
                            o = bank(("o", b, t))[:, :].rearrange("p (h r) -> p h r", r=VW)
                            dve.wait_ge(*full(n, ("o", b, t)))
                            dve.reciprocal(rden[:, b, t], o[:, :, XD]).then_inc(rden_ready.sem, 1)
                            dve.wait_ge(*rden_ready.of(n, k))
                            if t == 0:
                                dve.wait_ge(*x1_out[b].before(n, 1))
                            dve.tensor_tensor(x1[:, b, t].rearrange("p (h r) -> p h r", r=XD), o[:, :, 0:XD],
                                              rden[:, b, t].unsqueeze(2).to_broadcast([P, XH, XD]),
                                              ALU.mult).then_inc(att_ready.sem, 1)
                            dve.wait_ge(*att_ready.of(n, k))
                            dve.tensor_tensor(x1[:, b, t], x1[:, b, t], xin[:, b, t], ALU.add).then_inc(x1_ready.sem, 1)
                        dve.wait_ge(*x1_ready.of(n, T * (b + 1)))
                        dve.wait_ge(*y_out[b].before(n, 1))
                        layernorm(n, b, 1, x1, y, y_ready)


def layers(nc, io, dram, out):
    SCHEDULE = [("qkv", 0), ("qkv", 1), ("qkT", 0), ("lead", 0), ("heads_a", 0), ("heads_b", 0), ("heads_c", 0), ("qkT", 1),
                ("wo", 0), ("lead", 1), ("heads_a", 1), ("stats", 0), ("heads_b", 1), ("norm", 0),
                ("heads_c", 1), ("hturn", 0), ("wo", 1), ("w1a", 0), ("w1b", 0), ("stats", 1), ("w1c", 0),
                ("w2a", 0), ("norm", 1), ("hturn", 1), ("w2b", 0), ("w1a", 1), ("w1b", 1), ("w1c", 1),
                ("turn", 0), ("turn", 1), ("w2a", 1), ("w2b", 1)]
    HEADS = {"heads_a": range(0, 2), "heads_b": range(2, 5), "heads_c": range(5, H)}
    HIDDEN = {"w1a": range(0, 2), "w1b": range(2, 4), "w1c": range(4, J)}
    LEAD = 3
    ring, turn_ring, own = (0, 1, 2, 3, 4), (5,), (6, 7)
    order = []
    for stage, b in SCHEDULE:
        if stage == "turn":
            order += [(turn_ring, ("yT", b))]
        if stage == "qkv":
            order += [(ring, ("qkv", b, t, c)) for t in range(T) for c in range(3)]
        if stage == "qkT":
            order += [(ring, ("qkT", b, g, c)) for g in range(2) for c in range(2)]
        if stage == "lead":
            order += [(ring, ("s", b, head)) for head in range(LEAD)]
        if stage in HEADS:
            for head in HEADS[stage]:
                if head + LEAD < H:
                    order += [(ring, ("s", b, head + LEAD))]
                order += [(ring, ("pT", b, head))]
                if head % 4 == 0:
                    order += [(own, ("pv", b, head // 4))]
        if stage == "wo":
            order += [(ring, ("wo", b))]
        if stage == "hturn":
            order += [(ring, ("hT", b))]
        if stage in HIDDEN:
            order += [(ring, ("w1", b, j)) for j in HIDDEN[stage]]
        if stage == "w2a":
            order += [(ring, ("w2", b))]
    units, per_bank = place(order)
    signals = []
    ctx = ExitStack()
    with ctx:
        def sb(name, shape, dt):
            return ctx.enter_context(nc.sbuf_tensor("l_" + name, shape, dt))

        def signal(name, per_round, by=1):
            signals.append(Signal(ctx.enter_context(nc.semaphore("l_" + name)), per_round, by))
            return signals[-1]

        def sem(name):
            return ctx.enter_context(nc.semaphore("l_" + name))

        psum = [ctx.enter_context(nc.psum_tensor(f"l_ps{i}", [P, 512], F32)) for i in range(8)]
        ident = sb("ident", [P, P], F32)
        ident_b = sb("ident_b", [P, P], BF16)
        mask = sb("mask", [P, PAIRS_OF_TILES * P], BF16)
        turns = sb("turns", [P, 2, 2, T, HD], F32)
        mhalf = sb("mhalf", [P, H], F32)
        zero_row = sb("zero_row", [1, P], F32)
        scale = sb("scale", [P, 2, 2, HD], F32)
        table = sb("table", [P, 2, 2, T, HD], F32)
        wqkv = [sb("wqkv" + s, [P, KD, 3 * INNER], F32R) for s in ("hi", "lo")]
        wo = [sb("wo" + s, [P, HP, D], F32R) for s in ("hi", "lo")]
        w1 = [sb("w1" + s, [P, KD, 2 * HID + P - HID_LAST], F32R) for s in ("hi", "lo")]
        w2 = [sb("w2" + s, [P, J, D], F32R) for s in ("hi", "lo")]
        b1 = sb("b1", [P, 2, J], F32)
        b2 = sb("b2", [P, D], F32)
        ln = sb("ln", [P, 2, KD], F32)
        yn = sb("yn", [P, 2, T, D], F32)
        y1 = sb("y1", [P, 2, T, D], F32)
        h = sb("h", [P, 2, T, D], F32)
        x1 = sb("x1", [P, 2, T, D], F32)
        flat = [sb("yT" + s, [P, 2, 2 * (N + GAP)], F32R) for s in ("hi", "lo")]
        rot = sb("rot", [P, 10, INNER], F32)
        sq = sb("sq", [P, 2, INNER], F32)
        ssq = sb("ssq", [P, 2, T, 2, H], F32)
        rnorm = sb("rnorm", [P, 2, T, 2, H], F32)
        q = [sb("q" + s, [P, 2, HP, 2, N], F32R) for s in ("hi", "lo")]
        kk = sb("kk", [P, 2, 2, HP, N], F32R)
        k = [kk[:, 0], kk[:, 1]]
        v = sb("v", [P, 2, T, INNER], F32)
        nm = sb("nm", [P, 2, H, T], F32)
        total = sb("total", [P, 2, H, T], F32)
        share = sb("share", [P, 2, H, T], F32)
        both = sb("both", [P, 2, SLOTS, PAIRS_OF_TILES * P], F32)
        probs = both[:, 0]
        probsT = both[:, 1]
        stats = sb("stats", [P, 2, T, 6], F32)
        mv = sb("mv", [P, 2, T, 2], F32)
        veps = sb("veps", [P, 2, T], F32)
        eps = sb("eps", [P, T], F32)
        carrier = sb("carrier", [P, T], F32)
        rstd = sb("rstd", [P, 2, T], F32)
        u = [sb("u" + s, [P, J, N], F32R) for s in ("hi", "lo")]
        uf = sb("uf", [P, 2, N], F32)
        raw_qkv = rot[:, 0:3 * KD].rearrange("p a c -> p (a c)").rearrange("p (k n) -> p k n", k=KD)
        raw_wo = rot[:, 3 * KD:3 * KD + HP * D // INNER].rearrange("p a c -> p (a c)").rearrange("p (k n) -> p k n", k=HP)
        flat_v = v[:, :, :, :].rearrange("p b t n -> p (b t n)")
        raw_w1 = [both[:, :, :, :].rearrange("p a s c -> p (a s c)")[:, 0:2 * HID], flat_v[:, 0:2 * HID]]
        raw_w2 = rot[:, 3 * KD + HP * D // INNER:].rearrange("p a c -> p (a c)").rearrange("p (k n) -> p k n", n=D)
        j_rot = raw_w2.shape[1]
        raw_rest = flat_v[:, 2 * HID:2 * HID + (J - j_rot) * D].rearrange("p (k n) -> p k n", n=D)
        pieces = ([(w1, (slice(0, P), k, slice(0, 2 * HID)), raw_w1[k], (slice(0, P), slice(0, 2 * HID))) for k in range(KD)]
                  + [(w2, (slice(0, P), slice(0, j_rot)), raw_w2, (slice(0, P), slice(0, j_rot))),
                     (w2, (slice(0, P), slice(j_rot, J - 1)), raw_rest, (slice(0, P), slice(0, J - 1 - j_rot))),
                     (w2, (slice(0, HID_LAST), J - 1), raw_rest, (slice(0, HID_LAST), J - 1 - j_rot))])
        z = sq[:, 0]
        gate = sq[:, 1].rearrange("p (s t) -> p s t", s=2)

        consts_in, consts_cast, set_up = sem("consts_in"), sem("consts_cast"), sem("set_up")
        raw_a, raw_b = signal("raw_a", 2, 16), signal("raw_b", KD + 3, 16)
        small_in = signal("small_in", 13, 16)
        table_ready = signal("table_ready", 1)
        hi_a, lo_a, hi_b, lo_b = signal("hi_a", 1), signal("lo_a", 1), signal("hi_b", 1), signal("lo_b", 1)
        filled = {i: signal(f"filled{i}", m) for i, m in per_bank.items()}
        y_in = [signal(f"y_in{b}", 1, 16) for b in range(2)]
        x1_in = [signal(f"x1_in{b}", 1, 16) for b in range(2)]
        yT_hi, yT_lo = signal("yT_hi", 2), signal("yT_lo", 2)
        sq_ready, ssq_sum, ssq_ready = signal("sq_ready", 8), signal("ssq_sum", 8), signal("ssq_ready", 8)
        terms_ready, norm_ready, sum_ready = signal("terms_ready", 8), signal("norm_ready", 8), signal("sum_ready", 8)
        qk_ready, v_ready = signal("qk_ready", 8), signal("v_ready", 4)
        turned_hi, turned_lo = signal("turned_hi", 8), signal("turned_lo", 8)
        max_ready, exp_ready, probs_ready = signal("max_ready", 2 * H), signal("exp_ready", 2 * H), signal("probs_ready", 2 * H)
        share_ready = signal("share_ready", 2 * H)
        probsT_ready, probsT_used = signal("probsT_ready", 2 * H), signal("probsT_used", 2 * H)
        o_hi, o_lo = signal("o_hi", 4), signal("o_lo", 4)
        y1_ready = signal("y1_ready", 2)
        shifted = [signal(f"shifted{b}", 5, 16) for b in range(2)]
        stats_ready, var_ready = signal("stats_ready", 2), signal("var_ready", 2)
        eps_added, rstd_ready = signal("eps_added", 2), signal("rstd_ready", 2)
        h_ready, z_ready, z_hi, z_lo = signal("h_ready", 2), signal("z_ready", 2), signal("z_hi", 2), signal("z_lo", 2)
        y1b_ready = signal("y1b_ready", 2)
        gate_ready, uf_ready = signal("gate_ready", 2 * J), signal("uf_ready", 2 * J)
        u_hi, u_lo = signal("u_hi", 2 * J), signal("u_lo", 2 * J)
        y2_ready, out_ready = signal("y2_ready", 2), signal("out_ready", 2)
        y_out = [signal(f"y_out{b}", 1, 16) for b in range(2)]
        out_out = [signal(f"out_out{b}", 1, 16) for b in range(2)]

        reader = {
            "yT": lambda b: (yT_lo, b + 1),
            "qkv": lambda b, t, c: (terms_ready, 4 * b + 2 * t + c + 1) if c < 2 else (v_ready, T * b + t + 1),
            "qkT": lambda b, g, c: (turned_lo, 4 * b + 2 * g + c + 1),
            "s": lambda b, head: (exp_ready, H * b + head + 1), "pT": lambda b, head: (probsT_ready, H * b + head + 1),
            "pv": lambda b, g: (o_lo, 2 * b + g + 1), "wo": lambda b: (y1_ready, b + 1),
            "hT": lambda b: (z_ready, b + 1), "w1": lambda b, j: (uf_ready, J * b + j + 1),
            "w2": lambda b: (y2_ready, b + 1),
        }

        def bank(*unit):
            return psum[units[unit][0]]

        def full(n, *unit):
            return filled[units[unit][0]].of(n, units[unit][1])

        def fills(*unit):
            return filled[units[unit][0]].sem

        def emptied(n, *unit):
            _, _, last, same_round = units[unit]
            by, m = reader[last[0]](*last[1:])
            return by.of(n, m) if same_round else by.before(n, m)

        def halves(tile, b):
            return tile[:, b].rearrange("p (d c) -> p d c", d=2)[:, :, 0:N]

        def due(stage, head):
            group = HEADS[stage]
            heads = ([] if head == group[0] else [head + LEAD - 1]) + ([head + LEAD] if head == group[-1] else [])
            return [other for other in heads if other < H]

        products = ((0, 0), (0, 1), (1, 0))

        for s in signals:
            nc.sync.sem_inc(s.sem, s.per_round * s.by)

        block = ctx.enter_context(nc.Block())

        @block.sync
        def _(sp):
            sp.dma_start(ident[:, :], io["c_ident"]).then_inc(consts_in, 16)
            for c in range(2):
                for s in range(2):
                    sp.dma_start(turns[:, c, s], io["c_rot"][c, s].rearrange("(t p) d -> p t d", p=P)).then_inc(consts_in, 16)
            sp.dma_start(rot[:, 0, 0:PAIRS_OF_TILES * P], io["c_mask"]).then_inc(consts_in, 16)

            def load_y(n, b, at):
                sp.wait_ge(*y1_ready.before(n, b + 1))
                sp.dma_start(yn[:, b], dram["y"][at * 2 + b].rearrange("(t p) d -> p t d", p=P)).then_inc(y_in[b].sem, 16)

            load_y(0, 0, 0)
            load_y(0, 1, 0)
            with sp.Fori(0, LAYERS) as l:
                with sp.Fori(0, PAIRS) as i:
                    n = l * PAIRS + i
                    for stage, b in SCHEDULE:
                        if stage == "wo":
                            sp.wait_ge(*y1_ready.of(n, b + 1))
                            sp.wait_ge(*y_out[b].before(n, 1))
                            s = shifted[b].sem
                            sp.dma_start(h[:, b, :, 0:P], y1[:, b, :, 0:P]).then_inc(s, 16)
                            sp.dma_start(h[1:113, b, :, P:D], y1[0:112, b, :, P:D]).then_inc(s, 16)
                            sp.dma_start(h[113:P, b, :, P:D], y1[112:P - 1, b, :, P:D]).then_inc(s, 16)
                            sp.dma_start(h[0:1, b, 1, P:D], y1[P - 1:P, b, 0, P:D]).then_inc(s, 16)
                            sp.dma_start(h[0:1, b, 0, P:D], zero_row[:, :]).then_inc(s, 16)
                            load_y(n + 1, b, n + 1)
                            sp.wait_ge(*out_out[b].before(n, 1))
                            sp.dma_start(x1[:, b], dram["x1"][i * 2 + b].rearrange("(t p) d -> p t d", p=P)).then_inc(x1_in[b].sem, 16)
                        if stage == "w2b":
                            sp.wait_ge(*y2_ready.of(n, b + 1))
                            sp.dma_start(dram["y"][(n + PAIRS) * 2 + b].rearrange("(t p) d -> p t d", p=P), h[:, b]).then_inc(y_out[b].sem, 16)
                            sp.wait_ge(*out_ready.of(n, b + 1))
                            sp.dma_start(out[i * 2 + b].rearrange("(t p) d -> p t d", p=P), x1[:, b]).then_inc(out_out[b].sem, 16)
            for b in range(2):
                sp.wait_ge(*y_out[b].of(ROUNDS - 1, 1))
                sp.wait_ge(*out_out[b].of(ROUNDS - 1, 1))
                sp.wait_ge(*y_in[b].of(ROUNDS, 1))

        @block.tensor
        def _(pe):
            pe.wait_ge(consts_cast, 2)
            pe.wait_ge(consts_in, 16 * 6)
            pe.wait_ge(set_up, 13)

            def start_of(kind, b, d):
                return 0 if d == 0 else N + GAP - (1 if kind == "y" else 0)

            def turn(kind, n, b, src, ready):
                pe.wait_ge(*ready)
                pe.wait_ge(*emptied(n, kind, b))
                for d in range(KD):
                    for t in range(T):
                        mm = pe.transpose(bank(kind, b)[:, d * N + t * P:d * N + (t + 1) * P],
                                          src[:, b, t, d * P:(d + 1) * P], ident[:, :])
                mm.then_inc(fills(kind, b), 1)

            for b in range(2):
                turn("yT", 0, b, yn, y_in[b].of(0, 1))

            with pe.Fori(0, LAYERS) as l:
                with pe.Fori(0, PAIRS) as i:
                    n = l * PAIRS + i
                    for stage, b in SCHEDULE:
                        if stage == "turn":
                            turn("yT", n + 1, b, yn, y_in[b].of(n + 1, 1))
                        if stage == "hturn":
                            turn("hT", n, b, h, h_ready.of(n, b + 1))
                        if stage == "qkv":
                            if b == 0:
                                pe.wait_ge(*lo_a.of(l, 1))
                            pe.wait_ge(*yT_lo.of(n, b + 1))
                            for t in range(T):
                                for c in range(3):
                                    pe.wait_ge(*emptied(n, "qkv", b, t, c))
                                    for e, (x, w) in enumerate(products):
                                        for d in range(KD):
                                            at = start_of("y", b, d) + t * P
                                            mm = pe.matmul(bank("qkv", b, t, c)[:, :], flat[x][:, b, at:at + P],
                                                           wqkv[w][:, d, c * INNER:(c + 1) * INNER],
                                                           start=(e == 0 and d == 0), stop=(e == 2 and d == KD - 1))
                                    mm.then_inc(fills("qkv", b, t, c), 1)
                        if stage == "qkT":
                            pe.wait_ge(*qk_ready.of(n, 4 * b + 4))
                            for g in range(2):
                                for c in range(2):
                                    pe.wait_ge(*emptied(n, "qkT", b, g, c))
                                    for pr in range(2):
                                        for t in range(T):
                                            at = (2 * g + pr) * P
                                            mm = pe.transpose(bank("qkT", b, g, c)[:, pr * N + t * P:pr * N + (t + 1) * P],
                                                              rot[:, 4 * b + 2 * t + c, at:at + P], ident[:, :])
                                    mm.then_inc(fills("qkT", b, g, c), 1)
                        def scores(head):
                            pr, par = head // 2, head % 2
                            pe.wait_ge(*emptied(n, "s", b, head))
                            to = bank("s", b, head)
                            pe.matmul(to[:, 0:PAIRS_OF_TILES * P], ident_b[:, :], mask[:, :], start=True, stop=False,
                                      skip_group_check=True)
                            for t in range(T):
                                for e, (x, y) in enumerate(products):
                                    mm = pe.matmul(to[:, t * P:t * P + (t + 1) * P], q[x][:, b, pr, par, t * P:(t + 1) * P],
                                                   k[y][:, b, pr, 0:(t + 1) * P], start=False, stop=(e == 2),
                                                   skip_group_check=True)
                            mm.then_inc(fills("s", b, head), 1)

                        def turn_probs(head):
                            pe.wait_ge(*probs_ready.of(n, H * b + head + 1))
                            pe.wait_ge(*emptied(n, "pT", b, head))
                            for src, dst in enumerate((0, 1, 2)):
                                mm = pe.transpose(bank("pT", b, head)[:, dst * P:(dst + 1) * P],
                                                  probs[:, (H * b + head) % SLOTS, src * P:(src + 1) * P], ident[:, :])
                            mm.then_inc(fills("pT", b, head), 1)

                        def values(head):
                            g, pr, par = head // 4, head // 2 % 2, head % 2
                            if head % 4 == 0:
                                pe.wait_ge(*emptied(n, "pv", b, g))
                            pe.wait_ge(*probsT_ready.of(n, H * b + head + 1))
                            p = probsT[:, (H * b + head) % SLOTS]
                            for t in range(T):
                                mm = pe.matmul(bank("pv", b, g)[HD * par:HD * (par + 1), pr * N + t * P:(pr + 1) * N],
                                               v[:, b, t, head * HD:(head + 1) * HD], p[:, t * N:N + t * P],
                                               start=(t == 0), stop=(t == T - 1), skip_group_check=True)
                            mm.then_inc(probsT_used.sem, 1)

                        if stage == "lead":
                            pe.wait_ge(*turned_lo.of(n, 4 * b + 4))
                            for head in range(LEAD):
                                scores(head)
                            pe.wait_ge(*v_ready.of(n, T * (b + 1)))
                        if stage in HEADS:
                            for head in HEADS[stage]:
                                if head + LEAD < H:
                                    scores(head + LEAD)
                                turn_probs(head)
                                if head > 0:
                                    values(head - 1)
                            if head == H - 1:
                                values(head)
                        if stage == "wo":
                            pe.wait_ge(*o_lo.of(n, 2 * b + 2))
                            pe.wait_ge(*emptied(n, "wo", b))
                            for t in range(T):
                                for e, (x, w) in enumerate(products):
                                    for p in range(HP):
                                        mm = pe.matmul(bank("wo", b)[:, t * D:(t + 1) * D],
                                                       k[x][:, b, p, t * P:(t + 1) * P], wo[w][:, p, :],
                                                       start=(e == 0 and p == 0), stop=(e == 2 and p == HP - 1))
                            mm.then_inc(fills("wo", b), 1)
                        if stage in HIDDEN:
                            if b == 0 and stage == "w1a":
                                pe.wait_ge(*lo_b.of(l, 1))
                            if stage == "w1a":
                                pe.wait_ge(*z_lo.of(n, b + 1))
                            for j in HIDDEN[stage]:
                                pe.wait_ge(*emptied(n, "w1", b, j))
                                for a in range(2):
                                    for e, (w, x) in enumerate(products):
                                        for d in range(KD):
                                            at, c = start_of("h", b, d), a * HID + j * P
                                            mm = pe.matmul(bank("w1", b, j)[:, a * N:(a + 1) * N], w1[w][:, d, c:c + P],
                                                           flat[x][:, b, at:at + N],
                                                           start=(e == 0 and d == 0), stop=(e == 2 and d == KD - 1))
                                mm.then_inc(fills("w1", b, j), 1)
                        if stage in ("w2a", "w2b"):
                            if stage == "w2a":
                                pe.wait_ge(*emptied(n, "w2", b))
                            for j in range(J - 1) if stage == "w2a" else (J - 1,):
                                pe.wait_ge(*u_lo.of(n, J * b + j + 1))
                                for t in range(T):
                                    for e, (x, w) in enumerate(products):
                                        mm = pe.matmul(bank("w2", b)[:, t * D:(t + 1) * D], u[x][:, j, t * P:(t + 1) * P],
                                                       w2[w][:, j, :], start=(e == 0 and j == 0 and t == 0),
                                                       stop=(e == 2 and j == J - 1), skip_group_check=True)
                            if stage == "w2b":
                                mm.then_inc(fills("w2", b), 1)

        @block.scalar
        def _(act):
            act.wait_ge(consts_in, 16 * 6)
            act.activation(ident_b[:, :], ident[:, :], ACT.Copy).then_inc(consts_cast, 1)
            act.activation(mask[:, :], rot[:, 0, 0:PAIRS_OF_TILES * P], ACT.Copy).then_inc(consts_cast, 1)
            act.wait_ge(set_up, 13)

            def turn_high(n, b):
                act.wait_ge(*full(n, "yT", b))
                act.activation(halves(flat[0], b), bank("yT", b)[:, :].rearrange("p (d t) -> p d t", d=KD),
                               ACT.Copy).then_inc(yT_hi.sem, 1)

            turn_high(0, 0)
            turn_high(0, 1)
            with act.Fori(0, LAYERS) as l:
                act.wait_ge(*full(l * PAIRS - 1, "qkT", 1, 1, 1))
                act.dma_start(raw_qkv, io["wqkv"][l].rearrange("(k p) n -> p k n", p=P)).then_inc(raw_a.sem, 16)
                act.dma_start(raw_wo, io["wo"][l].rearrange("(k p) n -> p k n", p=P)).then_inc(raw_a.sem, 16)
                act.wait_ge(*full(l * PAIRS - 1, "wo", 1))
                for kd in range(KD):
                    act.dma_start(raw_w1[kd], io["w1"][l, kd * P:(kd + 1) * P]).then_inc(raw_b.sem, 16)
                for dst, first, end in ((raw_w2, 0, j_rot), (raw_rest[:, 0:J - 1 - j_rot], j_rot, J - 1)):
                    act.dma_start(dst, io["w2"][l, first * P:end * P].rearrange("(k p) n -> p k n", p=P)).then_inc(raw_b.sem, 16)
                act.dma_start(raw_rest[0:HID_LAST, J - 1 - j_rot], io["w2"][l, (J - 1) * P:HID]).then_inc(raw_b.sem, 16)
                half = HD // 2
                for c, name in enumerate(("q_scale", "k_scale")):
                    src = io[name][l]
                    act.dma_start(scale[:, c, 0], src.partition_broadcast(P)).then_inc(small_in.sem, 16)
                    act.dma_start(scale[:, c, 1, 0:half], src[half:HD].partition_broadcast(P)).then_inc(small_in.sem, 16)
                    act.dma_start(scale[:, c, 1, half:HD], src[0:half].partition_broadcast(P)).then_inc(small_in.sem, 16)
                for c in range(2):
                    src = io["b1"][l][c * HID:(c + 1) * HID]
                    m = (J - 1) * P
                    act.dma_start(b1[:, c, 0:J - 1], src[0:m].rearrange("(j p) -> p j", p=P),
                                  allow_slow_non_contiguous=True).then_inc(small_in.sem, 16)
                    act.dma_start(b1[0:HID_LAST, c, J - 1:J], src[m:HID].rearrange("(p j) -> p j", j=1),
                                  allow_slow_non_contiguous=True).then_inc(small_in.sem, 16)
                act.dma_start(b2[:, :], io["b2"][l].partition_broadcast(P)).then_inc(small_in.sem, 16)
                for c, name in enumerate(("ln_g", "ln_b")):
                    act.dma_start(ln[:, c], io[name][l].rearrange("(k p) -> p k", p=P),
                                  allow_slow_non_contiguous=True).then_inc(small_in.sem, 16)
                act.wait_ge(*raw_a.of(l, 2))
                act.activation(wqkv[0][:, :, :], raw_qkv, ACT.Copy)
                act.wait_ge(*full(l * PAIRS - 1, "wo", 1))
                act.activation(wo[0][:, :, :], raw_wo, ACT.Copy).then_inc(hi_a.sem, 1)
                act.wait_ge(*raw_b.of(l, KD + 3))
                act.wait_ge(*full(l * PAIRS - 1, "w2", 1))
                for w, dst, raw, src in pieces:
                    last = act.activation(w[0][dst], raw[src], ACT.Copy)
                last.then_inc(hi_b.sem, 1)

                with act.Fori(0, PAIRS) as i:
                    n = l * PAIRS + i
                    for stage, b in SCHEDULE:
                        if stage == "turn":
                            turn_high(n + 1, b)
                        if stage == "qkv":
                            for t in range(T):
                                for c in range(2):
                                    m = 4 * b + 2 * t + c + 1
                                    act.wait_ge(*full(n, "qkv", b, t, c))
                                    act.wait_ge(*(ssq_sum.of(n, m - 2) if m > 2 else ssq_sum.before(n, 8 + m - 2)))
                                    act.activation(sq[:, c], bank("qkv", b, t, c)[:, :], ACT.Square).then_inc(sq_ready.sem, 1)
                                act.wait_ge(*full(n, "qkv", b, t, 2))
                                if b == 0 and t == 0:
                                    act.wait_ge(*lo_b.of(l, 1))
                                act.activation(v[:, b, t], bank("qkv", b, t, 2)[:, :], ACT.Copy).then_inc(v_ready.sem, 1)
                        if stage == "qkT":
                            for g in range(2):
                                for c in range(2):
                                    act.wait_ge(*full(n, "qkT", b, g, c))
                                    src = bank("qkT", b, g, c)[:, :].rearrange("p (r t) -> p r t", r=2)
                                    if c == 0:
                                        for par in range(2):
                                            rows = slice(HD * par, HD * (par + 1))
                                            last = act.activation(q[0][rows, b, 2 * g:2 * g + 2, par], src[rows], ACT.Copy)
                                    else:
                                        last = act.activation(k[0][:, b, 2 * g:2 * g + 2], src, ACT.Copy)
                                    last.then_inc(turned_hi.sem, 1)
                        def exponentials(head):
                            m = H * b + head + 1
                            act.wait_ge(*max_ready.of(n, m))
                            if head >= SLOTS or b == 1:
                                act.wait_ge(*full(n, "pT", *divmod(m - 1 - SLOTS, H)))
                            else:
                                act.wait_ge(*full(n - 1, "pT", *divmod(2 * H + m - 1 - SLOTS, H)))
                            for t in range(T):
                                at = slice(t * P, t * P + (t + 1) * P)
                                last = act.activation(probs[:, (m - 1) % SLOTS, at], bank("s", b, head)[:, at], ACT.Exp,
                                                      bias=nm[:, b, head, t:t + 1], accum_out=total[:, b, head, t:t + 1])
                            last.then_inc(exp_ready.sem, 1)

                        def copy_turned(head):
                            m = H * b + head + 1
                            act.wait_ge(*full(n, "pT", b, head))
                            act.wait_ge(*(probsT_used.of(n, m - SLOTS) if m > SLOTS else probsT_used.before(n, 2 * H + m - SLOTS)))
                            act.activation(probsT[:, (m - 1) % SLOTS, :], bank("pT", b, head)[:, 0:PAIRS_OF_TILES * P],
                                           ACT.Copy).then_inc(probsT_ready.sem, 1)

                        def output(g):
                            act.wait_ge(*probsT_used.of(n, H * b + 4 * (g + 1)))
                            act.activation(k[0][:, b, 2 * g:2 * g + 2], bank("pv", b, g)[:, :].rearrange("p (r t) -> p r t", r=2),
                                           ACT.Copy).then_inc(o_hi.sem, 1)

                        if stage == "lead":
                            for head in range(LEAD):
                                exponentials(head)
                        if stage in HEADS:
                            for head in HEADS[stage]:
                                for later in due(stage, head):
                                    exponentials(later)
                                copy_turned(head)
                                if head == 4:
                                    output(0)
                            if head == H - 1:
                                output(1)
                        if stage == "hturn":
                            act.wait_ge(*z_ready.of(n, b + 1))
                            act.activation(halves(flat[0], b), z.rearrange("p (d t) -> p d t", d=KD), ACT.Copy).then_inc(z_hi.sem, 1)
                        if stage in HIDDEN:
                            def rows(j):
                                return P if j < J - 1 else HID_LAST

                            def gelu(j):
                                m, r = J * b + j + 1, rows(j)
                                if m == 1:
                                    act.wait_ge(*small_in.of(l, 13))
                                act.wait_ge(*full(n, "w1", b, j))
                                act.wait_ge(*(uf_ready.of(n, m - 2) if m > 2 else uf_ready.before(n, 2 * J + m - 2)))
                                act.activation(gate[0:r, j % 2], bank("w1", b, j)[0:r, N:2 * N], ACT.Gelu,
                                               bias=b1[0:r, 1, j:j + 1]).then_inc(gate_ready.sem, 1)

                            def high(j):
                                r = rows(j)
                                act.wait_ge(*uf_ready.of(n, J * b + j + 1))
                                act.activation(u[0][0:r, j], uf[0:r, j % 2], ACT.Copy).then_inc(u_hi.sem, 1)

                            js = list(HIDDEN[stage])
                            gelu(js[0])
                            for j in js[1:]:
                                gelu(j)
                                high(j - 1)
                            high(js[-1])

        @block.gpsimd
        def _(pool):
            for i in range(2):
                pool.memset(q[i][:, :, :, :, :].bitcast(F32), 0.0).then_inc(set_up, 1)
                pool.memset(flat[i][:, :, :].bitcast(F32), 0.0).then_inc(set_up, 1)
                pool.memset(u[i][:, J - 1].bitcast(F32), 0.0).then_inc(set_up, 1)
                pool.memset(w2[i][:, J - 1].bitcast(F32), 0.0).then_inc(set_up, 1)
                pool.memset(w1[i][:, :, 2 * HID:].bitcast(F32), 0.0).then_inc(set_up, 1)
            pool.memset(zero_row[:, :], 0.0).then_inc(set_up, 1)
            pool.memset(mhalf[:, :], -0.5).then_inc(set_up, 1)
            pool.memset(eps[:, :], EPS).then_inc(set_up, 1)

            with pool.Fori(0, LAYERS) as l:
                with pool.Fori(0, PAIRS) as i:
                    n = l * PAIRS + i
                    for stage, b in SCHEDULE:
                        if stage == "qkv":
                            for t in range(T):
                                for c in range(2):
                                    m = 4 * b + 2 * t + c
                                    slot = rot[:, m].rearrange("p (h d) -> p h d", d=HD)
                                    pool.wait_ge(*ssq_ready.of(n, m + 1))
                                    pool.tensor_tensor(rnorm[:, b, t, c], ssq[:, b, t, c], mhalf[:, :], ALU.pow).then_inc(norm_ready.sem, 1)
                                    pool.wait_ge(*norm_ready.of(n, m + 1))
                                    pool.wait_ge(*sum_ready.of(n, m + 1))
                                    pool.tensor_tensor(slot, slot, rnorm[:, b, t, c].unsqueeze(2).to_broadcast([P, H, HD]),
                                                       ALU.mult).then_inc(qk_ready.sem, 1)
                        if stage in HEADS:
                            for head in HEADS[stage]:
                                m = H * b + head + 1
                                pool.wait_ge(*share_ready.of(n, m))
                                for t in range(T):
                                    p = probs[:, (m - 1) % SLOTS, t * P:t * P + (t + 1) * P]
                                    last = pool.tensor_tensor(p, p, share[:, b, head, t:t + 1].to_broadcast([P, (t + 1) * P]), ALU.mult)
                                last.then_inc(probs_ready.sem, 1)
                        if stage == "stats":
                            pool.wait_ge(*var_ready.of(n, b + 1))
                            pool.tensor_tensor(veps[:, b], mv[:, b, :, 1], eps[:, :], ALU.add).then_inc(eps_added.sem, 1)
                            pool.wait_ge(*eps_added.of(n, b + 1))
                            pool.tensor_tensor(rstd[:, b], veps[:, b], mhalf[:, 0:T], ALU.pow).then_inc(rstd_ready.sem, 1)
                        if stage == "hturn":
                            if b == 0:
                                pool.wait_ge(*small_in.of(l, 13))
                            pool.wait_ge(*full(n, "hT", b))
                            for t in range(T):
                                last = pool.tensor_tensor(h[:, b, t], y1[:, b, t], b2[:, :], ALU.add)
                            last.then_inc(y1b_ready.sem, 1)
                        if stage in HIDDEN:
                            for j in HIDDEN[stage]:
                                r = P if j < J - 1 else HID_LAST
                                pool.wait_ge(*u_hi.of(n, J * b + j + 1))
                                pool.tensor_tensor(u[1][0:r, j], uf[0:r, j % 2], u[0][0:r, j].bitcast(F32),
                                                   ALU.subtract).then_inc(u_lo.sem, 1)
                        if stage == "w2b":
                            pool.wait_ge(*y2_ready.of(n, b + 1))
                            pool.wait_ge(*x1_in[b].of(n, 1))
                            for t in range(T):
                                last = pool.tensor_tensor(x1[:, b, t], h[:, b, t], x1[:, b, t], ALU.add)
                            last.then_inc(out_ready.sem, 1)

        @block.vector
        def _(dve):
            dve.wait_ge(set_up, 13)
            dve.wait_ge(consts_in, 16 * 6)

            def turn_low(n, b):
                dve.wait_ge(*yT_hi.of(n, b + 1))
                dve.tensor_tensor(halves(flat[1], b), bank("yT", b)[:, :].rearrange("p (d t) -> p d t", d=KD),
                                  halves(flat[0], b).bitcast(F32), ALU.subtract).then_inc(yT_lo.sem, 1)

            turn_low(0, 0)
            turn_low(0, 1)
            with dve.Fori(0, LAYERS) as l:
                dve.wait_ge(*hi_a.of(l, 1))
                dve.tensor_tensor(wqkv[1][:, :, :], raw_qkv, wqkv[0][:, :, :].bitcast(F32), ALU.subtract)
                dve.tensor_tensor(wo[1][:, :, :], raw_wo, wo[0][:, :, :].bitcast(F32), ALU.subtract).then_inc(lo_a.sem, 1)
                dve.wait_ge(*small_in.of(l, 13))
                for c in range(2):
                    for s in range(2):
                        last = dve.tensor_tensor(table[:, c, s], turns[:, c, s],
                                                 scale[:, c, s].unsqueeze(1).to_broadcast([P, T, HD]), ALU.mult)
                last.then_inc(table_ready.sem, 1)
                dve.wait_ge(*hi_b.of(l, 1))
                for w, dst, raw, src in pieces:
                    last = dve.tensor_tensor(w[1][dst], raw[src], w[0][dst].bitcast(F32), ALU.subtract)
                last.then_inc(lo_b.sem, 1)

                with dve.Fori(0, PAIRS) as i:
                    n = l * PAIRS + i
                    for stage, b in SCHEDULE:
                        if stage == "turn":
                            turn_low(n + 1, b)
                        if stage == "qkv":
                            for t in range(T):
                                for c in range(2):
                                    m = 4 * b + 2 * t + c
                                    src = bank("qkv", b, t, c)[:, :].rearrange("p (h d) -> p h d", d=HD)
                                    first = rot[:, m].rearrange("p (h d) -> p h d", d=HD)
                                    second = rot[:, 8 + m % 2].rearrange("p (h d) -> p h d", d=HD)
                                    half = HD // 2
                                    dve.wait_ge(*sq_ready.of(n, m + 1))
                                    dve.tensor_reduce(ssq[:, b, t, c], sq[:, c].rearrange("p (h d) -> p h d", d=HD),
                                                      AX_X, ALU.add).then_inc(ssq_sum.sem, 1)
                                    if m == 0:
                                        dve.wait_ge(*table_ready.of(l, 1))
                                        dve.wait_ge(*lo_b.of(l, 1))
                                    dve.tensor_tensor(first, src, table[:, c, 0, t].unsqueeze(1).to_broadcast([P, H, HD]), ALU.mult)
                                    dve.wait_ge(*(sum_ready.of(n, m - 1) if m >= 2 else sum_ready.before(n, 8 + m - 1)))
                                    dve.tensor_tensor(second[:, :, 0:half], src[:, :, half:HD],
                                                      table[:, c, 1, t, 0:half].unsqueeze(1).to_broadcast([P, H, half]), ALU.mult)
                                    dve.tensor_tensor(second[:, :, half:HD], src[:, :, 0:half],
                                                      table[:, c, 1, t, half:HD].unsqueeze(1).to_broadcast([P, H, half]),
                                                      ALU.mult).then_inc(terms_ready.sem, 1)
                                    dve.wait_ge(*ssq_sum.of(n, m + 1))
                                    dve.tensor_scalar(ssq[:, b, t, c], ssq[:, b, t, c], NORM_FLOOR ** 2, None,
                                                      ALU.max).then_inc(ssq_ready.sem, 1)
                                    dve.wait_ge(*terms_ready.of(n, m + 1))
                                    dve.tensor_tensor(rot[:, m], rot[:, m], rot[:, 8 + m % 2], ALU.add).then_inc(sum_ready.sem, 1)
                        if stage == "qkT":
                            for g in range(2):
                                for c in range(2):
                                    dve.wait_ge(*turned_hi.of(n, 4 * b + 2 * g + c + 1))
                                    src = bank("qkT", b, g, c)[:, :].rearrange("p (r t) -> p r t", r=2)
                                    if c == 0:
                                        for par in range(2):
                                            rows = slice(HD * par, HD * (par + 1))
                                            last = dve.tensor_tensor(q[1][rows, b, 2 * g:2 * g + 2, par], src[rows],
                                                                     q[0][rows, b, 2 * g:2 * g + 2, par].bitcast(F32), ALU.subtract)
                                    else:
                                        last = dve.tensor_tensor(k[1][:, b, 2 * g:2 * g + 2], src,
                                                                 k[0][:, b, 2 * g:2 * g + 2].bitcast(F32), ALU.subtract)
                                    last.then_inc(turned_lo.sem, 1)
                        def maxima(head):
                            dve.wait_ge(*full(n, "s", b, head))
                            for t in range(T):
                                last = dve.tensor_reduce(nm[:, b, head, t:t + 1], bank("s", b, head)[:, t * P:t * P + (t + 1) * P],
                                                         AX_X, ALU.max, negate=True)
                            last.then_inc(max_ready.sem, 1)

                        def invert(head):
                            m = H * b + head + 1
                            dve.wait_ge(*exp_ready.of(n, m))
                            dve.reciprocal(share[:, b, head], total[:, b, head]).then_inc(share_ready.sem, 1)

                        def output_low(g):
                            dve.wait_ge(*o_hi.of(n, 2 * b + g + 1))
                            dve.tensor_tensor(k[1][:, b, 2 * g:2 * g + 2], bank("pv", b, g)[:, :].rearrange("p (r t) -> p r t", r=2),
                                              k[0][:, b, 2 * g:2 * g + 2].bitcast(F32), ALU.subtract).then_inc(o_lo.sem, 1)

                        if stage == "lead":
                            for head in range(LEAD):
                                maxima(head)
                        if stage in HEADS:
                            for head in HEADS[stage]:
                                invert(head)
                                for later in due(stage, head):
                                    maxima(later)
                                if head == 5:
                                    output_low(0)
                            if head == H - 1:
                                output_low(1)
                        if stage == "wo":
                            dve.wait_ge(*full(n, "wo", b))
                            dve.tensor_tensor(y1[:, b], bank("wo", b)[:, :].rearrange("p (t d) -> p t d", t=T), yn[:, b],
                                              ALU.add).then_inc(y1_ready.sem, 1)
                        if stage == "stats":
                            dve.wait_ge(*shifted[b].of(n, 5))
                            for t in range(T):
                                last = dve.bn_stats(stats[:, b, t], h[:, b, t])
                            last.then_inc(stats_ready.sem, 1)
                            dve.wait_ge(*stats_ready.of(n, b + 1))
                            dve.tensor_copy(carrier[:, :], stats[:, b, :, 0])
                            for t in range(T):
                                last = dve.bn_aggr(mv[:, b, t], stats[:, b, t])
                            last.then_inc(var_ready.sem, 1)
                        if stage == "norm":
                            dve.wait_ge(*rstd_ready.of(n, b + 1))
                            for t in range(T):
                                last = dve.tensor_scalar(h[:, b, t], h[:, b, t], mv[:, b, t, 0:1], rstd[:, b, t:t + 1],
                                                         ALU.subtract, ALU.mult)
                            last.then_inc(h_ready.sem, 1)
                        if stage == "hturn":
                            dve.wait_ge(*full(n, "hT", b))
                            for d in range(KD):
                                last = dve.tensor_scalar(z[:, d * N:(d + 1) * N], bank("hT", b)[:, d * N:(d + 1) * N],
                                                         ln[:, 0, d:d + 1], ln[:, 1, d:d + 1], ALU.mult, ALU.add)
                            last.then_inc(z_ready.sem, 1)
                            dve.wait_ge(*z_hi.of(n, b + 1))
                            dve.tensor_tensor(halves(flat[1], b), z.rearrange("p (d t) -> p d t", d=KD),
                                              halves(flat[0], b).bitcast(F32), ALU.subtract).then_inc(z_lo.sem, 1)
                        if stage in HIDDEN:
                            for j in HIDDEN[stage]:
                                m, r = J * b + j + 1, (P if j < J - 1 else HID_LAST)
                                dve.wait_ge(*gate_ready.of(n, m))
                                dve.wait_ge(*(u_lo.of(n, m - 2) if m > 2 else u_lo.before(n, 2 * J + m - 2)))
                                dve.scalar_tensor_tensor(uf[0:r, j % 2], bank("w1", b, j)[0:r, 0:N], b1[0:r, 0, j:j + 1],
                                                         gate[0:r, j % 2], ALU.add, ALU.mult).then_inc(uf_ready.sem, 1)
                        if stage == "w2b":
                            dve.wait_ge(*full(n, "w2", b))
                            dve.wait_ge(*y1b_ready.of(n, b + 1))
                            dve.tensor_tensor(h[:, b], bank("w2", b)[:, :].rearrange("p (t d) -> p t d", t=T), h[:, b],
                                              ALU.add).then_inc(y2_ready.sem, 1)



INPUTS = (("x", "x"), ("ctx", "ctx_1024"), ("wq", "L0_xattn_wq"), ("bq", "L0_xattn_bq"), ("wk", "L0_xattn_wk"),
          ("bk", "L0_xattn_bk"), ("wv", "L0_xattn_wv"), ("bv", "L0_xattn_bv"), ("wqkv", "L0_ffn_wqkv"),
          ("q_scale", "L0_ffn_q_scale"), ("k_scale", "L0_ffn_k_scale"), ("wo", "L0_ffn_wo"),
          ("ln_g", "L0_ffn_ln_g"), ("ln_b", "L0_ffn_ln_b"), ("w1", "L0_ffn_w1"), ("b1", "L0_ffn_b1"),
          ("w2", "L0_ffn_w2"), ("b2", "L0_ffn_b2"))


def build(nc, io, out):
    dram = {
        "parts": nc.dram_tensor("parts", (2, 2, 3, D, N), BF16).ap(),
        "x1": nc.dram_tensor("x1", (B, N, D), F32).ap(),
        "y": nc.dram_tensor("y", ((LAYERS + 1) * B, N, D), F32).ap(),
    }
    cross_attention(nc, io, dram)
    layers(nc, io, dram, out)


def kernel(**inputs):
    import concourse.bacc as bacc
    from concourse.bass_utils import run_bass_kernel_spmd

    nc = bacc.Bacc("TRN2", target_bir_lowering=False, num_devices=1)
    arrays = {short: np.ascontiguousarray(inputs[name]) for short, name in INPUTS} | constants()
    io = {k: nc.dram_tensor("in_" + k, a.shape, mybir.dt.from_np(a.dtype), kind="ExternalInput").ap()
          for k, a in arrays.items()}
    out = nc.dram_tensor("out_dram", (B, N, D), F32, kind="ExternalOutput").ap()
    build(nc, io, out)
    r = run_bass_kernel_spmd(nc, [{"in_" + k: a for k, a in arrays.items()}], core_ids=[0])
    return r.results[0]["out_dram"]
```

```python
from collections import namedtuple
from contextlib import ExitStack

import concourse.mybir as mybir
import numpy as np

ALU = mybir.AluOpType
ACT = mybir.ActivationFunctionType
F32 = mybir.dt.float32
F32R = mybir.dt.float32r
BF16 = mybir.dt.bfloat16
AX_X = mybir.AxisListType.X

P = 128
B, N, D = 8, 256, 256
T = N // P
KD = D // P
PAIRS = B // 2
XH, XD = 16, D // 16
LAYERS = 2
H, HD = 8, 64
INNER = H * HD
HP = INNER // P
WINDOW = 128
HID = int(D * 4 * 2 / 3)
J = -(-HID // P)
HID_LAST = HID - (J - 1) * P
ROUNDS = LAYERS * PAIRS
VW = 32
PART_PAIRS = ((0, 0), (0, 1), (0, 2), (1, 0), (1, 1), (1, 2), (2, 0), (2, 1))
MASKED = -1e30
GAP = 2
PAIRS_OF_TILES = 3
SLOTS = 4
EPS = 1e-5
NORM_FLOOR = 1e-12


def constants():
    half = np.arange(0, HD, 2, dtype=np.float32)
    inv = (1.0 / np.float32(10000.0) ** (half / np.float32(HD))).astype(np.float32)
    t = np.arange(N, dtype=np.float32)
    f = (t[:, None] * inv[None, :]).astype(np.float32)
    f = np.concatenate([f, f], 1).astype(np.float64)
    base = (half + np.float32(0.4 * HD)) / np.float32(1.4 * HD)
    power = (t - N // 2) / np.float32(WINDOW // 2)
    s = (base[None, :].astype(np.float32) ** power[:, None].astype(np.float32)).astype(np.float64)
    s = np.concatenate([s, s], 1)
    sign = np.where(np.arange(HD) < HD // 2, -1.0, 1.0)[None, :]
    rot = np.stack([np.stack([np.cos(f) * s * 8, np.sin(f) * sign * s * 8]),
                    np.stack([np.cos(f) / s, np.sin(f) * sign / s])]).astype(np.float32)
    i, j = np.arange(N)[:, None], np.arange(N)[None, :]
    off = (i < j) | (i > j + WINDOW) | ((i < WINDOW) & (j >= WINDOW))
    mask = np.where(off, MASKED, 0.0).astype(np.float32)
    mask = np.concatenate([mask[0:P, 0:P], mask[P:N, :]], 1)
    sel = np.zeros((P, XH, P), np.float32)
    for h in range(XH):
        sel[h, h] = sel[32 + h, h] = 1.0
    return {"c_rot": rot, "c_mask": mask, "c_sel": sel, "c_ident": np.eye(P, dtype=np.float32)}
class Signal:

    def __init__(self, sem, per_round, by=1):
        self.sem, self.per_round, self.by = sem, per_round, by

    def of(self, n, k):
        return self.sem, (n * self.per_round + (self.per_round + k)) * self.by

    def before(self, n, k):
        return self.sem, (n * self.per_round + k) * self.by


Unit = namedtuple("Unit", "bank ahead number before")


def place(order):
    turn, inside = {}, {}
    for ring, unit, ahead in order:
        k = ring[turn.get(ring, 0) % len(ring)]
        turn[ring] = turn.get(ring, 0) + 1
        inside.setdefault(k, []).append((unit, ahead))
    at, counts = {}, {}
    for k, units in inside.items():
        names = [unit for unit, _ in units]
        for i, (unit, ahead) in enumerate(units):
            counts[k, ahead] = counts.get((k, ahead), 0) + 1
            before = [(0, u) for u in names[:i][::-1]] + [(1, u) for u in names[::-1]]
            at[unit] = Unit(k, ahead, counts[k, ahead], before)
    return at, counts


def cross_attention(nc, io, dram, raw):
    def attention(b):
        ahead, other = (1, 0) if b == 1 else (0, 1)
        half = XH // 2
        steps = [("ln", b, 1, ()), ("lead", b, 0, ())]
        for h in range(half):
            steps += [("heads", b, 0, (h,))] + ([("turn", b, 1, ())] if h == half - 3 else [])
        steps += [("kq", b, 1, ())]
        for h in range(half):
            steps += [("heads", b, 0, (half + h,))]
            steps += [("parts", b, 1, (h // 2,))] if h in (0, 2) else []
            steps += [("max", other, ahead, (2 * h, 2 * h + 1))]
        return steps + [("v", b, 1, ()), ("mT", other, ahead, ()), ("out", b, 0, ())]

    SCHEDULE = attention(0) + attention(1)
    FRONT = (("ln", ()), ("turn", ()), ("kq", ()), ("parts", (0,)), ("parts", (1,)))
    BEFORE = ([(stage, 0, 1, heads) for stage, heads in FRONT] + [("v", 0, 1, ())]
              + [(stage, 1, 1, heads) for stage, heads in FRONT]
              + [("max", 0, 1, tuple(range(XH))), ("v", 1, 1, ()), ("mT", 0, 1, ())])
    LEAD = 2
    ring, own = (0, 1, 2, 3, 4, 5), (6, 7)
    order = []
    for stage, b, ahead, heads in SCHEDULE:
        if stage == "turn":
            order += [(ring, ("cT", b), ahead), (ring, ("xT", b), ahead)]
        if stage == "kq":
            order += [(ring, (c, b), ahead) for c in "kq"]
        if stage == "v":
            order += [(ring, ("v", b), ahead)]
        if stage == "max":
            order += [(ring, ("s", b, h), ahead) for h in heads]
        if stage == "mT":
            order += [(ring, ("mT", b), ahead)]
        if stage == "lead":
            order += [(ring, ("e", b, h), ahead) for h in range(LEAD)]
        if stage == "heads":
            order += [(ring, ("e", b, h + LEAD), ahead) for h in heads if h + LEAD < XH]
            order += [(own, ("pv", b, h // 8), ahead) for h in heads if h % 8 == 0]
        if stage == "out":
            order += [(ring, ("o", b, t), ahead) for t in range(T)]
    units, per_bank = place(order)
    signals = []
    ctx = ExitStack()
    with ctx:
        def sb(name, shape, dt):
            return ctx.enter_context(nc.sbuf_tensor("x_" + name, shape, dt))

        def signal(name, per_round, by=1):
            signals.append(Signal(ctx.enter_context(nc.semaphore("x_" + name)), per_round, by))
            return signals[-1]

        def sem(name):
            return ctx.enter_context(nc.semaphore("x_" + name))

        psum = [ctx.enter_context(nc.psum_tensor(f"x_ps{i}", [P, 512], F32)) for i in range(8)]
        ident, ident_in = raw.ident, raw.ident_in
        sel_f = sb("sel_f", [P, XH, P], F32)
        sel = sb("sel", [P, XH, P], BF16)
        wraw = sb("wraw", [P, 3, KD, D], F32)
        whi = sb("whi", [P, 3, KD, D], F32R)
        wlo = sb("wlo", [P, 3, KD, D], F32R)
        bqk = sb("bqk", [P, 2, KD], F32)
        bv = sb("bv", [P, D], F32)
        mhalf = sb("mhalf", [P, T], F32)
        xin = sb("xin", [P, 2, T, D], F32)
        xres = sb("xres", [P, 2, T, D], F32)
        cin = sb("cin", [P, 2, T, D], F32)
        stats = sb("stats", [P, 2, 2, T, 6], F32)
        mv = sb("mv", [P, 2, 2, T, 2], F32)
        veps = sb("veps", [P, 2, 2, T], F32)
        eps = sb("eps", [P, T], F32)
        carrier = sb("carrier", [P, T], F32)
        rstd = sb("rstd", [P, 2, 2, T], F32)
        xn = sb("xn", [P, 2, T, D], F32)
        hi = sb("hi", [P, 2, 2, KD, N], F32R)
        lo = sb("lo", [P, 2, 2, KD, N], F32R)
        qk = sb("qk", [P, 2, 2, KD, N], F32)
        rest = sb("rest", [P, 2, 2, KD, N], F32)
        parts = sb("parts", [P, 2, 2, 3, KD, N], BF16)
        stack = sb("stack", [P, 2, 2, XH, N], BF16)
        va = sb("va", [P, 2, T, XH, VW], F32)
        nm = sb("nm", [P, 2, T, XH], F32)
        mrow = sb("mrow", [P, 2, N], BF16)
        probs = sb("probs", [P, SLOTS, T * N], F32)
        oT = sb("oT", [P, 2, 4, N], F32)
        rden = sb("rden", [P, 2, T, XH], F32)
        x1 = sb("x1", [P, 2, T, D], F32)
        y = sb("y", [P, 2, T, D], F32)

        consts_in, sel_cast = sem("consts_in"), sem("sel_cast")
        weights_in, biases_in = sem("weights_in"), sem("biases_in")
        whi_ready, wlo_ready, set_up = sem("whi_ready"), sem("wlo_ready"), sem("set_up")
        filled = {(k, ahead): signal(f"filled{k}_{ahead}", m) for (k, ahead), m in per_bank.items()}
        x_in = [signal(f"x_in{b}", 1, 16) for b in range(2)]
        xres_in = [signal(f"xres_in{b}", 1, 16) for b in range(2)]
        c_in = [signal(f"c_in{b}", 1, 16) for b in range(2)]
        stats_ready, var_ready = [[signal(f"{name}{s}", 2) for s in range(2)] for name in ("stats_ready", "var_ready")]
        eps_added, rstd_ready = [[signal(f"{name}{s}", 2) for s in range(2)] for name in ("eps_added", "rstd_ready")]
        xn_ready = signal("xn_ready", 2)
        hi_ready, lo_ready = signal("hi_ready", 4), signal("lo_ready", 4)
        qk_ready, p1_ready, rest_ready = signal("qk_ready", 4), signal("p1_ready", 4), signal("rest_ready", 4)
        p2_ready, p3_ready = signal("p2_ready", 4), signal("p3_ready", 4)
        v_ready = signal("v_ready", 2)
        parts_out = [signal(f"parts_out{b}", 2, 16) for b in range(2)]
        stacks_in = [signal(f"stacks_in{b}", 2 * len(PART_PAIRS), 16) for b in range(2)]
        max_ready = [signal(f"max_ready{b}", XH) for b in range(2)]
        m1_ready, m2_ready = [[signal(f"{name}{b}", 1) for b in range(2)] for name in ("m1_ready", "m2_ready")]
        probs_ready, probs_used = signal("probs_ready", 2 * XH), signal("probs_used", 2 * XH)
        oT_ready = signal("oT_ready", 4)
        rden_ready, att_ready, x1_ready = signal("rden_ready", 4), signal("att_ready", 4), signal("x1_ready", 4)
        y_ready = signal("y_ready", 2)
        x1_out = [signal(f"x1_out{b}", 1, 16) for b in range(2)]
        y_out = [signal(f"y_out{b}", 1, 16) for b in range(2)]

        reader = {
            "cT": lambda b: (lo_ready, 2 * b + 1), "xT": lambda b: (lo_ready, 2 * b + 2),
            "k": lambda b: (qk_ready, 2 * b + 1), "q": lambda b: (qk_ready, 2 * b + 2),
            "v": lambda b: (v_ready, b + 1),
            "s": lambda b, h: (max_ready[b], h + 1), "mT": lambda b: (m2_ready[b], 1),
            "e": lambda b, h: (probs_ready, XH * b + h + 1), "pv": lambda b, g: (oT_ready, 2 * b + g + 1),
            "o": lambda b, t: (att_ready, T * b + t + 1),
        }

        def bank(unit):
            return psum[units[unit].bank]

        def full(m, unit):
            u = units[unit]
            return filled[u.bank, u.ahead].of(m, u.number)

        def fills(unit):
            u = units[unit]
            return filled[u.bank, u.ahead].sem

        def wait_emptied(pe, n, unit, stages, last):
            for rounds_back, before in units[unit].before:
                ahead = units[before].ahead
                if stages is BEFORE and rounds_back:
                    return
                if (stages is BEFORE and not ahead) or (last and ahead and not rounds_back):
                    continue
                by, k = reader[before[0]](*before[1:])
                pe.wait_ge(*by.of(n - rounds_back + ahead, k))
                return

        for s in signals:
            nc.sync.sem_inc(s.sem, s.per_round * s.by)

        block = ctx.enter_context(nc.Block())

        @block.sync
        def _(sp):
            sp.dma_start(ident[:, :], io["c_ident"]).then_inc(ident_in, 16)

            def load(m, b):
                sp.wait_ge(*xn_ready.before(m, b + 1))
                sp.dma_start(xin[:, b], io["x"][m * 2 + b].rearrange("(t p) d -> p t d", p=P)).then_inc(x_in[b].sem, 16)
                sp.wait_ge(*full(m - 1, ("cT", b)))
                sp.dma_start(cin[:, b], io["ctx"][m * 2 + b].rearrange("(t p) d -> p t d", p=P)).then_inc(c_in[b].sem, 16)

            def restack(m, b):
                sp.wait_ge(*p3_ready.of(m, 2 * b + 2))
                for c in range(2):
                    sp.dma_start(dram["parts"][b, c].rearrange("s (k p) t -> p s k t", p=P),
                                 parts[:, b, c]).then_inc(parts_out[b].sem, 16)
                sp.wait_ge(*probs_used.of(m - 1, XH * (b + 1)))
                sp.wait_ge(*parts_out[b].of(m, 2))
                for c in range(2):
                    for g, pair in enumerate(PART_PAIRS):
                        sp.dma_start(stack[XD * g:XD * (g + 1), b, c],
                                     dram["parts"][b, c, pair[c]].rearrange("(h r) t -> r h t", r=XD)
                                     ).then_inc(stacks_in[b].sem, 16)

            def body(n, last):
                for b in range(2):
                    if not last:
                        load(n + 1, b)
                for b in range(2):
                    sp.wait_ge(*x1_ready.before(n, T * (b + 1)))
                    sp.dma_start(xres[:, b], io["x"][n * 2 + b].rearrange("(t p) d -> p t d", p=P)).then_inc(xres_in[b].sem, 16)
                if last:
                    for c in range(2):
                        for s in range(2):
                            sp.dma_start(raw.turns[:, c, s], io["c_rot"][c, s].rearrange("(t p) d -> p t d", p=P)).then_inc(raw.consts_in, 16)
                    sp.dma_start(raw.mask, io["c_mask"]).then_inc(raw.consts_in, 16)
                    for b in range(2):
                        sp.wait_ge(*y_out[b].of(0, 1))
                        sp.dma_start(raw.yn[:, b], dram["y"][b].rearrange("(t p) d -> p t d", p=P)).then_inc(raw.y_in[b].sem, 16)
                    load_weights(sp, io, raw, 0)
                    load_vectors(sp, io, raw, 0)
                for b in range(2):
                    if not last:
                        restack(n + 1, b)
                    sp.wait_ge(*x1_ready.of(n, T * (b + 1)))
                    sp.dma_start(dram["x1"][n * 2 + b].rearrange("(t p) d -> p t d", p=P), x1[:, b]).then_inc(x1_out[b].sem, 16)
                    sp.wait_ge(*y_ready.of(n, b + 1))
                    sp.dma_start(dram["y"][n * 2 + b].rearrange("(t p) d -> p t d", p=P), y[:, b]).then_inc(y_out[b].sem, 16)

            for b in range(2):
                load(0, b)
            sp.dma_start(sel_f[:, :, :], io["c_sel"]).then_inc(consts_in, 16)
            for b in range(2):
                restack(0, b)
            with sp.Fori(0, PAIRS - 1) as n:
                body(n, False)
            body(PAIRS - 1, True)
            for b in range(2):
                sp.wait_ge(*x1_out[b].of(PAIRS - 1, 1))
                sp.wait_ge(*y_out[b].of(PAIRS - 1, 1))

        @block.tensor
        def _(pe):
            pe.wait_ge(ident_in, 16)

            def body(n, stages, last):
                for stage, b, ahead, heads in stages:
                    m = n + ahead
                    if last and ahead:
                        continue
                    if stage == "turn":
                        for s, (kind, src) in enumerate((("cT", cin), ("xT", xn))):
                            if kind == "cT":
                                pe.wait_ge(*c_in[b].of(m, 1))
                            else:
                                pe.wait_ge(*xn_ready.of(m, b + 1))
                            wait_emptied(pe, n, (kind, b), stages, last)
                            for d in range(KD):
                                for t in range(T):
                                    mm = pe.transpose(bank((kind, b))[:, d * N + t * P:d * N + (t + 1) * P],
                                                      src[:, b, t, d * P:(d + 1) * P], ident[:, :])
                            mm.then_inc(fills((kind, b)), 1)
                    if stage in ("kq", "v"):
                        if stages is BEFORE and b == 0:
                            pe.wait_ge(whi_ready, 1)
                            pe.wait_ge(wlo_ready, 1)
                        pe.wait_ge(*lo_ready.of(m, 2 * b + 2))
                        for c in stage:
                            w = "kqv".index(c)
                            s = 1 if c == "q" else 0
                            wait_emptied(pe, n, (c, b), stages, last)
                            for half in range(2):
                                for i, (a, z) in enumerate(((hi, whi), (hi, wlo), (lo, whi))):
                                    for d in range(KD):
                                        at, wt = a[:, b, s, d], z[:, w, d]
                                        if c == "v":
                                            fixed, moving = at[:, half * P:(half + 1) * P], wt
                                        else:
                                            fixed, moving = wt[:, half * P:(half + 1) * P], at
                                        mm = pe.matmul(bank((c, b))[:, half * N:(half + 1) * N], fixed, moving,
                                                       start=(i == 0 and d == 0), stop=(i == 2 and d == KD - 1))
                            mm.then_inc(fills((c, b)), 1)
                    if stage == "max":
                        if heads[0] == 0:
                            pe.wait_ge(*stacks_in[b].of(m, 2 * len(PART_PAIRS)))
                        for h in heads:
                            wait_emptied(pe, n, ("s", b, h), stages, last)
                            for t in range(T):
                                mm = pe.matmul(bank(("s", b, h))[:, t * N:(t + 1) * N], stack[:, b, 1, h, t * P:(t + 1) * P],
                                               stack[:, b, 0, h, :], start=True, stop=True)
                            mm.then_inc(fills(("s", b, h)), 1)
                    if stage == "mT":
                        pe.wait_ge(*max_ready[b].of(m, XH))
                        wait_emptied(pe, n, ("mT", b), stages, last)
                        for t in range(T):
                            mm = pe.transpose(bank(("mT", b))[0:XH, t * P:(t + 1) * P], nm[:, b, t, :], ident[:, :])
                        mm.then_inc(fills(("mT", b)), 1)
                    if stage in ("lead", "heads"):
                        def scores(h):
                            wait_emptied(pe, n, ("e", b, h), stages, last)
                            for k in range(T):
                                to = bank(("e", b, h))[:, k * N:(k + 1) * N]
                                pe.matmul(to, stack[:, b, 0, h, k * P:(k + 1) * P], stack[:, b, 1, h, :],
                                          start=True, stop=False)
                                mm = pe.matmul(to, sel[:, h, :], mrow[:, b, :], start=False, stop=True)
                            mm.then_inc(fills(("e", b, h)), 1)

                        def values(pair):
                            g, c = pair[0] // 8, pair[0] // 4 % 2
                            if pair[0] % 8 == 0:
                                wait_emptied(pe, n, ("pv", b, g), stages, last)
                            pe.wait_ge(*probs_ready.of(n, XH * b + pair[-1] + 1))
                            for k in range(T):
                                for h in pair:
                                    q = VW * (h % 4)
                                    mm = pe.matmul(bank(("pv", b, g))[q:q + VW, c * N:(c + 1) * N], va[:, b, k, h, :],
                                                   probs[:, (XH * b + h) % SLOTS, k * N:(k + 1) * N],
                                                   start=(k == 0), stop=(k == T - 1), skip_group_check=True)
                                    if k == T - 1:
                                        mm.then_inc(probs_used.sem, 1)

                        if stage == "lead":
                            pe.wait_ge(*m2_ready[b].of(n, 1))
                            pe.wait_ge(*v_ready.of(n, b + 1))
                            for h in range(LEAD):
                                scores(h)
                        for h in heads:
                            if h + LEAD < XH:
                                scores(h + LEAD)
                            if h % 2 == 1:
                                values((h - 1, h))
                    if stage == "out":
                        pe.wait_ge(*oT_ready.of(n, 2 * b + 2))
                        for t in range(T):
                            wait_emptied(pe, n, ("o", b, t), stages, last)
                            for g in range(4):
                                mm = pe.transpose(bank(("o", b, t))[:, g * P:(g + 1) * P],
                                                  oT[:, b, g, t * P:(t + 1) * P], ident[:, :])
                            mm.then_inc(fills(("o", b, t)), 1)

            body(-1, BEFORE, False)
            pe.wait_ge(sel_cast, 1)
            pe.wait_ge(set_up, 5)
            for by, k in ((lo_ready, 4), (qk_ready, 4), (v_ready, 2), (max_ready[0], XH), (m2_ready[0], 1)):
                pe.wait_ge(*by.of(0, k))
            with pe.Fori(0, PAIRS - 1) as n:
                body(n, SCHEDULE, False)
            body(PAIRS - 1, SCHEDULE, True)

        @block.scalar
        def _(act):
            for c, w in enumerate(("wk", "wq", "wv")):
                act.dma_start(wraw[:, c], io[w].rearrange("(k p) n -> p k n", p=P)).then_inc(weights_in, 16)
            for c, w in enumerate(("bk", "bq")):
                act.dma_start(bqk[:, c], io[w].rearrange("(k p) -> p k", p=P),
                              allow_slow_non_contiguous=True).then_inc(biases_in, 16)
            act.dma_start(bv[:, :], io["bv"].partition_broadcast(P)).then_inc(biases_in, 16)
            act.wait_ge(weights_in, 16 * 3)
            act.activation(whi[:, :, :, :], wraw[:, :, :, :], ACT.Copy).then_inc(whi_ready, 1)
            act.wait_ge(set_up, 5)

            def body(n, stages, last):
                for stage, b, ahead, heads in stages:
                    m = n + ahead
                    if last and ahead:
                        continue
                    if stage == "turn":
                        for s, kind in enumerate(("cT", "xT")):
                            act.wait_ge(*full(m, (kind, b)))
                            act.activation(hi[:, b, s], bank((kind, b))[:, :].rearrange("p (k t) -> p k t", k=KD),
                                           ACT.Copy).then_inc(hi_ready.sem, 1)
                    if stage == "parts" and heads == (0,):
                        for c in range(2):
                            act.wait_ge(*qk_ready.of(m, 2 * b + c + 1))
                            act.activation(parts[:, b, c, 0], qk[:, b, c], ACT.Copy).then_inc(p1_ready.sem, 1)
                    if stage == "parts" and heads == (1,):
                        for c in range(2):
                            act.wait_ge(*rest_ready.of(m, 2 * b + c + 1))
                            act.activation(parts[:, b, c, 1], rest[:, b, c], ACT.Copy).then_inc(p2_ready.sem, 1)
                    if stage == "mT":
                        act.wait_ge(*full(m, ("mT", b)))
                        act.activation(mrow[0:XH, b, :], bank(("mT", b))[0:XH, 0:N], ACT.Copy).then_inc(m1_ready[b].sem, 1)
                    if stage == "heads":
                        def output(g):
                            act.wait_ge(*probs_used.of(n, XH * b + 8 * (g + 1)))
                            act.activation(oT[:, b, 2 * g:2 * g + 2],
                                           bank(("pv", b, g))[:, :].rearrange("p (g t) -> p g t", g=2),
                                           ACT.Copy).then_inc(oT_ready.sem, 1)

                        for h in heads:
                            i = XH * b + h
                            act.wait_ge(*full(n, ("e", b, h)))
                            act.wait_ge(*(probs_used.of(n, i + 1 - SLOTS) if i >= SLOTS
                                          else probs_used.before(n, 2 * XH + i + 1 - SLOTS)))
                            act.activation(probs[:, i % SLOTS, :], bank(("e", b, h))[:, :],
                                           ACT.Exp).then_inc(probs_ready.sem, 1)
                            if h == 8 + SLOTS:
                                output(0)
                            if h == XH - 1:
                                output(1)

            body(-1, BEFORE, False)
            act.wait_ge(consts_in, 16)
            act.activation(sel[:, :, :], sel_f[:, :, :], ACT.Copy).then_inc(sel_cast, 1)
            with act.Fori(0, PAIRS - 1) as n:
                body(n, SCHEDULE, False)
            body(PAIRS - 1, SCHEDULE, True)

        @block.gpsimd
        def _(pool):
            pool.memset(mhalf[:, :], -0.5).then_inc(set_up, 1)
            pool.memset(eps[:, :], EPS).then_inc(set_up, 1)
            pool.memset(mrow[:, :, :], 0.0).then_inc(set_up, 1)
            pool.memset(va[:, :, :, :, XD:VW], 0.0).then_inc(set_up, 1)
            pool.wait_ge(set_up, 4)
            pool.memset(va[:, :, :, :, XD:XD + 1], 1.0).then_inc(set_up, 1)

            def body(n, stages, last):
                for stage, b, ahead, heads in stages:
                    m = n + ahead
                    if last and ahead:
                        continue
                    if stage in ("ln", "out"):
                        s = 0 if stage == "ln" else 1
                        pool.wait_ge(*var_ready[s].of(m, b + 1))
                        pool.tensor_tensor(veps[:, b, s], mv[:, b, s, :, 1], eps[:, :], ALU.add).then_inc(eps_added[s].sem, 1)
                        pool.wait_ge(*eps_added[s].of(m, b + 1))
                        pool.tensor_tensor(rstd[:, b, s], veps[:, b, s], mhalf[:, :], ALU.pow).then_inc(rstd_ready[s].sem, 1)
                    if stage == "parts" and heads == (1,):
                        for c in range(2):
                            pool.wait_ge(*p2_ready.of(m, 2 * b + c + 1))
                            pool.tensor_tensor(parts[:, b, c, 2], rest[:, b, c], parts[:, b, c, 1],
                                               ALU.subtract).then_inc(p3_ready.sem, 1)

            body(-1, BEFORE, False)
            with pool.Fori(0, PAIRS - 1) as n:
                body(n, SCHEDULE, False)
            body(PAIRS - 1, SCHEDULE, True)

        @block.vector
        def _(dve):
            dve.wait_ge(whi_ready, 1)
            dve.tensor_tensor(wlo[:, :, :, :], wraw[:, :, :, :], whi[:, :, :, :].bitcast(F32),
                              ALU.subtract).then_inc(wlo_ready, 1)
            dve.wait_ge(set_up, 5)
            dve.wait_ge(biases_in, 16 * 3)

            def layernorm(n, b, s, src, dst, ready):
                for t in range(T):
                    done = dve.bn_stats(stats[:, b, s, t], src[:, b, t])
                done.then_inc(stats_ready[s].sem, 1)
                dve.wait_ge(*stats_ready[s].of(n, b + 1))
                dve.tensor_copy(carrier[:, :], stats[:, b, s, :, 0])
                for t in range(T):
                    done = dve.bn_aggr(mv[:, b, s, t], stats[:, b, s, t])
                done.then_inc(var_ready[s].sem, 1)
                dve.wait_ge(*rstd_ready[s].of(n, b + 1))
                for t in range(T):
                    done = dve.tensor_scalar(dst[:, b, t], src[:, b, t], mv[:, b, s, t, 0:1], rstd[:, b, s, t:t + 1],
                                             ALU.subtract, ALU.mult)
                done.then_inc(ready.sem, 1)

            def body(n, stages, last):
                for stage, b, ahead, heads in stages:
                    m = n + ahead
                    if last and ahead:
                        continue
                    if stage == "ln":
                        dve.wait_ge(*x_in[b].of(m, 1))
                        layernorm(m, b, 0, xin, xn, xn_ready)
                    if stage == "turn":
                        for s, kind in enumerate(("cT", "xT")):
                            dve.wait_ge(*hi_ready.of(m, 2 * b + s + 1))
                            dve.tensor_tensor(lo[:, b, s], bank((kind, b))[:, :].rearrange("p (k t) -> p k t", k=KD),
                                              hi[:, b, s].bitcast(F32), ALU.subtract).then_inc(lo_ready.sem, 1)
                    if stage == "kq":
                        for c, kind in enumerate("kq"):
                            dve.wait_ge(*full(m, (kind, b)))
                            for d in range(KD):
                                done = dve.tensor_scalar(qk[:, b, c, d], bank((kind, b))[:, d * N:(d + 1) * N],
                                                         bqk[:, c, d:d + 1], XD ** -0.5 if kind == "q" else 1.0,
                                                         ALU.add, ALU.mult)
                            done.then_inc(qk_ready.sem, 1)
                    if stage == "parts" and heads == (0,):
                        for c in range(2):
                            dve.wait_ge(*p1_ready.of(m, 2 * b + c + 1))
                            dve.tensor_tensor(rest[:, b, c], qk[:, b, c], parts[:, b, c, 0],
                                              ALU.subtract).then_inc(rest_ready.sem, 1)
                    if stage == "v":
                        dve.wait_ge(*full(m, ("v", b)))
                        for t in range(T):
                            done = dve.tensor_tensor(va[:, b, t, :, 0:XD],
                                                     bank(("v", b))[:, t * N:(t + 1) * N].rearrange("p (h r) -> p h r", r=XD),
                                                     bv[:, :].rearrange("p (h r) -> p h r", r=XD), ALU.add)
                        done.then_inc(v_ready.sem, 1)
                    if stage == "max":
                        for h in heads:
                            dve.wait_ge(*full(m, ("s", b, h)))
                            dve.tensor_reduce(nm[:, b, :, h], bank(("s", b, h))[:, :].rearrange("p (t k) -> p t k", t=T),
                                              AX_X, ALU.max, negate=True).then_inc(max_ready[b].sem, 1)
                    if stage == "mT":
                        dve.wait_ge(*m1_ready[b].of(m, 1))
                        dve.tensor_tensor(mrow[32:32 + XH, b, :], bank(("mT", b))[0:XH, 0:N], mrow[0:XH, b, :],
                                          ALU.subtract).then_inc(m2_ready[b].sem, 1)
                    if stage == "out":
                        for t in range(T):
                            k = T * b + t + 1
                            o = bank(("o", b, t))[:, :].rearrange("p (h r) -> p h r", r=VW)
                            dve.wait_ge(*full(n, ("o", b, t)))
                            dve.reciprocal(rden[:, b, t], o[:, :, XD]).then_inc(rden_ready.sem, 1)
                            dve.wait_ge(*rden_ready.of(n, k))
                            if t == 0:
                                dve.wait_ge(*x1_out[b].before(n, 1))
                            dve.tensor_tensor(x1[:, b, t].rearrange("p (h r) -> p h r", r=XD), o[:, :, 0:XD],
                                              rden[:, b, t].unsqueeze(2).to_broadcast([P, XH, XD]),
                                              ALU.mult).then_inc(att_ready.sem, 1)
                            dve.wait_ge(*att_ready.of(n, k))
                            if t == 0:
                                dve.wait_ge(*xres_in[b].of(n, 1))
                            dve.tensor_tensor(x1[:, b, t], x1[:, b, t], xres[:, b, t], ALU.add).then_inc(x1_ready.sem, 1)
                        dve.wait_ge(*x1_ready.of(n, T * (b + 1)))
                        dve.wait_ge(*y_out[b].before(n, 1))
                        layernorm(n, b, 1, x1, y, y_ready)

            body(-1, BEFORE, False)
            with dve.Fori(0, PAIRS - 1) as n:
                body(n, SCHEDULE, False)
            body(PAIRS - 1, SCHEDULE, True)

Raw = namedtuple("Raw", "ident yn y_in turns scale b1 b2 ln rot v both mask qkv wo w1 w2 j_rot rest a_in b_in small_in ident_in "
                        "consts_in")


def raw_tiles(nc, ctx):
    def sb(name, shape, dt):
        return ctx.enter_context(nc.sbuf_tensor("r_" + name, shape, dt))

    def signal(name, per_round, by):
        return Signal(ctx.enter_context(nc.semaphore("r_" + name)), per_round, by)

    ident = sb("ident", [P, P], F32)
    yn = sb("yn", [P, 2, T, D], F32)
    turns = sb("turns", [P, 2, 2, T, HD], F32)
    scale = sb("scale", [P, 2, 2, HD], F32)
    b1 = sb("b1", [P, 2, J], F32)
    b2 = sb("b2", [P, D], F32)
    ln = sb("ln", [P, 2, KD], F32)
    rot = sb("rot", [P, 10, INNER], F32)
    v = sb("v", [P, 2, T, INNER], F32)
    both = sb("both", [P, 2, SLOTS, PAIRS_OF_TILES * P], F32)
    qkv = rot[:, 0:3 * KD].rearrange("p a c -> p (a c)").rearrange("p (k n) -> p k n", k=KD)
    wo = rot[:, 3 * KD:3 * KD + HP * D // INNER].rearrange("p a c -> p (a c)").rearrange("p (k n) -> p k n", k=HP)
    flat_v = v[:, :, :, :].rearrange("p b t n -> p (b t n)")
    w1 = [both[:, :, :, :].rearrange("p a s c -> p (a s c)")[:, 0:2 * HID], flat_v[:, 0:2 * HID]]
    w2 = rot[:, 3 * KD + HP * D // INNER:].rearrange("p a c -> p (a c)").rearrange("p (k n) -> p k n", n=D)
    j_rot = w2.shape[1]
    rest = flat_v[:, 2 * HID:2 * HID + (J - j_rot) * D].rearrange("p (k n) -> p k n", n=D)
    mask_raw = both[:, :, :, :].rearrange("p a s c -> p (a s c)")[:, 2 * HID:2 * HID + PAIRS_OF_TILES * P]
    a_in = [signal(f"raw_a{kd}", 1, 16) for kd in range(KD)]
    b_in, small_in = signal("raw_b", KD + 4, 16), signal("small_in", 13, 16)
    y_in = [signal(f"y_in{b}", 1, 16) for b in range(2)]
    ident_in = ctx.enter_context(nc.semaphore("r_ident_in"))
    consts_in = ctx.enter_context(nc.semaphore("r_consts_in"))
    for s in a_in + y_in + [b_in, small_in]:
        nc.sync.sem_inc(s.sem, s.per_round * s.by)
    return Raw(ident, yn, y_in, turns, scale, b1, b2, ln, rot, v, both, mask_raw, qkv, wo, w1, w2, j_rot, rest, a_in, b_in, small_in,
               ident_in, consts_in)


def load_weights(sp, io, raw, l):
    for kd in range(KD):
        sp.dma_start(raw.qkv[:, kd], io["wqkv"][l, kd * P:(kd + 1) * P]).then_inc(raw.a_in[kd].sem, 16)
    sp.dma_start(raw.wo, io["wo"][l].rearrange("(k p) n -> p k n", p=P)).then_inc(raw.b_in.sem, 16)
    for kd in range(KD):
        sp.dma_start(raw.w1[kd], io["w1"][l, kd * P:(kd + 1) * P]).then_inc(raw.b_in.sem, 16)
    for dst, first, end in ((raw.w2, 0, raw.j_rot), (raw.rest[:, 0:J - 1 - raw.j_rot], raw.j_rot, J - 1)):
        sp.dma_start(dst, io["w2"][l, first * P:end * P].rearrange("(k p) n -> p k n", p=P)).then_inc(raw.b_in.sem, 16)
    sp.dma_start(raw.rest[0:HID_LAST, J - 1 - raw.j_rot], io["w2"][l, (J - 1) * P:HID]).then_inc(raw.b_in.sem, 16)


def load_vectors(sp, io, raw, l):
    half, done = HD // 2, raw.small_in.sem
    for c, name in enumerate(("q_scale", "k_scale")):
        src = io[name][l]
        sp.dma_start(raw.scale[:, c, 0], src.partition_broadcast(P)).then_inc(done, 16)
        sp.dma_start(raw.scale[:, c, 1, 0:half], src[half:HD].partition_broadcast(P)).then_inc(done, 16)
        sp.dma_start(raw.scale[:, c, 1, half:HD], src[0:half].partition_broadcast(P)).then_inc(done, 16)
    for c in range(2):
        src = io["b1"][l][c * HID:(c + 1) * HID]
        m = (J - 1) * P
        sp.dma_start(raw.b1[:, c, 0:J - 1], src[0:m].rearrange("(j p) -> p j", p=P),
                     allow_slow_non_contiguous=True).then_inc(done, 16)
        sp.dma_start(raw.b1[0:HID_LAST, c, J - 1:J], src[m:HID].rearrange("(p j) -> p j", j=1),
                     allow_slow_non_contiguous=True).then_inc(done, 16)
    sp.dma_start(raw.b2[:, :], io["b2"][l].partition_broadcast(P)).then_inc(done, 16)
    for c, name in enumerate(("ln_g", "ln_b")):
        sp.dma_start(raw.ln[:, c], io[name][l].rearrange("(k p) -> p k", p=P),
                     allow_slow_non_contiguous=True).then_inc(done, 16)


def layers(nc, io, dram, out, raw):
    SCHEDULE = [("qkv_a", 0), ("qkv_b", 0), ("qkv_a", 1), ("qkT", 0), ("qkv_b", 1), ("lead", 0), ("heads_a", 0), ("heads_b", 0),
                ("heads_c", 0), ("qkT", 1), ("wo", 0), ("lead", 1), ("heads_a", 1), ("stats", 0), ("heads_b", 1), ("norm", 0),
                ("heads_c", 1), ("hturn", 0), ("wo", 1), ("w1a", 0), ("w1b", 0), ("stats", 1), ("w1c", 0), ("w2a", 0),
                ("norm", 1), ("hturn", 1), ("turn", 0), ("w2b", 0), ("w2c", 0), ("w1a", 1), ("w1b", 1), ("w1c", 1),
                ("turn", 1), ("w2a", 1), ("w2b", 1), ("w2c", 1)]
    TILE = {"qkv_a": 0, "qkv_b": 1}
    PRODUCTS = {"w2a": range(0, 3), "w2b": range(3, J - 1), "w2c": range(J - 1, J)}
    HEADS = {"heads_a": range(0, 2), "heads_b": range(2, 5), "heads_c": range(5, H)}
    HIDDEN = {"w1a": range(0, 2), "w1b": range(2, 4), "w1c": range(4, J)}
    LEAD = 4
    ring, turn_ring, own = (0, 1, 2, 3, 4), (5,), (6, 7)
    order = []
    for stage, b in SCHEDULE:
        if stage == "turn":
            order += [(turn_ring, ("yT", b), 0)]
        if stage in TILE:
            order += [(ring, ("qkv", b, TILE[stage], c), 0) for c in range(3)]
        if stage == "qkT":
            order += [(ring, ("qkT", b, g, c), 0) for g in range(2) for c in range(2)]
        if stage == "lead":
            order += [(ring, ("s", b, head), 0) for head in range(LEAD)]
        if stage in HEADS:
            for head in HEADS[stage]:
                if head + LEAD < H:
                    order += [(ring, ("s", b, head + LEAD), 0)]
                order += [(ring, ("pT", b, head), 0)]
                if head % 4 == 0:
                    order += [(own, ("pv", b, head // 4), 0)]
        if stage == "wo":
            order += [(ring, ("wo", b), 0)]
        if stage == "hturn":
            order += [(ring, ("hT", b), 0)]
        if stage in HIDDEN:
            order += [(ring, ("w1", b, j), 0) for j in HIDDEN[stage]]
        if stage == "w2a":
            order += [(ring, ("w2", b), 0)]
    units, per_bank = place(order)
    signals = []
    ctx = ExitStack()
    with ctx:
        def sb(name, shape, dt):
            return ctx.enter_context(nc.sbuf_tensor("l_" + name, shape, dt))

        def signal(name, per_round, by=1):
            signals.append(Signal(ctx.enter_context(nc.semaphore("l_" + name)), per_round, by))
            return signals[-1]

        def sem(name):
            return ctx.enter_context(nc.semaphore("l_" + name))

        psum = [ctx.enter_context(nc.psum_tensor(f"l_ps{i}", [P, 512], F32)) for i in range(8)]
        ident, yn, y_in, turns, scale, b1 = raw.ident, raw.yn, raw.y_in, raw.turns, raw.scale, raw.b1
        b2, ln, rot, v, both = raw.b2, raw.ln, raw.rot, raw.v, raw.both
        ident_b = sb("ident_b", [P, P], BF16)
        mask = sb("mask", [P, PAIRS_OF_TILES * P], BF16)
        mhalf = sb("mhalf", [P, H], F32)
        zero_row = sb("zero_row", [1, P], F32)
        table = sb("table", [P, 2, 2, T, HD], F32)
        wqkv = [sb("wqkv" + s, [P, KD, 3 * INNER], F32R) for s in ("hi", "lo")]
        wo = [sb("wo" + s, [P, HP, D], F32R) for s in ("hi", "lo")]
        w1 = [sb("w1" + s, [P, KD, 2 * HID + P - HID_LAST], F32R) for s in ("hi", "lo")]
        w2 = [sb("w2" + s, [P, J, D], F32R) for s in ("hi", "lo")]
        y1 = sb("y1", [P, 2, T, D], F32)
        h = sb("h", [P, 2, T, D], F32)
        x1 = sb("x1", [P, 2, T, D], F32)
        flat = [sb("yT" + s, [P, 2, 2 * (N + GAP)], F32R) for s in ("hi", "lo")]
        sq = sb("sq", [P, 2, INNER], F32)
        ssq = sb("ssq", [P, 2, T, 2, H], F32)
        rnorm = sb("rnorm", [P, 2, T, 2, H], F32)
        q = [sb("q" + s, [P, 2, HP, 2, N], F32R) for s in ("hi", "lo")]
        kk = sb("kk", [P, 2, 2, HP, N], F32R)
        k = [kk[:, 0], kk[:, 1]]
        nm = sb("nm", [P, 2, H, T], F32)
        total = sb("total", [P, 2, H, T], F32)
        share = sb("share", [P, 2, H, T], F32)
        probs = both[:, 0]
        probsT = both[:, 1]
        stats = sb("stats", [P, 2, T, 6], F32)
        mv = sb("mv", [P, 2, T, 2], F32)
        veps = sb("veps", [P, 2, T], F32)
        eps = sb("eps", [P, T], F32)
        carrier = sb("carrier", [P, T], F32)
        unread = sb("unread", [P, 2], F32)
        rstd = sb("rstd", [P, 2, T], F32)
        u = [sb("u" + s, [P, J, N], F32R) for s in ("hi", "lo")]
        uf = sb("uf", [P, 2, N], F32)
        everything = (slice(0, P), slice(0, HP))
        pieces_w1 = [(w1, (slice(0, P), k, slice(0, 2 * HID)), raw.w1[k], (slice(0, P), slice(0, 2 * HID))) for k in range(KD)]
        pieces = [(wo, everything, raw.wo, everything),
                  (w2, (slice(0, P), slice(0, raw.j_rot)), raw.w2, (slice(0, P), slice(0, raw.j_rot))),
                  (w2, (slice(0, P), slice(raw.j_rot, J - 1)), raw.rest, (slice(0, P), slice(0, J - 1 - raw.j_rot))),
                  (w2, (slice(0, HID_LAST), J - 1), raw.rest, (slice(0, HID_LAST), J - 1 - raw.j_rot))]
        z = sq[:, 0]
        gate = sq[:, 1].rearrange("p (s t) -> p s t", s=2)

        q_set, consts_cast, set_up, flat_set = sem("q_set"), sem("consts_cast"), sem("set_up"), sem("flat_set")
        table_ready = signal("table_ready", 1)
        hi_a, lo_a, hi_b, lo_b = signal("hi_a", KD), signal("lo_a", KD), signal("hi_b", 2), signal("lo_b", 1)
        lo_w1 = signal("lo_w1", 1)
        filled = {i: signal(f"filled{i}", m) for (i, _), m in per_bank.items()}
        x1_in = [signal(f"x1_in{b}", 1, 16) for b in range(2)]
        yT_hi, yT_lo = signal("yT_hi", 2), signal("yT_lo", 2)
        sq_ready, ssq_sum, ssq_ready = signal("sq_ready", 8), signal("ssq_sum", 8), signal("ssq_ready", 8)
        terms_ready, norm_ready, sum_ready = signal("terms_ready", 8), signal("norm_ready", 8), signal("sum_ready", 8)
        qk_ready, v_ready = signal("qk_ready", 8), signal("v_ready", 4)
        turned_hi, turned_lo = signal("turned_hi", 8), signal("turned_lo", 8)
        max_ready, exp_ready, probs_ready = signal("max_ready", 2 * H), signal("exp_ready", 2 * H), signal("probs_ready", 2 * H)
        share_ready = signal("share_ready", 2 * H)
        probsT_ready, probsT_used = signal("probsT_ready", 2 * H), signal("probsT_used", 2 * H)
        o_hi, o_lo = signal("o_hi", 4), signal("o_lo", 4)
        y1_ready = signal("y1_ready", 2)
        shifted = [signal(f"shifted{b}", 5, 16) for b in range(2)]
        stats_ready, var_ready = signal("stats_ready", 2), signal("var_ready", 2)
        eps_added, rstd_ready = signal("eps_added", 2), signal("rstd_ready", 2)
        h_ready, z_ready, z_hi, z_lo = signal("h_ready", 2), signal("z_ready", 2), signal("z_hi", 2), signal("z_lo", 2)
        y1b_ready = signal("y1b_ready", 2)
        gate_ready, uf_ready = signal("gate_ready", 2 * J), signal("uf_ready", 2 * J)
        u_hi, u_lo = signal("u_hi", 2 * J), signal("u_lo", 2 * J)
        y2_ready, out_ready = signal("y2_ready", 2), signal("out_ready", 2)
        y_out = [signal(f"y_out{b}", 1, 16) for b in range(2)]
        out_out = [signal(f"out_out{b}", 1, 16) for b in range(2)]

        reader = {
            "yT": lambda b: (yT_lo, b + 1),
            "qkv": lambda b, t, c: (terms_ready, 4 * b + 2 * t + c + 1) if c < 2 else (v_ready, T * b + t + 1),
            "qkT": lambda b, g, c: (turned_lo, 4 * b + 2 * g + c + 1),
            "s": lambda b, head: (exp_ready, H * b + head + 1), "pT": lambda b, head: (probsT_ready, H * b + head + 1),
            "pv": lambda b, g: (o_lo, 2 * b + g + 1), "wo": lambda b: (y1_ready, b + 1),
            "hT": lambda b: (z_ready, b + 1), "w1": lambda b, j: (uf_ready, J * b + j + 1),
            "w2": lambda b: (y2_ready, b + 1),
        }

        def bank(*unit):
            return psum[units[unit].bank]

        def full(n, *unit):
            return filled[units[unit].bank].of(n, units[unit].number)

        def fills(*unit):
            return filled[units[unit].bank].sem

        def emptied(n, *unit):
            rounds_back, before = units[unit].before[0]
            by, m = reader[before[0]](*before[1:])
            return by.before(n, m) if rounds_back else by.of(n, m)

        def halves(tile, b):
            return tile[:, b].rearrange("p (d c) -> p d c", d=2)[:, :, 0:N]

        def due(stage, head):
            group = HEADS[stage]
            heads = ([] if head == group[0] else [head + LEAD - 1]) + ([head + LEAD] if head == group[-1] else [])
            return [other for other in heads if other < H]

        products = ((0, 0), (0, 1), (1, 0))

        for s in signals:
            nc.sync.sem_inc(s.sem, s.per_round * s.by)

        block = ctx.enter_context(nc.Block())

        @block.sync
        def _(sp):
            def load_y(n, b, at):
                sp.wait_ge(*y1_ready.before(n, b + 1))
                sp.dma_start(yn[:, b], dram["y"][at * 2 + b].rearrange("(t p) d -> p t d", p=P)).then_inc(y_in[b].sem, 16)

            def body(l, i, load_next):
                n = l * PAIRS + i
                for stage, b in SCHEDULE:
                    if stage == "wo":
                        sp.wait_ge(*y1_ready.of(n, b + 1))
                        sp.wait_ge(*y_out[b].before(n, 1))
                        s = shifted[b].sem
                        sp.dma_start(h[:, b, :, 0:P], y1[:, b, :, 0:P]).then_inc(s, 16)
                        sp.dma_start(h[1:113, b, :, P:D], y1[0:112, b, :, P:D]).then_inc(s, 16)
                        sp.dma_start(h[113:P, b, :, P:D], y1[112:P - 1, b, :, P:D]).then_inc(s, 16)
                        sp.dma_start(h[0:1, b, 1, P:D], y1[P - 1:P, b, 0, P:D]).then_inc(s, 16)
                        sp.dma_start(h[0:1, b, 0, P:D], zero_row[:, :]).then_inc(s, 16)
                        load_y(n + 1, b, n + 1)
                        sp.wait_ge(*out_out[b].before(n, 1))
                        sp.dma_start(x1[:, b], dram["x1"][i * 2 + b].rearrange("(t p) d -> p t d", p=P)).then_inc(x1_in[b].sem, 16)
                        if load_next and b == 1:
                            sp.wait_ge(*full(n, "qkT", 1, 1, 1))
                            sp.wait_ge(*full(n, "wo", 1))
                            load_weights(sp, io, raw, l + 1)
                    if stage == "w2c":
                        sp.wait_ge(*y2_ready.of(n, b + 1))
                        sp.dma_start(dram["y"][(n + PAIRS) * 2 + b].rearrange("(t p) d -> p t d", p=P), h[:, b]).then_inc(y_out[b].sem, 16)
                        sp.wait_ge(*out_ready.of(n, b + 1))
                        sp.dma_start(out[i * 2 + b].rearrange("(t p) d -> p t d", p=P), x1[:, b]).then_inc(out_out[b].sem, 16)

            def rounds(l, load_next):
                with sp.Fori(0, PAIRS - 1) as i:
                    body(l, i, False)
                body(l, PAIRS - 1, load_next)

            with sp.Fori(0, LAYERS - 1) as l:
                rounds(l, True)
                load_vectors(sp, io, raw, l + 1)
            rounds(LAYERS - 1, False)
            for b in range(2):
                sp.wait_ge(*y_out[b].of(ROUNDS - 1, 1))
                sp.wait_ge(*out_out[b].of(ROUNDS - 1, 1))
                sp.wait_ge(*y_in[b].of(ROUNDS, 1))

        @block.tensor
        def _(pe):
            pe.wait_ge(raw.ident_in, 16)

            def start_of(kind, b, d):
                return 0 if d == 0 else N + GAP - (1 if kind == "y" else 0)

            def turn(kind, n, b, src, ready):
                pe.wait_ge(*ready)
                pe.wait_ge(*emptied(n, kind, b))
                for d in range(KD):
                    for t in range(T):
                        mm = pe.transpose(bank(kind, b)[:, d * N + t * P:d * N + (t + 1) * P],
                                          src[:, b, t, d * P:(d + 1) * P], ident[:, :])
                mm.then_inc(fills(kind, b), 1)

            for b in range(2):
                turn("yT", 0, b, yn, y_in[b].of(0, 1))
            pe.wait_ge(consts_cast, 2)
            pe.wait_ge(set_up, 9)

            with pe.Fori(0, LAYERS) as l:
                with pe.Fori(0, PAIRS) as i:
                    n = l * PAIRS + i
                    for stage, b in SCHEDULE:
                        if stage == "turn":
                            turn("yT", n + 1, b, yn, y_in[b].of(n + 1, 1))
                        if stage == "hturn":
                            turn("hT", n, b, h, h_ready.of(n, b + 1))
                        if stage in TILE:
                            if b == 0:
                                pe.wait_ge(*lo_a.of(l, KD))
                            pe.wait_ge(*yT_lo.of(n, b + 1))
                            for t in (TILE[stage],):
                                for c in range(3):
                                    pe.wait_ge(*emptied(n, "qkv", b, t, c))
                                    for e, (x, w) in enumerate(products):
                                        for d in range(KD):
                                            at = start_of("y", b, d) + t * P
                                            mm = pe.matmul(bank("qkv", b, t, c)[:, :], flat[x][:, b, at:at + P],
                                                           wqkv[w][:, d, c * INNER:(c + 1) * INNER],
                                                           start=(e == 0 and d == 0), stop=(e == 2 and d == KD - 1))
                                    mm.then_inc(fills("qkv", b, t, c), 1)
                        if stage == "qkT":
                            pe.wait_ge(*qk_ready.of(n, 4 * b + 4))
                            for g in range(2):
                                for c in range(2):
                                    pe.wait_ge(*emptied(n, "qkT", b, g, c))
                                    for pr in range(2):
                                        for t in range(T):
                                            at = (2 * g + pr) * P
                                            mm = pe.transpose(bank("qkT", b, g, c)[:, pr * N + t * P:pr * N + (t + 1) * P],
                                                              rot[:, 4 * b + 2 * t + c, at:at + P], ident[:, :])
                                    mm.then_inc(fills("qkT", b, g, c), 1)
                        def scores(head):
                            pr, par = head // 2, head % 2
                            pe.wait_ge(*emptied(n, "s", b, head))
                            to = bank("s", b, head)
                            pe.matmul(to[:, 0:PAIRS_OF_TILES * P], ident_b[:, :], mask[:, :], start=True, stop=False,
                                      skip_group_check=True)
                            for t in range(T):
                                for e, (x, y) in enumerate(products):
                                    mm = pe.matmul(to[:, t * P:t * P + (t + 1) * P], q[x][:, b, pr, par, t * P:(t + 1) * P],
                                                   k[y][:, b, pr, 0:(t + 1) * P], start=False, stop=(e == 2),
                                                   skip_group_check=True)
                            mm.then_inc(fills("s", b, head), 1)

                        def turn_probs(head):
                            pe.wait_ge(*probs_ready.of(n, H * b + head + 1))
                            pe.wait_ge(*emptied(n, "pT", b, head))
                            for src, dst in enumerate((0, 1, 2)):
                                mm = pe.transpose(bank("pT", b, head)[:, dst * P:(dst + 1) * P],
                                                  probs[:, (H * b + head) % SLOTS, src * P:(src + 1) * P], ident[:, :])
                            mm.then_inc(fills("pT", b, head), 1)

                        def values(head):
                            g, pr, par = head // 4, head // 2 % 2, head % 2
                            if head % 4 == 0:
                                pe.wait_ge(*emptied(n, "pv", b, g))
                            pe.wait_ge(*probsT_ready.of(n, H * b + head + 1))
                            p = probsT[:, (H * b + head) % SLOTS]
                            for t in range(T):
                                mm = pe.matmul(bank("pv", b, g)[HD * par:HD * (par + 1), pr * N + t * P:(pr + 1) * N],
                                               v[:, b, t, head * HD:(head + 1) * HD], p[:, t * N:N + t * P],
                                               start=(t == 0), stop=(t == T - 1), skip_group_check=True)
                            mm.then_inc(probsT_used.sem, 1)

                        if stage == "lead":
                            pe.wait_ge(*turned_lo.of(n, 4 * b + 2))
                            for head in range(LEAD):
                                scores(head)
                            pe.wait_ge(*v_ready.of(n, T * (b + 1)))
                        if stage in HEADS:
                            for head in HEADS[stage]:
                                if head + LEAD == H // 2:
                                    pe.wait_ge(*turned_lo.of(n, 4 * b + 4))
                                if head + LEAD < H:
                                    scores(head + LEAD)
                                turn_probs(head)
                                if head > 0:
                                    values(head - 1)
                            if head == H - 1:
                                values(head)
                        if stage == "wo":
                            if b == 0:
                                pe.wait_ge(*lo_b.of(l, 1))
                            pe.wait_ge(*o_lo.of(n, 2 * b + 2))
                            pe.wait_ge(*emptied(n, "wo", b))
                            for t in range(T):
                                for e, (x, w) in enumerate(products):
                                    for p in range(HP):
                                        mm = pe.matmul(bank("wo", b)[:, t * D:(t + 1) * D],
                                                       k[x][:, b, p, t * P:(t + 1) * P], wo[w][:, p, :],
                                                       start=(e == 0 and p == 0), stop=(e == 2 and p == HP - 1))
                            mm.then_inc(fills("wo", b), 1)
                        if stage in HIDDEN:
                            if stage == "w1a":
                                if b == 0:
                                    pe.wait_ge(*lo_w1.of(l, 1))
                                pe.wait_ge(*z_lo.of(n, b + 1))
                            for j in HIDDEN[stage]:
                                pe.wait_ge(*emptied(n, "w1", b, j))
                                for a in range(2):
                                    for e, (w, x) in enumerate(products):
                                        for d in range(KD):
                                            at, c = start_of("h", b, d), a * HID + j * P
                                            mm = pe.matmul(bank("w1", b, j)[:, a * N:(a + 1) * N], w1[w][:, d, c:c + P],
                                                           flat[x][:, b, at:at + N],
                                                           start=(e == 0 and d == 0), stop=(e == 2 and d == KD - 1))
                                mm.then_inc(fills("w1", b, j), 1)
                        if stage in PRODUCTS:
                            if stage == "w2a":
                                pe.wait_ge(*emptied(n, "w2", b))
                            for j in PRODUCTS[stage]:
                                pe.wait_ge(*u_lo.of(n, J * b + j + 1))
                                for t in range(T):
                                    for e, (x, w) in enumerate(products):
                                        mm = pe.matmul(bank("w2", b)[:, t * D:(t + 1) * D], u[x][:, j, t * P:(t + 1) * P],
                                                       w2[w][:, j, :], start=(e == 0 and j == 0 and t == 0),
                                                       stop=(e == 2 and j == J - 1), skip_group_check=True)
                            if stage == "w2c":
                                mm.then_inc(fills("w2", b), 1)

        @block.scalar
        def _(act):
            act.wait_ge(raw.ident_in, 16)
            act.wait_ge(raw.consts_in, 16 * 5)
            act.activation(ident_b[:, :], ident[:, :], ACT.Copy).then_inc(consts_cast, 1)
            act.activation(mask[:, :], raw.mask, ACT.Copy).then_inc(consts_cast, 1)
            act.wait_ge(flat_set, 2)

            def turn_high(n, b):
                act.wait_ge(*full(n, "yT", b))
                act.activation(halves(flat[0], b), bank("yT", b)[:, :].rearrange("p (d t) -> p d t", d=KD),
                               ACT.Copy).then_inc(yT_hi.sem, 1)

            turn_high(0, 0)
            turn_high(0, 1)
            act.wait_ge(set_up, 9)
            with act.Fori(0, LAYERS) as l:
                for kd in range(KD):
                    act.wait_ge(*raw.a_in[kd].of(l, 1))
                    act.activation(wqkv[0][:, kd], raw.qkv[:, kd], ACT.Copy).then_inc(hi_a.sem, 1)
                act.wait_ge(*raw.b_in.of(l, KD + 4))
                act.wait_ge(*full(l * PAIRS - 1, "w2", 1))
                for group in (pieces, pieces_w1):
                    for w, dst, land, src in group:
                        last = act.activation(w[0][dst], land[src], ACT.Copy)
                    last.then_inc(hi_b.sem, 1)

                with act.Fori(0, PAIRS) as i:
                    n = l * PAIRS + i
                    for stage, b in SCHEDULE:
                        if stage == "turn":
                            turn_high(n + 1, b)
                            if b == 1:
                                act.activation(unread[:, 1:2], mhalf[:, 0:1], ACT.Exp)
                        if stage in TILE:
                            for t in (TILE[stage],):
                                for c in range(2):
                                    m = 4 * b + 2 * t + c + 1
                                    act.wait_ge(*full(n, "qkv", b, t, c))
                                    act.wait_ge(*(ssq_sum.of(n, m - 2) if m > 2 else ssq_sum.before(n, 8 + m - 2)))
                                    act.activation(sq[:, c], bank("qkv", b, t, c)[:, :], ACT.Square).then_inc(sq_ready.sem, 1)
                                act.wait_ge(*full(n, "qkv", b, t, 2))
                                if b == 0 and t == 0:
                                    act.wait_ge(*lo_b.of(l, 1))
                                    act.wait_ge(*lo_w1.of(l, 1))
                                act.activation(v[:, b, t], bank("qkv", b, t, 2)[:, :], ACT.Copy).then_inc(v_ready.sem, 1)
                        if stage == "qkT":
                            if b == 0:
                                act.wait_ge(q_set, 2)
                            for g in range(2):
                                for c in range(2):
                                    act.wait_ge(*full(n, "qkT", b, g, c))
                                    src = bank("qkT", b, g, c)[:, :].rearrange("p (r t) -> p r t", r=2)
                                    if c == 0:
                                        for par in range(2):
                                            rows = slice(HD * par, HD * (par + 1))
                                            last = act.activation(q[0][rows, b, 2 * g:2 * g + 2, par], src[rows], ACT.Copy)
                                    else:
                                        last = act.activation(k[0][:, b, 2 * g:2 * g + 2], src, ACT.Copy)
                                    last.then_inc(turned_hi.sem, 1)
                        def exponentials(head):
                            m = H * b + head + 1
                            act.wait_ge(*max_ready.of(n, m))
                            if head >= SLOTS or b == 1:
                                act.wait_ge(*full(n, "pT", *divmod(m - 1 - SLOTS, H)))
                            else:
                                act.wait_ge(*full(n - 1, "pT", *divmod(2 * H + m - 1 - SLOTS, H)))
                            for t in range(T):
                                at = slice(t * P, t * P + (t + 1) * P)
                                last = act.activation(probs[:, (m - 1) % SLOTS, at], bank("s", b, head)[:, at], ACT.Exp,
                                                      bias=nm[:, b, head, t:t + 1], accum_out=total[:, b, head, t:t + 1])
                            last.then_inc(exp_ready.sem, 1)

                        def copy_turned(head):
                            m = H * b + head + 1
                            act.wait_ge(*full(n, "pT", b, head))
                            act.wait_ge(*(probsT_used.of(n, m - SLOTS) if m > SLOTS else probsT_used.before(n, 2 * H + m - SLOTS)))
                            act.activation(probsT[:, (m - 1) % SLOTS, :], bank("pT", b, head)[:, 0:PAIRS_OF_TILES * P],
                                           ACT.Copy).then_inc(probsT_ready.sem, 1)

                        def output(g):
                            act.wait_ge(*probsT_used.of(n, H * b + 4 * (g + 1)))
                            act.activation(k[0][:, b, 2 * g:2 * g + 2], bank("pv", b, g)[:, :].rearrange("p (r t) -> p r t", r=2),
                                           ACT.Copy).then_inc(o_hi.sem, 1)

                        if stage == "lead":
                            for head in range(LEAD):
                                exponentials(head)
                        if stage in HEADS:
                            for head in HEADS[stage]:
                                for later in due(stage, head):
                                    exponentials(later)
                                copy_turned(head)
                                if head == 4:
                                    output(0)
                            if head == H - 1:
                                output(1)
                                if b == 1:
                                    act.activation(unread[:, 0:1], mhalf[:, 0:1], ACT.Gelu)
                        if stage == "hturn":
                            act.wait_ge(*z_ready.of(n, b + 1))
                            act.activation(halves(flat[0], b), z.rearrange("p (d t) -> p d t", d=KD), ACT.Copy).then_inc(z_hi.sem, 1)
                        if stage in HIDDEN:
                            def rows(j):
                                return P if j < J - 1 else HID_LAST

                            def gelu(j):
                                m, r = J * b + j + 1, rows(j)
                                if m == 1:
                                    act.wait_ge(*raw.small_in.of(l, 13))
                                act.wait_ge(*full(n, "w1", b, j))
                                act.wait_ge(*(uf_ready.of(n, m - 2) if m > 2 else uf_ready.before(n, 2 * J + m - 2)))
                                act.activation(gate[0:r, j % 2], bank("w1", b, j)[0:r, N:2 * N], ACT.Gelu,
                                               bias=b1[0:r, 1, j:j + 1]).then_inc(gate_ready.sem, 1)

                            def high(j):
                                r = rows(j)
                                act.wait_ge(*uf_ready.of(n, J * b + j + 1))
                                act.activation(u[0][0:r, j], uf[0:r, j % 2], ACT.Copy).then_inc(u_hi.sem, 1)

                            js = list(HIDDEN[stage])
                            gelu(js[0])
                            for j in js[1:]:
                                gelu(j)
                                high(j - 1)
                            high(js[-1])

        @block.gpsimd
        def _(pool):
            for i in range(2):
                pool.memset(flat[i][:, :, :].bitcast(F32), 0.0).then_inc(flat_set, 1)
            for i in range(2):
                pool.memset(u[i][:, J - 1].bitcast(F32), 0.0).then_inc(set_up, 1)
                pool.memset(w2[i][:, J - 1].bitcast(F32), 0.0).then_inc(set_up, 1)
                pool.memset(w1[i][:, :, 2 * HID:].bitcast(F32), 0.0).then_inc(set_up, 1)
            pool.memset(zero_row[:, :], 0.0).then_inc(set_up, 1)
            pool.memset(mhalf[:, :], -0.5).then_inc(set_up, 1)
            pool.memset(eps[:, :], EPS).then_inc(set_up, 1)
            for i in range(2):
                pool.memset(q[i][:, :, :, :, :].bitcast(F32), 0.0).then_inc(q_set, 1)
            pool.wait_ge(set_up, 9)

            with pool.Fori(0, LAYERS) as l:
                pool.wait_ge(*hi_b.of(l, 2))
                for w, dst, land, src in pieces_w1:
                    last = pool.tensor_tensor(w[1][dst], land[src], w[0][dst].bitcast(F32), ALU.subtract)
                last.then_inc(lo_w1.sem, 1)
                with pool.Fori(0, PAIRS) as i:
                    n = l * PAIRS + i
                    for stage, b in SCHEDULE:
                        if stage in TILE:
                            for t in (TILE[stage],):
                                for c in range(2):
                                    m = 4 * b + 2 * t + c
                                    slot = rot[:, m].rearrange("p (h d) -> p h d", d=HD)
                                    pool.wait_ge(*ssq_ready.of(n, m + 1))
                                    pool.tensor_tensor(rnorm[:, b, t, c], ssq[:, b, t, c], mhalf[:, :], ALU.pow).then_inc(norm_ready.sem, 1)
                                    pool.wait_ge(*norm_ready.of(n, m + 1))
                                    pool.wait_ge(*sum_ready.of(n, m + 1))
                                    pool.tensor_tensor(slot, slot, rnorm[:, b, t, c].unsqueeze(2).to_broadcast([P, H, HD]),
                                                       ALU.mult).then_inc(qk_ready.sem, 1)
                        def divide(head):
                            m = H * b + head + 1
                            pool.wait_ge(*share_ready.of(n, m))
                            for t in range(T):
                                p = probs[:, (m - 1) % SLOTS, t * P:t * P + (t + 1) * P]
                                last = pool.tensor_tensor(p, p, share[:, b, head, t:t + 1].to_broadcast([P, (t + 1) * P]), ALU.mult)
                            last.then_inc(probs_ready.sem, 1)

                        if stage == "lead":
                            divide(0)
                        if stage in HEADS:
                            for head in HEADS[stage]:
                                if head + 1 < H:
                                    divide(head + 1)
                        if stage == "stats":
                            pool.wait_ge(*var_ready.of(n, b + 1))
                            pool.tensor_tensor(veps[:, b], mv[:, b, :, 1], eps[:, :], ALU.add).then_inc(eps_added.sem, 1)
                            pool.wait_ge(*eps_added.of(n, b + 1))
                            pool.tensor_tensor(rstd[:, b], veps[:, b], mhalf[:, 0:T], ALU.pow).then_inc(rstd_ready.sem, 1)
                        if stage == "hturn":
                            if b == 0:
                                pool.wait_ge(*raw.small_in.of(l, 13))
                            pool.wait_ge(*full(n, "hT", b))
                            for t in range(T):
                                last = pool.tensor_tensor(h[:, b, t], y1[:, b, t], b2[:, :], ALU.add)
                            last.then_inc(y1b_ready.sem, 1)
                        if stage in HIDDEN:
                            for j in HIDDEN[stage]:
                                r = P if j < J - 1 else HID_LAST
                                pool.wait_ge(*u_hi.of(n, J * b + j + 1))
                                pool.tensor_tensor(u[1][0:r, j], uf[0:r, j % 2], u[0][0:r, j].bitcast(F32),
                                                   ALU.subtract).then_inc(u_lo.sem, 1)
                        if stage == "w2c":
                            pool.wait_ge(*y2_ready.of(n, b + 1))
                            pool.wait_ge(*x1_in[b].of(n, 1))
                            for t in range(T):
                                last = pool.tensor_tensor(x1[:, b, t], h[:, b, t], x1[:, b, t], ALU.add)
                            last.then_inc(out_ready.sem, 1)

        @block.vector
        def _(dve):
            dve.wait_ge(raw.consts_in, 16 * 5)

            def turn_low(n, b):
                dve.wait_ge(*yT_hi.of(n, b + 1))
                dve.tensor_tensor(halves(flat[1], b), bank("yT", b)[:, :].rearrange("p (d t) -> p d t", d=KD),
                                  halves(flat[0], b).bitcast(F32), ALU.subtract).then_inc(yT_lo.sem, 1)

            turn_low(0, 0)
            turn_low(0, 1)
            dve.wait_ge(set_up, 9)
            with dve.Fori(0, LAYERS) as l:
                for kd in range(KD):
                    dve.wait_ge(*hi_a.of(l, kd + 1))
                    dve.tensor_tensor(wqkv[1][:, kd], raw.qkv[:, kd], wqkv[0][:, kd].bitcast(F32), ALU.subtract).then_inc(lo_a.sem, 1)
                dve.wait_ge(*raw.small_in.of(l, 13))
                for c in range(2):
                    for s in range(2):
                        last = dve.tensor_tensor(table[:, c, s], turns[:, c, s],
                                                 scale[:, c, s].unsqueeze(1).to_broadcast([P, T, HD]), ALU.mult)
                last.then_inc(table_ready.sem, 1)
                dve.wait_ge(*hi_b.of(l, 1))
                for w, dst, land, src in pieces:
                    last = dve.tensor_tensor(w[1][dst], land[src], w[0][dst].bitcast(F32), ALU.subtract)
                last.then_inc(lo_b.sem, 1)

                with dve.Fori(0, PAIRS) as i:
                    n = l * PAIRS + i
                    for stage, b in SCHEDULE:
                        if stage == "turn":
                            turn_low(n + 1, b)
                        if stage in TILE:
                            for t in (TILE[stage],):
                                for c in range(2):
                                    m = 4 * b + 2 * t + c
                                    src = bank("qkv", b, t, c)[:, :].rearrange("p (h d) -> p h d", d=HD)
                                    first = rot[:, m].rearrange("p (h d) -> p h d", d=HD)
                                    second = rot[:, 8 + m % 2].rearrange("p (h d) -> p h d", d=HD)
                                    half = HD // 2
                                    dve.wait_ge(*sq_ready.of(n, m + 1))
                                    dve.tensor_reduce(ssq[:, b, t, c], sq[:, c].rearrange("p (h d) -> p h d", d=HD),
                                                      AX_X, ALU.add).then_inc(ssq_sum.sem, 1)
                                    if m == 0:
                                        dve.wait_ge(*table_ready.of(l, 1))
                                        dve.wait_ge(*lo_b.of(l, 1))
                                    dve.tensor_tensor(first, src, table[:, c, 0, t].unsqueeze(1).to_broadcast([P, H, HD]), ALU.mult)
                                    dve.wait_ge(*(sum_ready.of(n, m - 1) if m >= 2 else sum_ready.before(n, 8 + m - 1)))
                                    dve.tensor_tensor(second[:, :, 0:half], src[:, :, half:HD],
                                                      table[:, c, 1, t, 0:half].unsqueeze(1).to_broadcast([P, H, half]), ALU.mult)
                                    dve.tensor_tensor(second[:, :, half:HD], src[:, :, 0:half],
                                                      table[:, c, 1, t, half:HD].unsqueeze(1).to_broadcast([P, H, half]),
                                                      ALU.mult).then_inc(terms_ready.sem, 1)
                                    dve.wait_ge(*ssq_sum.of(n, m + 1))
                                    dve.tensor_scalar(ssq[:, b, t, c], ssq[:, b, t, c], NORM_FLOOR ** 2, None,
                                                      ALU.max).then_inc(ssq_ready.sem, 1)
                                    dve.wait_ge(*terms_ready.of(n, m + 1))
                                    dve.tensor_tensor(rot[:, m], rot[:, m], rot[:, 8 + m % 2], ALU.add).then_inc(sum_ready.sem, 1)
                        if stage == "qkT":
                            if b == 0:
                                dve.wait_ge(q_set, 2)
                            for g in range(2):
                                for c in range(2):
                                    dve.wait_ge(*turned_hi.of(n, 4 * b + 2 * g + c + 1))
                                    src = bank("qkT", b, g, c)[:, :].rearrange("p (r t) -> p r t", r=2)
                                    if c == 0:
                                        for par in range(2):
                                            rows = slice(HD * par, HD * (par + 1))
                                            last = dve.tensor_tensor(q[1][rows, b, 2 * g:2 * g + 2, par], src[rows],
                                                                     q[0][rows, b, 2 * g:2 * g + 2, par].bitcast(F32), ALU.subtract)
                                    else:
                                        last = dve.tensor_tensor(k[1][:, b, 2 * g:2 * g + 2], src,
                                                                 k[0][:, b, 2 * g:2 * g + 2].bitcast(F32), ALU.subtract)
                                    last.then_inc(turned_lo.sem, 1)
                        def maxima(head):
                            dve.wait_ge(*full(n, "s", b, head))
                            for t in range(T):
                                last = dve.tensor_reduce(nm[:, b, head, t:t + 1], bank("s", b, head)[:, t * P:t * P + (t + 1) * P],
                                                         AX_X, ALU.max, negate=True)
                            last.then_inc(max_ready.sem, 1)

                        def invert(head):
                            m = H * b + head + 1
                            dve.wait_ge(*exp_ready.of(n, m))
                            dve.reciprocal(share[:, b, head], total[:, b, head]).then_inc(share_ready.sem, 1)

                        def output_low(g):
                            dve.wait_ge(*o_hi.of(n, 2 * b + g + 1))
                            dve.tensor_tensor(k[1][:, b, 2 * g:2 * g + 2], bank("pv", b, g)[:, :].rearrange("p (r t) -> p r t", r=2),
                                              k[0][:, b, 2 * g:2 * g + 2].bitcast(F32), ALU.subtract).then_inc(o_lo.sem, 1)

                        if stage == "lead":
                            for head in range(LEAD):
                                maxima(head)
                            invert(0)
                        if stage in HEADS:
                            for head in HEADS[stage]:
                                for later in due(stage, head):
                                    maxima(later)
                                if head + 1 < H:
                                    invert(head + 1)
                                if head == 5:
                                    output_low(0)
                            if head == H - 1:
                                output_low(1)
                        if stage == "wo":
                            dve.wait_ge(*full(n, "wo", b))
                            dve.tensor_tensor(y1[:, b], bank("wo", b)[:, :].rearrange("p (t d) -> p t d", t=T), yn[:, b],
                                              ALU.add).then_inc(y1_ready.sem, 1)
                        if stage == "stats":
                            dve.wait_ge(*shifted[b].of(n, 5))
                            for t in range(T):
                                last = dve.bn_stats(stats[:, b, t], h[:, b, t])
                            last.then_inc(stats_ready.sem, 1)
                            dve.wait_ge(*stats_ready.of(n, b + 1))
                            dve.tensor_copy(carrier[:, :], stats[:, b, :, 0])
                            for t in range(T):
                                last = dve.bn_aggr(mv[:, b, t], stats[:, b, t])
                            last.then_inc(var_ready.sem, 1)
                        if stage == "norm":
                            dve.wait_ge(*rstd_ready.of(n, b + 1))
                            for t in range(T):
                                last = dve.tensor_scalar(h[:, b, t], h[:, b, t], mv[:, b, t, 0:1], rstd[:, b, t:t + 1],
                                                         ALU.subtract, ALU.mult)
                            last.then_inc(h_ready.sem, 1)
                        if stage == "hturn":
                            dve.wait_ge(*full(n, "hT", b))
                            for d in range(KD):
                                last = dve.tensor_scalar(z[:, d * N:(d + 1) * N], bank("hT", b)[:, d * N:(d + 1) * N],
                                                         ln[:, 0, d:d + 1], ln[:, 1, d:d + 1], ALU.mult, ALU.add)
                            last.then_inc(z_ready.sem, 1)
                            dve.wait_ge(*z_hi.of(n, b + 1))
                            dve.tensor_tensor(halves(flat[1], b), z.rearrange("p (d t) -> p d t", d=KD),
                                              halves(flat[0], b).bitcast(F32), ALU.subtract).then_inc(z_lo.sem, 1)
                        if stage in HIDDEN:
                            for j in HIDDEN[stage]:
                                m, r = J * b + j + 1, (P if j < J - 1 else HID_LAST)
                                dve.wait_ge(*gate_ready.of(n, m))
                                dve.wait_ge(*(u_lo.of(n, m - 2) if m > 2 else u_lo.before(n, 2 * J + m - 2)))
                                dve.scalar_tensor_tensor(uf[0:r, j % 2], bank("w1", b, j)[0:r, 0:N], b1[0:r, 0, j:j + 1],
                                                         gate[0:r, j % 2], ALU.add, ALU.mult).then_inc(uf_ready.sem, 1)
                        if stage == "w2c":
                            dve.wait_ge(*full(n, "w2", b))
                            dve.wait_ge(*y1b_ready.of(n, b + 1))
                            dve.tensor_tensor(h[:, b], bank("w2", b)[:, :].rearrange("p (t d) -> p t d", t=T), h[:, b],
                                              ALU.add).then_inc(y2_ready.sem, 1)



INPUTS = (("x", "x"), ("ctx", "ctx_1024"), ("wq", "L0_xattn_wq"), ("bq", "L0_xattn_bq"), ("wk", "L0_xattn_wk"),
          ("bk", "L0_xattn_bk"), ("wv", "L0_xattn_wv"), ("bv", "L0_xattn_bv"), ("wqkv", "L0_ffn_wqkv"),
          ("q_scale", "L0_ffn_q_scale"), ("k_scale", "L0_ffn_k_scale"), ("wo", "L0_ffn_wo"),
          ("ln_g", "L0_ffn_ln_g"), ("ln_b", "L0_ffn_ln_b"), ("w1", "L0_ffn_w1"), ("b1", "L0_ffn_b1"),
          ("w2", "L0_ffn_w2"), ("b2", "L0_ffn_b2"))


def build(nc, io, out):
    dram = {
        "parts": nc.dram_tensor("parts", (2, 2, 3, D, N), BF16).ap(),
        "x1": nc.dram_tensor("x1", (B, N, D), F32).ap(),
        "y": nc.dram_tensor("y", ((LAYERS + 1) * B, N, D), F32).ap(),
    }
    with ExitStack() as ctx:
        raw = raw_tiles(nc, ctx)
        cross_attention(nc, io, dram, raw)
        layers(nc, io, dram, out, raw)


def kernel(**inputs):
    import concourse.bacc as bacc
    from concourse.bass_utils import run_bass_kernel_spmd

    nc = bacc.Bacc("TRN2", target_bir_lowering=False, num_devices=1)
    arrays = {short: np.ascontiguousarray(inputs[name]) for short, name in INPUTS} | constants()
    io = {k: nc.dram_tensor("in_" + k, a.shape, mybir.dt.from_np(a.dtype), kind="ExternalInput").ap()
          for k, a in arrays.items()}
    out = nc.dram_tensor("out_dram", (B, N, D), F32, kind="ExternalOutput").ap()
    build(nc, io, out)
    r = run_bass_kernel_spmd(nc, [{"in_" + k: a for k, a in arrays.items()}], core_ids=[0])
    return r.results[0]["out_dram"]
```
